# Optimizing a Trainium2 kernel written in Bass

```python
import numpy as np
import jax
import jax.numpy as jnp

def _softmax(x, axis=-1):
    return jax.nn.softmax(x, axis=axis)

def _gelu(x):
    return jax.nn.gelu(x, approximate=True)

def _silu(x):
    return jax.nn.silu(x)

def _sigmoid(x):
    return jax.nn.sigmoid(x)

def _layernorm(x, axis=-1, eps=1e-05):
    m = jnp.mean(x, axis=axis, keepdims=True)
    v = jnp.var(x, axis=axis, keepdims=True)
    return (x - m) / jnp.sqrt(v + eps)

def _scatter_add(tgt, idx, src, axis=0):
    return tgt.at[idx].add(src)

def _segment_sum(src, seg, n):
    return jax.ops.segment_sum(src, seg, n)
kernel_name = 'mk_gnn_ffn_d2_gnn_r16_4bb171'

def setup_inputs(seed: int=0):
    np.random.seed(seed)
    _w = jnp.asarray

    def _rec_inputs():
        import jax
        import jax.numpy as jnp
        _gk = jax.random.key(seed)
        x = -0.0002117 + 1 * jax.random.normal(jax.random.fold_in(_gk, 1), (6250, 256), jnp.float32)
        src = jax.random.randint(jax.random.fold_in(_gk, 2), (100000,), 0, 6250, jnp.int32)
        dst = jax.random.randint(jax.random.fold_in(_gk, 3), (100000,), 0, 6250, jnp.int32)
        _o = jnp.argsort(dst, stable=True)
        src = src[_o]
        dst = dst[_o]
        edge_attr_4 = jax.random.uniform(jax.random.fold_in(_gk, 11), (100000, 4), jnp.float32, 0.0, 0.999999)
        edge_weight = jax.random.uniform(jax.random.fold_in(_gk, 13), (100000,), jnp.float32, 0.0, 0.999998)
        return (x, src, dst, edge_attr_4, edge_weight)
    x, src, dst, edge_attr_4, edge_weight = _rec_inputs()

    def _L0_gnn_setup():
        import jax, jax.numpy as jnp
        import numpy as np
        N, D, E = (6250, 256, 312500)
        H = 2 * D
        EPS = 0.0
        key = jax.random.key(seed)
        k1, k2, k3, k4, k5, k6, k7 = jax.random.split(key, 7)
        x = jax.random.normal(k1, (N, D), dtype=jnp.float32)
        edge_index = jax.random.randint(k2, (2, E), 0, N, dtype=jnp.int64)
        edge_weight = jax.random.uniform(k3, (E,), dtype=jnp.float32)
        s1 = 1.0 / np.sqrt(D)
        s2 = 1.0 / np.sqrt(H)
        W1 = jax.random.uniform(k4, (D, H), dtype=jnp.float32, minval=-s1, maxval=s1)
        b1 = jax.random.uniform(k5, (H,), dtype=jnp.float32, minval=-s1, maxval=s1)
        W2 = jax.random.uniform(k6, (H, D), dtype=jnp.float32, minval=-s2, maxval=s2)
        b2 = jax.random.uniform(k7, (D,), dtype=jnp.float32, minval=-s2, maxval=s2)
        return {'x': x, 'edge_index': edge_index, 'edge_weight': edge_weight, 'W1': W1, 'b1': b1, 'W2': W2, 'b2': b2}
    _L0_gnn_all = _L0_gnn_setup()
    _L0_gnn_in = {k: v for k, v in _L0_gnn_all.items() if k in ('W1', 'b1', 'W2', 'b2')}
    del _L0_gnn_all

    def _L0_ffn_setup():
        import jax, jax.numpy as jnp
        import numpy as np
        NUM_EXPERTS = 8
        TOP_K = 2
        B, S, D = (8, 512, 256)

        def _moe(tokens, router_w, w1, b1, w2, b2):
            N = tokens.shape[0]
            E = router_w.shape[0]
            logits = tokens.astype(jnp.float32) @ router_w.astype(jnp.float32).T
            probs = jax.nn.softmax(logits, axis=-1)
            rw, re = jax.lax.top_k(probs, TOP_K)
            if TOP_K > 1:
                rw = rw / jnp.maximum(rw.sum(-1, keepdims=True), 1e-12)
            rw = rw.astype(tokens.dtype)
            combine = jnp.zeros((N, E), tokens.dtype).at[jnp.arange(N)[:, None], re].set(rw)
            out = tokens
            for e in range(E):
                h = jax.nn.gelu(tokens @ w1[e] + b1[e], approximate=False)
                y = h @ w2[e] + b2[e]
                out = out + combine[:, e:e + 1] * y
            return out
        key = jax.random.key(seed)
        ks = jax.random.split(key, 4)
        scale = 1.0 / np.sqrt(D).astype(np.float32)
        return {'input_embeddings': jax.random.normal(ks[0], (B, S, D), jnp.float32), 'router_w': jax.random.normal(ks[1], (NUM_EXPERTS, D), jnp.float32) * scale, 'w1': jax.random.normal(ks[2], (NUM_EXPERTS, D, D), jnp.float32) * scale, 'b1': jnp.zeros((NUM_EXPERTS, D), jnp.float32), 'w2': jax.random.normal(ks[3], (NUM_EXPERTS, D, D), jnp.float32) * scale, 'b2': jnp.zeros((NUM_EXPERTS, D), jnp.float32)}
    _L0_ffn_all = _L0_ffn_setup()
    _L0_ffn_in = {k: v for k, v in _L0_ffn_all.items() if k in ('router_w', 'w1', 'b1', 'w2', 'b2')}
    del _L0_ffn_all

    def _L1_gnn_setup():
        import jax, jax.numpy as jnp
        import numpy as np
        N_NODES = 3125
        N_EDGES = 20000
        HIDDEN = 256
        N_LAYERS = 5
        BN_EPS = 1e-05

        def _mpnn(x, edge_index, edge_attr, mlp_w, mlp_b, ew1, ew2, bn_g, bn_b):
            n = x.shape[0]
            row, col = (edge_index[0], edge_index[1])
            deg = jax.ops.segment_sum(jnp.ones((edge_index.shape[1],), x.dtype), col, num_segments=n)
            dinv = jnp.where(deg > 0, deg ** (-0.5), 0.0)
            norm = dinv[row] * dinv[col]
            h = x
            for l in range(N_LAYERS):
                edge_fea = jnp.concatenate([edge_attr[:, 3:] @ ew1[l], edge_attr[:, 0:3] @ ew2[l]], axis=-1)
                msg = norm[:, None] * (h[row] + edge_fea)
                agg = jax.ops.segment_sum(msg, col, num_segments=n)
                h = jax.nn.relu(jnp.concatenate([h, agg], axis=1) @ mlp_w[l] + mlp_b[l])
                mu = h.mean(axis=0)
                var = h.var(axis=0)
                h = (h - mu) * jax.lax.rsqrt(var + BN_EPS) * bn_g[l] + bn_b[l]
                if l != N_LAYERS - 1:
                    h = jax.nn.relu(h)
            return h
        key = jax.random.key(seed)
        ks = jax.random.split(key, 8)
        x = jax.random.normal(ks[0], (N_NODES, HIDDEN), dtype=jnp.float32)
        edge_index = jax.random.randint(ks[1], (2, N_EDGES), 0, N_NODES, dtype=jnp.int64)
        edge_attr = jax.random.uniform(ks[2], (N_EDGES, 4), dtype=jnp.float32)
        mlp_w = jax.random.normal(ks[3], (N_LAYERS, 2 * HIDDEN, HIDDEN), dtype=jnp.float32) * (1.0 / np.sqrt(2 * HIDDEN))
        mlp_b = jnp.zeros((N_LAYERS, HIDDEN), dtype=jnp.float32)
        ew1 = jax.random.normal(ks[4], (N_LAYERS, 1, HIDDEN // 2), dtype=jnp.float32)
        ew2 = jax.random.normal(ks[5], (N_LAYERS, 3, HIDDEN // 2), dtype=jnp.float32) * (1.0 / np.sqrt(3.0))
        bn_g = jnp.ones((N_LAYERS, HIDDEN), dtype=jnp.float32)
        bn_b = jnp.zeros((N_LAYERS, HIDDEN), dtype=jnp.float32)
        return {'x': x, 'edge_index': edge_index, 'edge_attr': edge_attr, 'mlp_w': mlp_w, 'mlp_b': mlp_b, 'ew1': ew1, 'ew2': ew2, 'bn_g': bn_g, 'bn_b': bn_b}
    _L1_gnn_all = _L1_gnn_setup()
    _L1_gnn_in = {k: v for k, v in _L1_gnn_all.items() if k in ('mlp_w', 'mlp_b', 'ew1', 'ew2', 'bn_g', 'bn_b')}
    del _L1_gnn_all

    def _L1_ffn_setup():
        import jax, jax.numpy as jnp
        import numpy as np
        B, N, D = (16, 256, 256)
        NUM_EXPERTS, TOP_K, HEADS = (4, 2, 4)
        N_EDGES = 65536
        LN_EPS = 1e-05

        def _layernorm(x, g, b):
            mu = x.mean(-1, keepdims=True)
            var = ((x - mu) ** 2).mean(-1, keepdims=True)
            return (x - mu) * jax.lax.rsqrt(var + LN_EPS) * g + b

        def _forward(x, edge_index, W_gat, att_src, att_dst, b_gat, ln_gamma, ln_beta, W1, b1, W2, b2):
            Bc, Nc, Dc = x.shape
            M = Bc * Nc
            x_flat = x.reshape(M, Dc)
            h = (x_flat @ W_gat).reshape(M, HEADS, NUM_EXPERTS)
            loops = jnp.arange(M, dtype=edge_index.dtype)
            src = jnp.concatenate([edge_index[0], loops])
            dst = jnp.concatenate([edge_index[1], loops])
            a_src = (h * att_src).sum(-1)
            a_dst = (h * att_dst).sum(-1)
            e = jax.nn.leaky_relu(a_src[src] + a_dst[dst], negative_slope=0.2)
            e_max = jax.ops.segment_max(e, dst, num_segments=M)
            ee = jnp.exp(e - e_max[dst])
            denom = jax.ops.segment_sum(ee, dst, num_segments=M)
            alpha = ee / (denom[dst] + 1e-16)
            msg = h[src] * alpha[:, :, None]
            agg = jax.ops.segment_sum(msg, dst, num_segments=M).reshape(M, HEADS * NUM_EXPERTS) + b_gat
            scores = _layernorm(agg, ln_gamma, ln_beta).reshape(M, HEADS, NUM_EXPERTS).mean(1)
            scores = scores.reshape(Bc, Nc, NUM_EXPERTS)
            topk_s, topk_i = jax.lax.top_k(scores, TOP_K)
            w = jax.nn.softmax(topk_s, axis=-1)
            out = jnp.zeros_like(x)
            for ei in range(NUM_EXPERTS):
                g = jnp.where(topk_i == ei, w, 0.0).sum(-1)
                hh = jax.nn.gelu(x @ W1[ei] + b1[ei], approximate=False)
                out = out + g[..., None] * (hh @ W2[ei] + b2[ei])
            return out
        key = jax.random.key(seed)
        ks = jax.random.split(key, 8)
        s = 0.05
        return {'x': jax.random.normal(ks[0], (B, N, D), jnp.float32), 'W_gat': jax.random.normal(ks[1], (D, HEADS * NUM_EXPERTS), jnp.float32) * s, 'att_src': jax.random.normal(ks[2], (HEADS, NUM_EXPERTS), jnp.float32) * s, 'att_dst': jax.random.normal(ks[3], (HEADS, NUM_EXPERTS), jnp.float32) * s, 'b_gat': jnp.zeros((HEADS * NUM_EXPERTS,), jnp.float32), 'ln_gamma': jnp.ones((HEADS * NUM_EXPERTS,), jnp.float32), 'ln_beta': jnp.zeros((HEADS * NUM_EXPERTS,), jnp.float32), 'W1': jax.random.normal(ks[4], (NUM_EXPERTS, D, 2 * D), jnp.float32) * s, 'b1': jnp.zeros((NUM_EXPERTS, 2 * D), jnp.float32), 'W2': jax.random.normal(ks[5], (NUM_EXPERTS, 2 * D, D), jnp.float32) * s, 'b2': jnp.zeros((NUM_EXPERTS, D), jnp.float32), 'edge_index': jax.random.randint(ks[6], (2, N_EDGES), 0, B * N, jnp.int32)}
    _L1_ffn_all = _L1_ffn_setup()
    _L1_ffn_in = {k: v for k, v in _L1_ffn_all.items() if k in ('W_gat', 'att_src', 'att_dst', 'b_gat', 'ln_gamma', 'ln_beta', 'W1', 'b1', 'W2', 'b2', 'edge_index')}
    del _L1_ffn_all
    return {'x': x, 'src': src, 'dst': dst, 'edge_attr_4': edge_attr_4, 'edge_weight': edge_weight, 'L0_gnn_W1': _L0_gnn_in['W1'], 'L0_gnn_b1': _L0_gnn_in['b1'], 'L0_gnn_W2': _L0_gnn_in['W2'], 'L0_gnn_b2': _L0_gnn_in['b2'], 'L0_ffn_router_w': _L0_ffn_in['router_w'], 'L0_ffn_w1': _L0_ffn_in['w1'], 'L0_ffn_b1': _L0_ffn_in['b1'], 'L0_ffn_w2': _L0_ffn_in['w2'], 'L0_ffn_b2': _L0_ffn_in['b2'], 'L1_gnn_mlp_w': _L1_gnn_in['mlp_w'], 'L1_gnn_mlp_b': _L1_gnn_in['mlp_b'], 'L1_gnn_ew1': _L1_gnn_in['ew1'], 'L1_gnn_ew2': _L1_gnn_in['ew2'], 'L1_gnn_bn_g': _L1_gnn_in['bn_g'], 'L1_gnn_bn_b': _L1_gnn_in['bn_b'], 'L1_ffn_W_gat': _L1_ffn_in['W_gat'], 'L1_ffn_att_src': _L1_ffn_in['att_src'], 'L1_ffn_att_dst': _L1_ffn_in['att_dst'], 'L1_ffn_b_gat': _L1_ffn_in['b_gat'], 'L1_ffn_ln_gamma': _L1_ffn_in['ln_gamma'], 'L1_ffn_ln_beta': _L1_ffn_in['ln_beta'], 'L1_ffn_W1': _L1_ffn_in['W1'], 'L1_ffn_b1': _L1_ffn_in['b1'], 'L1_ffn_W2': _L1_ffn_in['W2'], 'L1_ffn_b2': _L1_ffn_in['b2'], 'L1_ffn_edge_index': _L1_ffn_in['edge_index']}

def reference(x, src, dst, edge_attr_4, edge_weight, L0_gnn_W1, L0_gnn_b1, L0_gnn_W2, L0_gnn_b2, L0_ffn_router_w, L0_ffn_w1, L0_ffn_b1, L0_ffn_w2, L0_ffn_b2, L1_gnn_mlp_w, L1_gnn_mlp_b, L1_gnn_ew1, L1_gnn_ew2, L1_gnn_bn_g, L1_gnn_bn_b, L1_ffn_W_gat, L1_ffn_att_src, L1_ffn_att_dst, L1_ffn_b_gat, L1_ffn_ln_gamma, L1_ffn_ln_beta, L1_ffn_W1, L1_ffn_b1, L1_ffn_W2, L1_ffn_b2, L1_ffn_edge_index):
    import jax
    import jax.numpy as jnp

    def _L0_gnn_ref(x, edge_index, edge_weight, W1, b1, W2, b2):
        import jax, jax.numpy as jnp
        import numpy as np
        N, D, E = (6250, 256, 312500)
        H = 2 * D
        EPS = 0.0
        row, col = (edge_index[0], edge_index[1])
        messages = x[col] * edge_weight[:, None]
        agg = jax.ops.segment_sum(messages, row, num_segments=N)
        h = (1.0 + EPS) * x + agg
        h = jax.nn.relu(h @ W1 + b1)
        out = h @ W2 + b2
        return out

    def _L0_ffn_ref(input_embeddings, router_w, w1, b1, w2, b2):
        import jax, jax.numpy as jnp
        import numpy as np
        NUM_EXPERTS = 8
        TOP_K = 2
        B, S, D = (8, 512, 256)

        def _moe(tokens, router_w, w1, b1, w2, b2):
            N = tokens.shape[0]
            E = router_w.shape[0]
            logits = tokens.astype(jnp.float32) @ router_w.astype(jnp.float32).T
            probs = jax.nn.softmax(logits, axis=-1)
            rw, re = jax.lax.top_k(probs, TOP_K)
            if TOP_K > 1:
                rw = rw / jnp.maximum(rw.sum(-1, keepdims=True), 1e-12)
            rw = rw.astype(tokens.dtype)
            combine = jnp.zeros((N, E), tokens.dtype).at[jnp.arange(N)[:, None], re].set(rw)
            out = tokens
            for e in range(E):
                h = jax.nn.gelu(tokens @ w1[e] + b1[e], approximate=False)
                y = h @ w2[e] + b2[e]
                out = out + combine[:, e:e + 1] * y
            return out
        b, s, d = input_embeddings.shape
        tokens = input_embeddings.reshape(b * s, d)
        return _moe(tokens, router_w, w1, b1, w2, b2).reshape(b, s, d)

    def _L1_gnn_ref(x, edge_index, edge_attr, mlp_w, mlp_b, ew1, ew2, bn_g, bn_b):
        import jax, jax.numpy as jnp
        import numpy as np
        N_NODES = 3125
        N_EDGES = 20000
        HIDDEN = 256
        N_LAYERS = 5
        BN_EPS = 1e-05

        def _mpnn(x, edge_index, edge_attr, mlp_w, mlp_b, ew1, ew2, bn_g, bn_b):
            n = x.shape[0]
            row, col = (edge_index[0], edge_index[1])
            deg = jax.ops.segment_sum(jnp.ones((edge_index.shape[1],), x.dtype), col, num_segments=n)
            dinv = jnp.where(deg > 0, deg ** (-0.5), 0.0)
            norm = dinv[row] * dinv[col]
            h = x
            for l in range(N_LAYERS):
                edge_fea = jnp.concatenate([edge_attr[:, 3:] @ ew1[l], edge_attr[:, 0:3] @ ew2[l]], axis=-1)
                msg = norm[:, None] * (h[row] + edge_fea)
                agg = jax.ops.segment_sum(msg, col, num_segments=n)
                h = jax.nn.relu(jnp.concatenate([h, agg], axis=1) @ mlp_w[l] + mlp_b[l])
                mu = h.mean(axis=0)
                var = h.var(axis=0)
                h = (h - mu) * jax.lax.rsqrt(var + BN_EPS) * bn_g[l] + bn_b[l]
                if l != N_LAYERS - 1:
                    h = jax.nn.relu(h)
            return h
        return _mpnn(x, edge_index, edge_attr, mlp_w, mlp_b, ew1, ew2, bn_g, bn_b)

    def _L1_ffn_ref(x, W_gat, att_src, att_dst, b_gat, ln_gamma, ln_beta, W1, b1, W2, b2, edge_index):
        import jax, jax.numpy as jnp
        import numpy as np
        B, N, D = (16, 256, 256)
        NUM_EXPERTS, TOP_K, HEADS = (4, 2, 4)
        N_EDGES = 65536
        LN_EPS = 1e-05

        def _layernorm(x, g, b):
            mu = x.mean(-1, keepdims=True)
            var = ((x - mu) ** 2).mean(-1, keepdims=True)
            return (x - mu) * jax.lax.rsqrt(var + LN_EPS) * g + b

        def _forward(x, edge_index, W_gat, att_src, att_dst, b_gat, ln_gamma, ln_beta, W1, b1, W2, b2):
            Bc, Nc, Dc = x.shape
            M = Bc * Nc
            x_flat = x.reshape(M, Dc)
            h = (x_flat @ W_gat).reshape(M, HEADS, NUM_EXPERTS)
            loops = jnp.arange(M, dtype=edge_index.dtype)
            src = jnp.concatenate([edge_index[0], loops])
            dst = jnp.concatenate([edge_index[1], loops])
            a_src = (h * att_src).sum(-1)
            a_dst = (h * att_dst).sum(-1)
            e = jax.nn.leaky_relu(a_src[src] + a_dst[dst], negative_slope=0.2)
            e_max = jax.ops.segment_max(e, dst, num_segments=M)
            ee = jnp.exp(e - e_max[dst])
            denom = jax.ops.segment_sum(ee, dst, num_segments=M)
            alpha = ee / (denom[dst] + 1e-16)
            msg = h[src] * alpha[:, :, None]
            agg = jax.ops.segment_sum(msg, dst, num_segments=M).reshape(M, HEADS * NUM_EXPERTS) + b_gat
            scores = _layernorm(agg, ln_gamma, ln_beta).reshape(M, HEADS, NUM_EXPERTS).mean(1)
            scores = scores.reshape(Bc, Nc, NUM_EXPERTS)
            topk_s, topk_i = jax.lax.top_k(scores, TOP_K)
            w = jax.nn.softmax(topk_s, axis=-1)
            out = jnp.zeros_like(x)
            for ei in range(NUM_EXPERTS):
                g = jnp.where(topk_i == ei, w, 0.0).sum(-1)
                hh = jax.nn.gelu(x @ W1[ei] + b1[ei], approximate=False)
                out = out + g[..., None] * (hh @ W2[ei] + b2[ei])
            return out
        return _forward(x, edge_index, W_gat, att_src, att_dst, b_gat, ln_gamma, ln_beta, W1, b1, W2, b2)
    edge_index = jnp.stack([src, dst])
    x = x + _L0_gnn_ref(_layernorm(x, axis=-1), edge_index, edge_weight, L0_gnn_W1, L0_gnn_b1, L0_gnn_W2, L0_gnn_b2)
    x = x + _L0_ffn_ref(_layernorm(x, axis=-1)[None], L0_ffn_router_w, L0_ffn_w1, L0_ffn_b1, L0_ffn_w2, L0_ffn_b2)[0]
    x = x + _L1_gnn_ref(_layernorm(x, axis=-1), edge_index, edge_attr_4, L1_gnn_mlp_w, L1_gnn_mlp_b, L1_gnn_ew1, L1_gnn_ew2, L1_gnn_bn_g, L1_gnn_bn_b)
    x = x + _L1_ffn_ref(_layernorm(x, axis=-1)[None], L1_ffn_W_gat, L1_ffn_att_src, L1_ffn_att_dst, L1_ffn_b_gat, L1_ffn_ln_gamma, L1_ffn_ln_beta, L1_ffn_W1, L1_ffn_b1, L1_ffn_W2, L1_ffn_b2, L1_ffn_edge_index)[0]
    return x

_drawn_inputs = setup_inputs


def setup_inputs(seed=0):
    import zlib

    import numpy as np

    out = dict(_drawn_inputs(seed))
    spreads = {'L0_ffn_b1': (0.0, 0.1),
     'L0_ffn_b2': (0.0, 0.1),
     'L1_gnn_mlp_b': (0.0, 0.1),
     'L1_gnn_bn_g': (1.0, 0.2),
     'L1_gnn_bn_b': (0.0, 0.1),
     'L1_ffn_b_gat': (0.0, 0.1),
     'L1_ffn_ln_gamma': (1.0, 0.2),
     'L1_ffn_ln_beta': (0.0, 0.1),
     'L1_ffn_b1': (0.0, 0.351),
     'L1_ffn_b2': (0.0, 0.27)}
    factors = {'L1_ffn_att_src': 4.384, 'L1_ffn_att_dst': 23.367}
    for name, (base, spread) in spreads.items():
        noise = np.random.default_rng([zlib.crc32(name.encode()), seed]).standard_normal(out[name].shape)
        drawn = base * np.exp(spread * noise) if base else spread * noise
        out[name] = jnp.asarray(drawn.astype(out[name].dtype))
    for name, factor in factors.items():
        out[name] = (out[name] * factor).astype(out[name].dtype)
    return out
```

```python
from contextlib import ExitStack

import concourse.bass as bass
from concourse import mybir

F32 = mybir.dt.float32
I32 = mybir.dt.int32
ALU = mybir.AluOpType
ACT = mybir.ActivationFunctionType
AX = mybir.AxisListType
ds = bass.ds

P = 128
N, D = 6250, 256
NT = -(-N // P)
NP = NT * P
FB = D // P
E1 = 100000
E1P, E1T = 125, 800
E2 = 65536
E2T = E2 // P + NT
GT = 7
NG = NT // GT
GW = GT * P
HW = GW // 2
U = 8
LAYERS = 5
HEADS, XD = 4, 4
HX = HEADS * XD
XB = 8
LN_EPS = 1e-5
BN_EPS = 1e-5
BIG = 1e30
TW = D + 4
AW = HEADS + HX


def chunks_of(edges):
    most = (edges + NT * (P - 1)) // P
    return -(-most // (2 * U)) * 2 * U


NC1 = chunks_of(E1)
NC2 = chunks_of(E2 + NP)
RA, RC, RD = 3, 6, 2


class Chain:

    def __init__(self, eng, sem, base=0):
        self.eng, self.sem, self.n = eng, sem, base

    def __call__(self, ins):
        self.n = self.n + 1
        ins.then_inc(self.sem, 1)
        self.eng.wait_ge(self.sem, self.n)


def hold(eng):
    eng.nop(nofuse=True)


class Shared:
    pass


class Space:

    def __init__(self, nc, ctx, sems, name):
        self.nc, self.ctx, self.sems, self.name = nc, ctx, sems, name

    def sb(self, name, shape, dt=F32):
        return self.ctx.enter_context(self.nc.sbuf_tensor(f"{self.name}_{name}", shape, dt))[:]

    def ps(self, name, shape):
        return self.ctx.enter_context(self.nc.psum_tensor(f"{self.name}_{name}", shape, F32))[:]

    def sem(self, name, pool_dma=False):
        handle = self.nc.alloc_semaphore(f"{self.name}_{name}")
        if not pool_dma:
            self.sems.append(handle)
        return handle




class Sort:

    def __init__(self, sp, sh, parts, T, nchunks, key, rec, row, cw):
        self.sh, self.parts, self.T, self.nchunks = sh, parts, T, nchunks
        self.key, self.rec, self.row, self.cw = key, rec, row, cw
        self.tmp_i, self.tmp_j = sp.sb("tmp_i", [parts, T], I32), sp.sb("tmp_j", [parts, T], I32)
        self.win, self.mask = sp.sb("win", [parts, T]), sp.sb("mask", [parts, T])
        self.rank, self.pos = sp.sb("rank", [parts, T]), sp.sb("pos", [parts, T])
        self.count = sp.sb("count", [parts, 1])
        self.start, self.endcol = sp.sb("start", [P, 1]), sp.sb("endcol", [NT, 1])
        self.ends = sp.sb("ends", [P, NT + 1])
        self.len_i, self.len_j = sp.sb("len_i", [P, 1], I32), sp.sb("len_j", [P, 1], I32)
        self.len_f = sp.sb("len_f", [P, 1])
        self.after = sp.sb("after", [NT, nchunks])
        self.sums = sp.ps("sums", [P, 512])
        self.endps = self.sums[0:NT, 64:65]
        self.cwps = sp.ps("cwps", [P, 1024])[0:1, :]
        self.link, self.summed, self.turned = sp.sem("link"), sp.sem("summed"), sp.sem("turned")
        self.after_done, self.winsum, self.rows_done = sp.sem("after_done"), sp.sem("winsum"), sp.sem("rows_done")

    BEFORE, PER = 6, 8

    def dve(self, nc, dve):
        sh, parts = self.sh, self.parts
        link = Chain(dve, self.link)
        link(nc.vector.tensor_scalar(self.tmp_i, self.key, 7, None, ALU.arith_shift_right))
        link(nc.vector.tensor_copy(self.win, self.tmp_i))
        link(nc.vector.tensor_scalar(self.tmp_j, self.key, P - 1, None, ALU.bitwise_and))
        link(nc.vector.tensor_copy(self.rec[:, :, 1], self.tmp_j))
        link(nc.vector.memset(self.pos, 0.0))
        link(nc.vector.memset(self.ends[:, 0:1], 0.0))
        before, per = self.BEFORE, self.PER
        assert link.n == before
        with dve.Fori(0, NT) as w:
            link = Chain(dve, self.link, w * per + before)
            link(nc.vector.tensor_scalar(self.mask, self.win, sh.wincol[0:parts, ds(w, 1)], 0.0, ALU.is_equal,
                                         ALU.add, accum_out=self.count))
            dve.wait_ge(self.summed, w + 1)
            link(nc.vector.tensor_tensor(self.start[0:parts, :], self.sums[0:parts, 0:1],
                                         self.ends[0:parts, ds(w, 1)], ALU.add))
            link(nc.vector.tensor_tensor_scan(self.rank, sh.ones[0:parts, 0:1].to_broadcast([parts, self.T]),
                                              self.mask, self.start[0:parts, 0:1], ALU.mult, ALU.add))
            link(nc.vector.tensor_scalar(self.len_i, self.sums[:, 1:2], float(P - 1), None, ALU.add))
            link(nc.vector.tensor_scalar(self.len_j, self.len_i, 7, 7, ALU.arith_shift_right,
                                         ALU.arith_shift_left))
            link(nc.vector.tensor_copy(self.len_f, self.len_j))
            nc.vector.tensor_tensor(self.ends[:, ds(w + 1, 1)], self.ends[:, ds(w, 1)], self.len_f,
                                    ALU.add).then_inc(self.link, 1)
            link.n = link.n + 1
            link(nc.vector.copy_predicated(self.pos, self.mask.bitcast(I32), self.rank))
        link = Chain(dve, self.link, NT * per + before)
        link(nc.vector.tensor_scalar(self.pos, self.pos, -1.0, None, ALU.add))
        link(nc.vector.tensor_copy(self.tmp_i, self.pos))
        link(nc.vector.tensor_scalar(self.tmp_j, self.tmp_i, P - 1, None, ALU.bitwise_and))
        link(nc.vector.tensor_copy(self.rank, self.tmp_j))
        link(nc.vector.tensor_scalar(self.tmp_j, self.tmp_i, 7, None, ALU.arith_shift_right))
        link(nc.vector.tensor_copy(self.pos, self.tmp_j))
        nc.vector.scalar_tensor_tensor(self.row, self.rank, float(self.nchunks), self.pos, ALU.mult,
                                       ALU.add).then_inc(self.rows_done, 1)
        dve.wait_ge(self.turned, 1)
        link(nc.vector.tensor_copy(self.endcol, self.endps))
        nc.vector.tensor_scalar(self.after, sh.chunkrow[0:NT, 0:self.nchunks], self.endcol[:, 0:1], None,
                                ALU.is_ge).then_inc(self.after_done, 1)
        for n, b in enumerate(range(0, self.nchunks, 512)):
            m = min(512, self.nchunks - b)
            dve.wait_ge(self.winsum, n + 1)
            nc.vector.tensor_scalar(self.cw[:, b:b + m], self.cwps[:, b:b + m], float(NT - 1), None,
                                    ALU.min).then_inc(self.rows_done, 1)

    def pe(self, nc, pe):
        sh, parts = self.sh, self.parts
        with pe.Fori(0, NT) as w:
            pe.wait_ge(self.link, w * self.PER + (self.BEFORE + 1))
            nc.tensor.matmul(self.sums[:, 0:1], sh.below[0:parts, :], self.count, start=True, stop=True)
            nc.tensor.matmul(self.sums[:, 1:2], sh.ones[0:parts, :], self.count, start=True,
                             stop=True).then_inc(self.summed, 1)
        pe.wait_ge(self.link, NT * self.PER + self.BEFORE)
        nc.tensor.matmul(self.endps, self.ends[0:1, 1:NT + 1], sh.ones[0:1, 0:1], start=True,
                         stop=True).then_inc(self.turned, 1)
        pe.wait_ge(self.after_done, 1)
        for b in range(0, self.nchunks, 512):
            m = min(512, self.nchunks - b)
            nc.tensor.matmul(self.cwps[:, b:b + m], sh.ones[0:NT, 0:1], self.after[:, b:b + m], start=True,
                             stop=True).then_inc(self.winsum, 1)


class Scatter:

    def __init__(self, sp, parts, T, nchunks, row, rec, table, words):
        self.parts, self.T, self.row, self.rec, self.table, self.words = parts, T, row, rec, table, words
        self.sets = T // (2 * U)
        self.rest = T - self.sets * 2 * U
        self.at = [sp.sb(f"at{h}", [P, U], I32) for h in range(2)]
        self.what = [sp.sb(f"what{h}", [P, U * words]) for h in range(2)]
        self.ready = sp.sem("ready")
        self.written = [sp.sem(f"written{h}", pool_dma=True) for h in range(2)]

    def pool(self, nc, pool):
        with pool.Fori(0, self.sets) as i:
            for h in range(2):
                pool.wait_ge(self.written[h], i * (16 * U))
                self._send(nc, pool, h, (i * 2 + h) * U, U, (i * 2 + h) * 2 + 2)
        if self.rest:
            pool.wait_ge(self.written[0], self.sets * 16 * U)
            self._send(nc, pool, 0, self.sets * 2 * U, self.rest, self.sets * 4 + 2)
        pool.wait_ge(self.written[0], self.sets * 16 * U + 16 * self.rest)
        pool.wait_ge(self.written[1], self.sets * 16 * U)

    def _send(self, nc, pool, h, t, n, ready):
        p, w = self.parts, self.words
        flat = self.rec.rearrange("p t w -> p (t w)")
        nc.gpsimd.tensor_copy(self.at[h][0:p, 0:n], self.row[:, ds(t, n)]).then_inc(self.ready, 1)
        nc.gpsimd.tensor_copy(self.what[h][0:p, 0:n * w], flat[:, ds(t * w, n * w)]).then_inc(self.ready, 1)
        pool.wait_ge(self.ready, ready)
        hold(pool)
        for u in range(n):
            nc.gpsimd.indirect_dma_start(
                out=self.table, out_offset=bass.IndirectOffsetOnAxis(ap=self.at[h][0:p, u:u + 1], axis=0),
                in_=self.what[h][0:p, u * w:(u + 1) * w], in_offset=None).then_inc(self.written[h], 16)




class Gather:

    def __init__(self, sp, nchunks, edges, words, table, width, tracked=True, place=True):
        self.edges, self.words, self.table, self.width = edges, words, table, width
        self.iters = nchunks // (2 * U)
        self.idx = [sp.sb(f"idx{h}", [P, U], I32) for h in range(2)]
        self.rows = [sp.sb(f"rows{h}", [P, U, width]) for h in range(2)] if place else None
        self.ready = [sp.sem(f"ready{h}") for h in range(2)]
        self.here = [sp.sem(f"here{h}", pool_dma=True) for h in range(2)]
        self.used = sp.sem("used") if tracked else None

    def act_set(self, nc, act, it, i, h):
        act.wait_ge(self.here[h], it * (16 * U))
        nodes = self.edges[:, ds((i * 2 + h) * U, U), 0].bitcast(I32)
        nc.scalar.copy(self.idx[h], nodes).then_inc(self.ready[h], 1)

    def pool_set(self, nc, pool, it, h):
        pool.wait_ge(self.ready[h], it + 1)
        if self.used is not None:
            pool.wait_ge(self.used, it * (2 * U) + h * U)
        hold(pool)
        for u in range(U):
            nc.gpsimd.indirect_dma_start(
                out=self.rows[h][:, u, :], out_offset=None, in_=self.table,
                in_offset=bass.IndirectOffsetOnAxis(ap=self.idx[h][:, u:u + 1], axis=0)).then_inc(self.here[h], 16)


class Aggregate:

    BANKS = 4

    def __init__(self, sp, sh, g, edges, cw, agg, weighted, agge=None, place=True):
        self.sh, self.g, self.edges, self.cw, self.agg, self.weighted, self.agge = sh, g, edges, cw, agg, weighted, agge
        self.hot = [sp.sb(f"hot{h}", [P, U, P]) for h in range(2)] if place else None
        self.hot_ready = [sp.sem(f"hot_ready{h}") for h in range(2)]
        self.bank = [sp.ps(f"bank{b}", [P, 512]) for b in range(self.BANKS)]
        self.added = [sp.sem(f"added{b}") for b in range(self.BANKS)]
        if agge is not None:
            self.attr = [sp.sb(f"attr{h}", [P, U, 4]) for h in range(2)]

    def dve_set(self, nc, dve, it, i, h, edge_terms):
        per = U // self.BANKS
        dve.wait_ge(self.g.used, it * (2 * U) + h * U)
        for u in range(U):
            c = (i * 2 + h) * U + u
            place = self.edges[:, ds(c, 1), 1]
            if self.weighted:
                ins = nc.vector.tensor_scalar(self.hot[h][:, u, :], self.sh.iota, place, self.edges[:, ds(c, 1), 2],
                                              ALU.is_equal, ALU.mult)
            else:
                ins = nc.vector.tensor_scalar(self.hot[h][:, u, :], self.sh.iota, place, None, ALU.is_equal)
        if edge_terms:
            dve.wait_ge(self.g.here[h], (it + 1) * (16 * U))
            ins = nc.vector.tensor_tensor(self.attr[h], self.edges[:, ds((i * 2 + h) * U, U), 2:6],
                                          self.g.rows[h][:, :, D:D + 1].to_broadcast([P, U, 4]), ALU.mult)
        ins.then_inc(self.hot_ready[h], 1)
        for u in range(U):
            c = (i * 2 + h) * U + u
            b = u % self.BANKS
            w = dve.value_load(self.cw[0:1, ds(c, 1)], min_val=0, max_val=NT - 1)
            dve.wait_ge(self.g.used, it * (2 * U) + (h * U + u + 1 + U))
            prev = (u - 1) % self.BANKS
            done = (it * 2 + h) * per + (u + self.BANKS - 1 - prev) // self.BANKS
            dve.wait_ge(self.added[prev], done)
            to = self.agg[:, :, ds(w * P, P)]
            prod = self.bank[b][:, 0:D].rearrange("p (f n) -> p f n", f=FB)
            if edge_terms:
                te = self.agge[:, ds(w * P, P)]
                nc.vector.tensor_tensor(te, te, self.bank[b][0:4, D:D + P], ALU.add)
            nc.vector.tensor_tensor(to, to, prod, ALU.add).then_inc(self.added[b], 1)

    def pe_set(self, nc, pe, it, h, edge_terms):
        per = U // self.BANKS
        pe.wait_ge(self.hot_ready[h], it + 1)
        pe.wait_ge(self.g.here[h], (it + 1) * (16 * U))
        for u in range(U):
            b = u % self.BANKS
            pe.wait_ge(self.added[b], (it * 2 + h) * per + u // self.BANKS)
            for f in range(FB):
                ins = nc.tensor.matmul(self.bank[b][:, f * P:(f + 1) * P], self.g.rows[h][:, u, f * P:(f + 1) * P],
                                       self.hot[h][:, u, :], start=True, stop=True)
            if edge_terms:
                ins = nc.tensor.matmul(self.bank[b][0:4, D:D + P], self.attr[h][:, u, :], self.hot[h][:, u, :],
                                       start=True, stop=True)
            ins.then_inc(self.g.used, 1)




def group_rows(table, g):
    return table[ds(g * GW, GW), :].rearrange("(t p) d -> p t d", p=P)


class Ffn:

    def __init__(self, sp, sh, tok, E, HB, w1, b1, w2, b2, func, share, base, out):
        self.sh, self.tok, self.E, self.HB, self.func, self.share = sh, tok, E, HB, func, share
        self.base, self.out = base, out
        self.d = (w1, b1, w2, b2)
        self.w1, self.b1 = sp.sb("w1", [P, E, FB, HB * P]), sp.sb("b1", [P, E * HB])
        self.w2, self.b2 = sp.sb("w2", [P, E * HB, D]), sp.sb("b2", [P, E, D])
        self.nh = min(2, E)
        self.hid = [sp.sb(f"hid{j}", [P, HB, GW]) for j in range(self.nh)]
        self.acc = sp.sb("acc", [P, GT, D])
        self.pre = [sp.ps(f"pre{j}", [P, 2, 512]) for j in range(2)]
        self.y = [sp.ps(f"y{j}", [P, 512]) for j in range(4)]
        self.loaded, self.pre_done = sp.sem("loaded"), sp.sem("pre_done")
        self.act_done = [sp.sem(f"act_done{j}") for j in range(2)]
        self.y_done = sp.sem("y_done")
        self.y_used = [sp.sem(f"y_used{j}") for j in range(4)]
        self.base_here, self.link, self.stored = sp.sem("base_here"), sp.sem("link"), sp.sem("stored")

    def sp_load(self, nc, sp):
        w1, b1, w2, b2 = self.d
        for e in range(self.E):
            sp.dma_start(self.w1[:, e], w1[e].rearrange("(f p) h -> p f h", p=P)).then_inc(self.loaded, 16)
            sp.dma_start(self.w2[:, e * self.HB:(e + 1) * self.HB],
                         w2[e].rearrange("(b p) d -> p b d", p=P)).then_inc(self.loaded, 16)
        sp.dma_start(self.b1, b1.rearrange("e (b p) -> p (e b)", p=P),
                     allow_slow_non_contiguous=True).then_inc(self.loaded, 16)
        sp.dma_start(self.b2, b2.partition_broadcast(P)).then_inc(self.loaded, 16)

    LOADS = property(lambda self: 16 * (2 * self.E + 2))

    def sp(self, nc, sp):
        def group(g):
            sp.wait_ge(self.stored, g * 16)
            hold(sp)
            sp.dma_start(self.acc, group_rows(self.base, g)).then_inc(self.base_here, 16)
            for j in range(4):
                sp.wait_ge(self.y_used[j], (g + 1) * (self.E * len(range(j, GT, 4))))
                hold(sp)

        with sp.Fori(0, NG - 1) as g:
            group(g)
            sp.dma_start(group_rows(self.out, g), self.acc).then_inc(self.stored, 16)
        group(NG - 1)
        rows = self.out.shape[0] - (NG - 1) * GW
        whole, rest = rows // P, rows % P
        at = (NG - 1) * GW
        sp.dma_start(self.out[at:at + whole * P, :].rearrange("(t p) d -> p t d", p=P),
                     self.acc[:, 0:whole, :]).then_inc(self.stored, 16)
        if rest:
            sp.dma_start(self.out[at + whole * P:at + rows, :], self.acc[0:rest, whole, :]).then_inc(self.stored, 16)
        sp.wait_ge(self.stored, NG * 16 + (16 if rest else 0))

    def pe(self, nc, pe):
        E, HB = self.E, self.HB
        pe.wait_ge(self.loaded, self.LOADS)

        def up(g, e):
            for b in range(HB):
                j = b % 2
                pe.wait_ge(self.act_done[j], (g * E + e) * (HB // 2) + b // 2)
                for m in range(2):
                    for f in range(FB):
                        ins = nc.tensor.matmul(self.pre[j][:, m, 0:HW], self.w1[:, e, f, b * P:(b + 1) * P],
                                               self.tok[:, f, ds(g * GW + m * HW, HW)], start=(f == 0),
                                               stop=(f == FB - 1))
                ins.then_inc(self.pre_done, 1)

        def down(g, e):
            for j in range(2):
                pe.wait_ge(self.act_done[j], (g * E + e + 1) * (HB // 2))
            for s in range(GT):
                j = s % 4
                n = len(range(j, GT, 4))
                pe.wait_ge(self.y_used[j], (g * E + e) * n + s // 4)
                for b in range(HB):
                    ins = nc.tensor.matmul(self.y[j][:, 0:D], self.hid[e % self.nh][:, b, s * P:(s + 1) * P],
                                           self.w2[:, e * HB + b, :], start=(b == 0), stop=(b == HB - 1))
                ins.then_inc(self.y_done, 1)

        nc.tensor.sem_inc(self.y_done, self.nh * GT)
        with pe.Fori(0, NG) as g:
            up(g, 0)
            for e in range(E):
                if e + 1 < E:
                    up(g, e + 1)
                down(g, e)

    def act(self, nc, act):
        E, HB, nh = self.E, self.HB, self.nh
        act.wait_ge(self.loaded, self.LOADS)
        hold(act)
        with act.Fori(0, NG) as g:
            for e in range(E):
                act.wait_ge(self.y_done, (g * E + e + 1) * GT)
                for b in range(HB):
                    act.wait_ge(self.pre_done, (g * E + e) * HB + b + 1)
                    nc.scalar.activation(self.hid[e % nh][:, b, :].rearrange("p (m n) -> p m n", m=2),
                                         self.pre[b % 2][:, :, 0:HW], self.func,
                                         bias=self.b1[:, e * HB + b:e * HB + b + 1]).then_inc(self.act_done[b % 2], 1)

    def dve(self, nc, dve):
        E = self.E
        dve.wait_ge(self.loaded, self.LOADS)
        hold(dve)
        with dve.Fori(0, NG) as g:
            dve.wait_ge(self.base_here, (g + 1) * 16)
            for e in range(E):
                for s in range(GT):
                    j = s % 4
                    n = len(range(j, GT, 4))
                    share = self.share[:, ds(g * GT + s, 1), e]
                    a = self.acc[:, s, :]
                    dve.wait_ge(self.y_used[j], (g * E + e) * n + s // 4)
                    nc.vector.scalar_tensor_tensor(a, self.b2[:, e, :], share, a, ALU.mult,
                                                   ALU.add).then_inc(self.link, 1)
                    dve.wait_ge(self.link, (g * E + e) * GT + s + 1)
                    dve.wait_ge(self.y_done, (g * E + e + self.nh) * GT + s + 1)
                    nc.vector.scalar_tensor_tensor(a, self.y[j][:, 0:D], share, a, ALU.mult,
                                                   ALU.add).then_inc(self.y_used[j], 1)


class Norm:

    def __init__(self, sp, sh, src, normed=None, both=None, tok=None, head=None, head_out=None, add=None,
                 summed=None):
        self.sh, self.src, self.normed, self.both, self.tok = sh, src, normed, both, tok
        self.head, self.head_out, self.add, self.summed = head, head_out, add, summed
        self.x, self.xn = sp.sb("x", [P, GT, D]), sp.sb("xn", [P, GT, D])
        self.sum = sp.sb("sum", [P, GT, D]) if both is not None else None
        self.stats, self.mv, self.rstd = sp.sb("stats", [P, GT, 6]), sp.sb("mv", [P, GT, 2]), sp.sb("rstd", [P, GT])
        if tok is not None:
            self.turn = [sp.ps(f"turn{j}", [P, 512]) for j in range(4)]
        self.here, self.link, self.stored = sp.sem("here"), sp.sem("link"), sp.sem("stored")
        self.var_done, self.root_done = sp.sem("var_done"), sp.sem("root_done")
        self.turned, self.xn_done, self.out_done = sp.sem("turned"), sp.sem("xn_done"), sp.sem("out_done")
        self.stores = (normed is not None) + (both is not None) + (summed is not None)
        if tok is not None:
            self.slot = sp.sb("slot", [P, GT, D])
            self.copied = [sp.sem(f"copied{j}") for j in range(2)]
            self.slotted = sp.sem("slotted")
        if head is not None:
            self.M = head_out.shape[2]
            self.prod = sp.ps("prod", [P, 512])
            self.head_done, self.head_used = sp.sem("head_done"), sp.sem("head_used")
        if add is not None:
            self.raw = sp.sb("raw", [P, FB, GW])
            self.applied = sp.sem("applied")
            self.added = [sp.sem(f"added{j}") for j in range(2)]
            self.add_turned = sp.sem("add_turned")

    def sp(self, nc, sp):
        with sp.Fori(0, NG) as g:
            sp.wait_ge(self.stored, g * (16 * self.stores))
            hold(sp)
            sp.wait_ge(self.out_done, g)
            hold(sp)
            sp.dma_start(self.x, group_rows(self.src, g)).then_inc(self.here, 16)
            if self.summed is not None:
                sp.wait_ge(self.added[0], (g + 1) * 4)
                hold(sp)
                sp.wait_ge(self.added[1], (g + 1) * 3)
                hold(sp)
                sp.dma_start(group_rows(self.summed, g), self.x).then_inc(self.stored, 16)
            sp.wait_ge(self.out_done, g + 1)
            hold(sp)
            if self.normed is not None:
                sp.dma_start(group_rows(self.normed, g), self.xn).then_inc(self.stored, 16)
            if self.both is not None:
                sp.dma_start(group_rows(self.both, g), self.sum).then_inc(self.stored, 16)
        sp.wait_ge(self.stored, NG * 16 * self.stores)

    PER = 3

    def dve(self, nc, dve):
        with dve.Fori(0, NG) as g:
            link = Chain(dve, self.link, g * self.PER)
            dve.wait_ge(self.here, (g + 1) * 16)
            if self.add is not None:
                for t in range(GT):
                    dve.wait_ge(self.add_turned, g * GT + t + 1)
                    nc.vector.tensor_tensor(self.x[:, t, :], self.x[:, t, :], self.turn[t % 2][:, 0:D],
                                            ALU.add).then_inc(self.added[t % 2], 1)
                dve.wait_ge(self.added[0], (g + 1) * 4)
                dve.wait_ge(self.added[1], (g + 1) * 3)
            for t in range(GT):
                ins = nc.vector.bn_stats(self.stats[:, t, :], self.x[:, t, :])
            link(ins)
            hold(dve)
            for t in range(GT):
                ins = nc.vector.bn_aggr(self.mv[:, t, :], self.stats[:, t, :])
            link(ins)
            nc.vector.tensor_scalar(self.rstd, self.mv[:, :, 1], LN_EPS, None, ALU.add).then_inc(self.var_done, 1)
            dve.wait_ge(self.root_done, g + 1)
            link(nc.vector.reciprocal(self.rstd, self.rstd))
            if self.tok is not None:
                dve.wait_ge(self.turned, g * GT)
            for t in range(GT):
                ins = nc.vector.tensor_scalar(self.xn[:, t, :], self.x[:, t, :], self.mv[:, t, 0:1],
                                              self.rstd[:, t:t + 1], ALU.subtract, ALU.mult)
                ins.then_inc(self.xn_done, 1)
            dve.wait_ge(self.xn_done, (g + 1) * GT)
            if self.both is not None:
                nc.vector.tensor_tensor(self.sum, self.x, self.xn, ALU.add).then_inc(self.out_done, 1)
            else:
                nc.vector.sem_inc(self.out_done, 1)
            if self.head is not None:
                dve.wait_ge(self.head_done, (g + 1) * GT)
                nc.vector.tensor_copy(self.head_out[:, ds(g * GT, GT), :],
                                      self.prod[:, 0:GT * 64].rearrange("p (t m) -> p t m", t=GT)[:, :, 0:self.M]
                                      ).then_inc(self.head_used, 1)

    def pe(self, nc, pe):
        if self.add is None and self.tok is None:
            return
        with pe.Fori(0, NG) as g:
            if self.add is not None:
                pe.wait_ge(self.applied, g + 1)
                for t in range(GT):
                    j = t % 2
                    pe.wait_ge(self.added[j], g * (4 - j) + t // 2)
                    for f in range(FB):
                        ins = nc.tensor.transpose(self.turn[j][:, f * P:(f + 1) * P],
                                                  self.raw[:, f, t * P:(t + 1) * P], self.sh.ident)
                    ins.then_inc(self.add_turned, 1)

            def head(t):
                pe.wait_ge(self.slotted, g * GT + t + 1)
                if t == 0:
                    pe.wait_ge(self.head_used, g)
                for f in range(FB):
                    ins = nc.tensor.matmul(self.prod[:, t * 64:t * 64 + self.M], self.slot[:, t, f * P:(f + 1) * P],
                                           self.head[:, f, :], start=(f == 0), stop=(f == FB - 1))
                ins.then_inc(self.head_done, 1)

            for t in range(GT):
                j = t % 2
                pe.wait_ge(self.xn_done, g * GT + t + 1)
                pe.wait_ge(self.copied[j], g * (4 - j) + t // 2)
                for f in range(FB):
                    ins = nc.tensor.transpose(self.turn[2 + j][:, f * P:(f + 1) * P],
                                              self.xn[:, t, f * P:(f + 1) * P], self.sh.ident)
                ins.then_inc(self.turned, 1)
                if self.head is not None and t:
                    head(t - 1)
            if self.head is not None:
                head(GT - 1)

    def act(self, nc, act):
        with act.Fori(0, NG) as g:
            if self.add is not None:
                act.wait_ge(self.add_turned, g * GT)
                for f in range(FB):
                    ins = nc.scalar.activation(self.raw[:, f, :], self.add[:, f, ds(g * GW, GW)], ACT.Identity,
                                               bias=self.sh.shift[:, f:f + 1], scale=self.sh.scale[:, f:f + 1])
                ins.then_inc(self.applied, 1)
            act.wait_ge(self.var_done, g + 1)
            nc.scalar.activation(self.rstd, self.rstd, ACT.Sqrt).then_inc(self.root_done, 1)
            for t in range(GT if self.tok is not None else 0):
                j = t % 2
                act.wait_ge(self.turned, g * GT + t + 1)
                if self.head is not None:
                    act.wait_ge(self.head_done, g * GT)
                    nc.scalar.copy(self.slot[:, t, :], self.turn[2 + j][:, 0:D]).then_inc(self.slotted, 1)
                nc.scalar.copy(self.tok[:, :, ds((g * GT + t) * P, P)],
                               self.turn[2 + j][:, 0:D].rearrange("p (f n) -> p f n", f=FB)).then_inc(self.copied[j], 1)


class Degree:

    def __init__(self, sp, sh, edges, cw):
        self.sh, self.edges, self.cw, self.iters = sh, edges, cw, NC1 // (2 * U)
        self.hot = [sp.sb(f"hot{h}", [P, U, P]) for h in range(2)]
        self.bank = [sp.ps(f"bank{j}", [P, 512]) for j in range(4)]
        self.junk, self.low = sp.sb("junk", [P, P]), sp.sb("low", [P, GW])
        self.hot_ready, self.counted, self.added = sp.sem("hot_ready"), sp.sem("counted"), sp.sem("added")
        self.link, self.some_done, self.root_done = sp.sem("link"), sp.sem("some_done"), sp.sem("root_done")

    def dve(self, nc, dve):
        sh = self.sh
        link = Chain(dve, self.link)
        link(nc.vector.memset(sh.dinv_row, 0.0))
        with dve.Fori(0, self.iters) as i:
            for h in range(2):
                dve.wait_ge(self.counted, i * 4)
                for u in range(U):
                    ins = nc.vector.tensor_scalar(self.hot[h][:, u, :], sh.iota,
                                                  self.edges[:, ds((i * 2 + h) * U + u, 1), 1], None, ALU.is_equal)
                ins.then_inc(self.hot_ready, 1)
            for h in range(2):
                for u in range(U):
                    c = h * U + u
                    w = dve.value_load(self.cw[0:1, ds(i * (2 * U) + c, 1)], min_val=0, max_val=NT - 1)
                    dve.wait_ge(self.counted, i * 4 + (c // 4 + 1))
                    dve.wait_ge(self.added, i * (2 * U) + c)
                    to = sh.dinv_row[:, ds(w * P, P)]
                    nc.vector.tensor_tensor(to, to, self.bank[c // 4][:, (c % 4) * P:(c % 4 + 1) * P],
                                            ALU.add).then_inc(self.added, 1)
        dve.wait_ge(self.added, NC1)
        for g in range(NG):
            row = sh.dinv_row[:, g * GW:(g + 1) * GW]
            link(nc.vector.tensor_scalar(self.low, row, 1.0, None, ALU.min))
            nc.vector.tensor_scalar(row, row, 1.0, None, ALU.max).then_inc(self.some_done, 1)
            dve.wait_ge(self.root_done, g + 1)
            link(nc.vector.reciprocal(row, row))
            link(nc.vector.tensor_tensor(row, row, self.low, ALU.mult))
        for t in range(NT):
            link(nc.vector.tensor_tensor(self.junk, sh.dinv_row[:, t * P:(t + 1) * P], sh.ident, ALU.mult))
            link(nc.vector.tensor_reduce(sh.dinv_col[:, t:t + 1], self.junk, AX.X, ALU.add))

    def act(self, nc, act):
        for g in range(NG):
            row = self.sh.dinv_row[:, g * GW:(g + 1) * GW]
            act.wait_ge(self.some_done, g + 1)
            nc.scalar.activation(row, row, ACT.Sqrt).then_inc(self.root_done, 1)

    def pe(self, nc, pe):
        with pe.Fori(0, self.iters) as i:
            for h in range(2):
                pe.wait_ge(self.hot_ready, i * 2 + (h + 1))
                if h == 0:
                    pe.wait_ge(self.added, i * (2 * U))
                for q in range(2):
                    nc.tensor.matmul(self.bank[2 * h + q], self.sh.ones,
                                     self.hot[h][:, q * 4:(q + 1) * 4, :].rearrange("p u n -> p (u n)"),
                                     start=True, stop=True).then_inc(self.counted, 1)


class Layers:

    TILES = NP // HW
    LAST = N - (NP // HW - 1) * HW

    def __init__(self, sp, sh, edges, cw, table, mlp_w, mlp_b, ew1, ew2, bn_g, bn_b):
        self.sh, self.d, self.table = sh, (mlp_w, mlp_b, ew1, ew2, bn_g, bn_b), table
        self.g = Gather(sp, NC1, edges, RC, table, TW, place=False)
        self.agge = sp.sb("agge", [4, NP])
        self.a = Aggregate(sp, sh, self.g, edges, cw, sh.agg, False, self.agge, place=False)
        both = FB * GW
        place = sp.sb("place", [P, 2 * U * TW])
        self.g.rows = [place[:, h * U * TW:(h + 1) * U * TW].rearrange("p (u w) -> p u w", u=U) for h in range(2)]
        by_block = lambda a: a.rearrange("p (f n) -> p f n", f=FB)
        self.raw, self.clamped = by_block(place[:, 0:both]), by_block(place[:, both:2 * both])
        self.full = [by_block(place[:, j * both // 2:(j + 1) * both // 2]) for j in range(2)]
        hots = sp.sb("hots", [P, 2 * U * P])
        self.a.hot = [hots[:, h * U * P:(h + 1) * U * P].rearrange("p (u n) -> p u n", u=U) for h in range(2)]
        self.rows = hots[:, 0:GT * TW].rearrange("p (t w) -> p t w", t=GT)
        self.w, self.ew = sp.sb("w", [P, 2 * FB, D]), sp.sb("ew", [4, D])
        self.b, self.bn_g, self.bn_b = (sp.sb(n, [P, LAYERS * FB]) for n in ("b", "bn_g", "bn_b"))
        self.stats, self.mv = sp.sb("stats", [P, FB, self.TILES, 6]), sp.sb("mv", [P, FB, 2])
        self.rstd, self.part = sp.sb("rstd", [P, FB]), sp.sb("part", [P, FB])
        self.turn = [sp.ps(f"turn{j}", [P, 512]) for j in range(2)]
        self.edge = sp.ps("edge", [P, 2, 512])
        self.link, self.var_done, self.root_done = sp.sem("link"), sp.sem("var_done"), sp.sem("root_done")
        self.loaded, self.w_here = sp.sem("loaded"), sp.sem("w_here")
        self.normed, self.clamp_done, self.back = sp.sem("normed"), sp.sem("clamp_done"), sp.sem("back")
        self.turned = sp.sem("turned")
        self.row_done = [sp.sem(f"row_done{j}") for j in range(2)]
        self.stored, self.zeroed = sp.sem("stored"), sp.sem("zeroed")
        self.edge_done, self.edge_used, self.full_done = sp.sem("edge_done"), sp.sem("edge_used"), sp.sem("full_done")
        self.mixed, self.relu_done, self.bn_ready = sp.sem("mixed"), sp.sem("relu_done"), sp.sem("bn_ready")

    def each(self, eng, layer):
        layer(0, True)
        with eng.Fori(1, LAYERS) as l:
            layer(l, False)

    def sp(self, nc, sp):
        mlp_w, mlp_b, ew1, ew2, bn_g, bn_b = self.d
        for to, src in ((self.b, mlp_b), (self.bn_g, bn_g), (self.bn_b, bn_b)):
            sp.dma_start(to, src.rearrange("l (f p) -> p (l f)", p=P),
                         allow_slow_non_contiguous=True).then_inc(self.loaded, 16)

        def layer(l, first):
            sp.wait_ge(self.bn_ready, l + 1)
            hold(sp)
            sp.dma_start(self.w, mlp_w[ds(l, 1)].rearrange("l (k p) d -> p (l k) d", p=P)).then_inc(self.w_here, 16)
            sp.dma_start(self.ew[3:4, 0:P], ew1[ds(l, 1)].rearrange("l k d -> (l k) d")).then_inc(self.w_here, 16)
            sp.dma_start(self.ew[0:3, P:D], ew2[ds(l, 1)].rearrange("l k d -> (l k) d")).then_inc(self.w_here, 16)
            with sp.Fori(0, NG) as g:
                it = l * NG + g
                for j in range(2):
                    sp.wait_ge(self.row_done[j], (it + 1) * (4 - j))
                    hold(sp)
                hold(sp)
                sp.dma_start(group_rows(self.table, g), self.rows).then_inc(self.stored, 16)
        self.each(sp, layer)

    def act(self, nc, act):
        sh = self.sh
        act.wait_ge(self.loaded, 48)

        def layer(l, first):
            act.wait_ge(self.bn_ready, l + 1)
            hold(act)
            with act.Fori(0, NG) as g:
                it = l * NG + g
                here = sh.h[:, :, ds(g * GW, GW)]
                act.wait_ge(self.clamp_done, it)
                for f in range(FB):
                    ins = nc.scalar.activation(self.raw[:, f, :], sh.h[:, f, ds(g * GW, GW)], ACT.Identity,
                                               bias=sh.shift[:, f:f + 1], scale=sh.scale[:, f:f + 1])
                ins.then_inc(self.normed, 1)
                act.wait_ge(self.clamp_done, it + 1)
                hold(act)
                nc.scalar.copy(here, self.clamped).then_inc(self.back, 1)
            with act.Fori(0, self.g.iters) as i:
                for h in range(2):
                    self.g.act_set(nc, act, l * self.g.iters + i, i, h)
            with act.Fori(0, self.TILES // 2) as m2:
                for j in range(2):
                    act.wait_ge(self.mixed, l * self.TILES + m2 * 2 + (j + 1))
                    for o in range(FB):
                        ins = nc.scalar.activation(sh.h[:, o, ds((m2 * 2 + j) * HW, HW)],
                                                   self.a.bank[2 * j + o][:, 0:HW], ACT.Relu,
                                                   bias=self.b[:, ds(l * FB + o, 1)])
                    ins.then_inc(self.relu_done, 1)
            act.wait_ge(self.var_done, l + 1)
            nc.scalar.activation(self.rstd, self.rstd, ACT.Sqrt).then_inc(self.root_done, 1)
        self.each(act, layer)

    def pool(self, nc, pool):
        def layer(l, first):
            if first:
                nc.gpsimd.memset(self.agge, 0.0).then_inc(self.zeroed, 1)
            else:
                pool.wait_ge(self.full_done, l * self.TILES)
            hold(pool)
            nc.gpsimd.memset(self.sh.agg, 0.0).then_inc(self.zeroed, 1)
            pool.wait_ge(self.stored, (l + 1) * (NG * 16))
            pool.wait_ge(self.back, (l + 1) * NG)
            hold(pool)
            with pool.Fori(0, self.g.iters) as i:
                for h in range(2):
                    self.g.pool_set(nc, pool, l * self.g.iters + i, h)
        self.each(pool, layer)

    def pe(self, nc, pe):
        sh = self.sh
        nc.tensor.sem_inc(self.g.used, U)

        def layer(l, first):
            with pe.Fori(0, NG) as g:
                it = l * NG + g
                pe.wait_ge(self.clamp_done, it + 1)
                for t in range(GT):
                    j = t % 2
                    pe.wait_ge(self.row_done[j], it * (4 - j) + t // 2)
                    for f in range(FB):
                        ins = nc.tensor.transpose(self.turn[j][:, f * P:(f + 1) * P],
                                                  self.clamped[:, f, t * P:(t + 1) * P], sh.ident)
                    ins.then_inc(self.turned, 1)
            if not first:
                pe.wait_ge(self.relu_done, l * self.TILES)
            hold(pe)
            with pe.Fori(0, self.g.iters) as i:
                for h in range(2):
                    self.a.pe_set(nc, pe, l * self.g.iters + i, h, first)
            pe.wait_ge(self.w_here, (l + 1) * 48)
            pe.wait_ge(self.back, (l + 1) * NG)
            for b in range(Aggregate.BANKS):
                pe.wait_ge(self.a.added[b], (l + 1) * (NC1 // Aggregate.BANKS))
            hold(pe)
            with pe.Fori(0, self.TILES // 2) as m2:
                for j in range(2):
                    m = m2 * 2 + j
                    it = l * self.TILES + m2 * 2 + j
                    pe.wait_ge(self.edge_used, it)
                    for f in range(FB):
                        ins = nc.tensor.matmul(self.edge[:, f, 0:HW], self.ew[:, f * P:(f + 1) * P],
                                               self.agge[:, ds(m * HW, HW)], start=True, stop=True)
                    ins.then_inc(self.edge_done, 1)
                    pe.wait_ge(self.full_done, it + 1)
                    pe.wait_ge(self.relu_done, l * self.TILES + m2 * 2)
                    for o in range(FB):
                        for kk in range(2 * FB):
                            rhs = sh.h[:, kk, ds(m * HW, HW)] if kk < FB else self.full[j][:, kk - FB, :]
                            ins = nc.tensor.matmul(self.a.bank[2 * j + o][:, 0:HW], self.w[:, kk, o * P:(o + 1) * P],
                                                   rhs, start=(kk == 0), stop=(kk == 2 * FB - 1))
                    ins.then_inc(self.mixed, 1)
        self.each(pe, layer)

    PER = 5

    def dve(self, nc, dve):
        sh = self.sh
        link0 = Chain(dve, self.link)
        link0(nc.vector.memset(sh.scale, 1.0))
        link0(nc.vector.memset(sh.shift, 0.0))
        link0(nc.vector.memset(self.ew, 0.0))
        nc.vector.sem_inc(self.bn_ready, 1)
        dve.wait_ge(self.loaded, 48)
        before = link0.n

        def layer(l, first):
            with dve.Fori(0, NG) as g:
                it = l * NG + g
                dve.wait_ge(self.normed, it + 1)
                dve.wait_ge(self.turned, it * GT)
                dve.wait_ge(self.back, it)
                nc.vector.tensor_scalar(self.clamped, self.raw, -3e38 if first else 0.0, None,
                                        ALU.max).then_inc(self.clamp_done, 1)
                dve.wait_ge(self.stored, it * 16)
                nc.vector.tensor_copy(self.rows[:, :, D:TW], sh.dinv_col[:, ds(g * GT, GT)].rearrange(
                    "p (t o) -> p t o", o=1).to_broadcast([P, GT, TW - D]))
                for t in range(GT):
                    j = t % 2
                    dve.wait_ge(self.turned, it * GT + (t + 1))
                    nc.vector.tensor_scalar(self.rows[:, t, 0:D], self.turn[j][:, 0:D],
                                            sh.dinv_col[:, ds(g * GT + t, 1)], None,
                                            ALU.mult).then_inc(self.row_done[j], 1)
            dve.wait_ge(self.zeroed, l + 2)
            dve.wait_ge(self.stored, (l + 1) * (NG * 16))
            hold(dve)
            with dve.Fori(0, self.g.iters) as i:
                for h in range(2):
                    self.a.dve_set(nc, dve, l * self.g.iters + i, i, h, first)
            for b in range(Aggregate.BANKS):
                dve.wait_ge(self.a.added[b], (l + 1) * (NC1 // Aggregate.BANKS))
            hold(dve)
            with dve.Fori(0, self.TILES // 2) as m2:
                for j in range(2):
                    m = m2 * 2 + j
                    it = l * self.TILES + m2 * 2 + j
                    dve.wait_ge(self.edge_done, it + 1)
                    dve.wait_ge(self.mixed, l * self.TILES + m2 * 2)
                    nc.vector.tensor_tensor(self.full[j], self.edge[:, :, 0:HW], sh.agg[:, :, ds(m * HW, HW)],
                                            ALU.add).then_inc(self.edge_used, 1)
                    dve.wait_ge(self.edge_used, it + 1)
                    for f in range(FB):
                        ins = nc.vector.tensor_tensor(self.full[j][:, f, :], self.full[j][:, f, :],
                                                      sh.dinv_row[:, ds(m * HW, HW)], ALU.mult)
                    ins.then_inc(self.full_done, 1)
            link = Chain(dve, self.link, l * self.PER + before)
            for m in range(self.TILES):
                n = HW if m + 1 < self.TILES else self.LAST
                dve.wait_ge(self.relu_done, l * self.TILES + (m + 1))
                for o in range(FB):
                    ins = nc.vector.bn_stats(self.stats[:, o, m, :], sh.h[:, o, m * HW:m * HW + n])
            link(ins)
            hold(dve)
            for o in range(FB):
                ins = nc.vector.bn_aggr(self.mv[:, o, :], self.stats[:, o].rearrange("p m s -> p (m s)"))
            link(ins)
            nc.vector.tensor_scalar(self.rstd, self.mv[:, :, 1], BN_EPS, None, ALU.add).then_inc(self.var_done, 1)
            dve.wait_ge(self.root_done, l + 1)
            link(nc.vector.reciprocal(self.rstd, self.rstd))
            dve.wait_ge(self.normed, (l + 1) * NG)
            link(nc.vector.tensor_tensor(sh.scale, self.bn_g[:, ds(l * FB, FB)], self.rstd, ALU.mult))
            link(nc.vector.tensor_tensor(self.part, self.mv[:, :, 0], sh.scale, ALU.mult))
            nc.vector.tensor_tensor(sh.shift, self.bn_b[:, ds(l * FB, FB)], self.part,
                                    ALU.subtract).then_inc(self.bn_ready, 1)
        self.each(dve, layer)


def top2(nc, link, v, rank, cmp, E):
    link(nc.vector.memset(rank, 0.0))
    for j in range(E):
        for lo, hi, op in ((0, j, ALU.is_gt), (j + 1, E, ALU.is_ge)):
            if lo < hi:
                link(nc.vector.tensor_tensor(cmp[:, :, lo:hi], v[:, :, j:j + 1].to_broadcast([P, NT, hi - lo]),
                                             v[:, :, lo:hi], op))
                link(nc.vector.tensor_tensor(rank[:, :, lo:hi], rank[:, :, lo:hi], cmp[:, :, lo:hi], ALU.add))


class Shares:

    def __init__(self, sp, v, E, all_first, share):
        self.v, self.E, self.all_first, self.share = v, E, all_first, share
        self.rank, self.cmp, self.ex = (sp.sb(n, [P, NT, E]) for n in ("rank", "cmp", "ex"))
        self.most, self.total = sp.sb("most", [P, NT]), sp.sb("total", [P, NT])
        self.low_done, self.ex_done = sp.sem("gate_low"), sp.sem("gate_ex")

    def dve(self, nc, dve, link):
        E = self.E
        wide = lambda x: x.rearrange("p (t o) -> p t o", o=1).to_broadcast([P, NT, E])
        link(nc.vector.tensor_reduce(self.most, self.v, AX.X, ALU.max))
        nc.vector.tensor_tensor(self.ex, self.v, wide(self.most), ALU.subtract).then_inc(self.low_done, 1)
        dve.wait_ge(self.ex_done, 1)
        if self.all_first:
            link(nc.vector.tensor_reduce(self.total, self.ex, AX.X, ALU.add))
            link(nc.vector.reciprocal(self.total, self.total))
            link(nc.vector.tensor_tensor(self.ex, self.ex, wide(self.total), ALU.mult))
        top2(nc, link, self.ex if self.all_first else self.v, self.rank, self.cmp, E)
        link(nc.vector.scalar_tensor_tensor(self.share, self.rank, 1.5, self.ex, ALU.is_lt, ALU.mult))
        link(nc.vector.tensor_reduce(self.total, self.share, AX.X, ALU.add))
        link(nc.vector.tensor_scalar(self.total, self.total, 1e-12, None, ALU.max))
        link(nc.vector.reciprocal(self.total, self.total))
        link(nc.vector.tensor_tensor(self.share, self.share, wide(self.total), ALU.mult))

    def act(self, nc, act):
        act.wait_ge(self.low_done, 1)
        nc.scalar.activation(self.ex, self.ex, ACT.Exp).then_inc(self.ex_done, 1)


class Attention:

    def __init__(self, sp, sh, h16, table, edges, cw, share, d):
        self.sh, self.h16, self.table, self.edges, self.cw, self.d = sh, h16, table, edges, cw, d
        self.share = share
        self.g = Gather(sp, NC2, edges, RD, table, AW, tracked=False)
        self.iters = self.g.iters
        self.all = sh.agg.rearrange("p f n -> p (f n)")[:, 0:NC2 * AW].rearrange("p (c w) -> p c w", w=AW)
        self.att = sp.sb("att", [P, 5, HX])
        self.row = sp.sb("row", [P, NT, AW])
        self.prod = sp.sb("prod", [P, NT, HX])
        self.node = sp.sb("node", [P, NT, 2 * HEADS])
        self.top, self.low = sp.sb("top", [P, NT, HEADS]), sp.sb("low", [P, NT, HEADS])
        self.sums = sp.sb("sums", [P, NT, AW])
        self.hot = [sp.sb(f"hot{h}", [P, U, P]) for h in range(2)]
        bf = mybir.dt.bfloat16
        self.cold = [sp.sb(f"cold{h}", [P, U, P], bf) for h in range(2)]
        self.off = sp.sb("off", [P, HEADS, P], bf)
        self.diag = [sp.sb(f"diag{h}", [P, U, HEADS, P]) for h in range(2)]
        self.turned = [sp.sb(f"turned{h}", [P, U, P]) for h in range(2)]
        self.red = sp.sb("red", [P, 4, HEADS])
        self.z, self.z2 = sp.sb("z", [P, U, HEADS]), sp.sb("z2", [P, U, HEADS])
        self.pay = [sp.sb(f"pay{h}", [P, U, AW]) for h in range(2)]
        self.bank = [sp.ps(f"bank{j}", [P, 512]) for j in range(4)]
        self.pt, self.pn, self.pd = sp.ps("pt", [P, 2, 512]), sp.ps("pn", [P, 512]), sp.ps("pd", [P, 512])
        names = ("loaded", "link", "rows_ready", "stored", "kept", "diag_done", "hot_ready", "spread", "reduced",
                 "maxed", "hot2", "turn_done", "turn_kept", "nodes_done", "z_done", "ex_done", "pay_done", "paid",
                 "summed")
        (self.loaded, self.link, self.rows_ready, self.stored, self.kept, self.diag_done, self.cold_ready,
         self.spread, self.reduced, self.maxed, self.hot2, self.turn_done, self.turn_kept, self.nodes_done,
         self.z_done, self.ex_done, self.pay_done, self.paid, self.summed) = (sp.sem(n) for n in names)
        self.var_done, self.root_done = sp.sem("var_done"), sp.sem("root_done")
        self.gate = Shares(sp, sp.sb("scores", [P, NT, XD]), XD, False, share)

    def sp(self, nc, sp):
        for n, src in enumerate(self.d):
            sp.dma_start(self.att[:, n, :], src.partition_broadcast(P)).then_inc(self.loaded, 16)
        sp.wait_ge(self.rows_ready, 1)
        hold(sp)
        sp.dma_start(self.table.rearrange("(t p) w -> p t w", p=P), self.row).then_inc(self.stored, 16)

    def pool(self, nc, pool):
        pool.wait_ge(self.stored, 16)
        hold(pool)
        with pool.Fori(0, self.iters) as i:
            for h in range(2):
                self.g.pool_set(nc, pool, i, h)

    def act(self, nc, act):
        sh = self.sh
        for h in range(2):
            self.g.act_set(nc, act, 0, 0, h)
        with act.Fori(0, self.iters) as i:
            for h in range(2):
                act.wait_ge(self.g.here[h], (i + 1) * (16 * U))
                c = (i * 2 + h) * U
                hold(act)
                nc.scalar.copy(self.all[:, ds(c, U), :], self.g.rows[h]).then_inc(self.kept, 1)
                act.wait_ge(self.spread, i * (2 * U) + h * U)
                for u in range(U):
                    for a in range(HEADS):
                        ins = nc.scalar.activation(self.diag[h][:, u, a, :], sh.ident, ACT.Copy,
                                                   scale=self.g.rows[h][:, u, a:a + 1])
                ins.then_inc(self.diag_done, 1)
                nodes = self.edges[:, ds(c + 2 * U, U), 0].bitcast(I32)
                nc.scalar.copy(self.g.idx[h], nodes).then_inc(self.g.ready[h], 1)
        with act.Fori(0, self.iters) as i:
            for h in range(2):
                k = i * 2 + h
                act.wait_ge(self.turn_done, (k + 1) * 2)
                act.wait_ge(self.nodes_done, i * 2 + h)
                nc.scalar.copy(self.turned[h].rearrange("p u n -> p (u n)").rearrange("p (b n) -> p b n", b=2),
                               self.pt).then_inc(self.turn_kept, 1)
                act.wait_ge(self.z_done, (k + 1) * 3)
                nc.scalar.activation(self.pay[h][:, :, 0:HEADS], self.z, ACT.Exp).then_inc(self.ex_done, 1)
        act.wait_ge(self.var_done, 1)
        nc.scalar.activation(self.top[:, :, 0], self.top[:, :, 0], ACT.Sqrt).then_inc(self.root_done, 1)
        self.gate.act(nc, act)

    def pe(self, nc, pe):
        sh = self.sh
        nc.tensor.sem_inc(self.spread, U)
        with pe.Fori(0, self.iters) as i:
            for h in range(2):
                k = i * 2 + h
                pe.wait_ge(self.diag_done, i * 2 + (h + 1))
                pe.wait_ge(self.cold_ready, i * 2 + (h + 1))
                for u in range(U):
                    b = u % 4
                    pe.wait_ge(self.reduced, i * (2 * U) + (h * U + u))
                    nc.tensor.matmul(self.bank[b], sh.ones, self.diag[h][:, u].rearrange("p a n -> p (a n)"),
                                     start=True, stop=False)
                    nc.tensor.matmul(self.bank[b], self.cold[h][:, u, :], self.off.rearrange("p a n -> p (a n)"),
                                     start=False, stop=True).then_inc(self.spread, 1)
        with pe.Fori(0, self.iters) as i:
            for h in range(2):
                k = i * 2 + h
                pe.wait_ge(self.hot2, i * 2 + (h + 1))
                pe.wait_ge(self.turn_kept, i * 2 + h)
                for u in range(U):
                    ins = nc.tensor.transpose(self.pt[:, u // 4, (u % 4) * P:(u % 4 + 1) * P],
                                              self.hot[h][:, u, :], sh.ident)
                    if u % 4 == 3:
                        ins.then_inc(self.turn_done, 1)
                pe.wait_ge(self.turn_kept, i * 2 + (h + 1))
                pe.wait_ge(self.z_done, (i * 2 + h) * 3)
                for u in range(U):
                    c = (i * 2 + h) * U + u
                    w = pe.value_load(self.cw[0:1, ds(c, 1)], min_val=0, max_val=NT - 1)
                    ins = nc.tensor.matmul(self.pn[:, u * 2 * HEADS:(u + 1) * 2 * HEADS], self.turned[h][:, u, :],
                                           self.node[:, ds(w, 1), :].rearrange("p o c -> p (o c)"), start=True,
                                           stop=True)
                ins.then_inc(self.nodes_done, 1)
                pe.wait_ge(self.pay_done, i * 2 + (h + 1))
                pe.wait_ge(self.summed, i * (2 * U) + h * U)
                for u in range(U):
                    ins = nc.tensor.matmul(self.pd[:, u * 32:u * 32 + AW], self.hot[h][:, u, :],
                                           self.pay[h][:, u, :], start=True, stop=True)
                ins.then_inc(self.paid, 1)

    def dve(self, nc, dve):
        sh = self.sh
        link = Chain(dve, self.link)
        dve.wait_ge(self.loaded, 5 * 16)
        across = lambda n: self.att[:, n:n + 1, :].to_broadcast([P, NT, HX])
        by_head = lambda x: x.rearrange("p t (h x) -> p t h x", h=HEADS)
        for n, to in ((0, self.row[:, :, 0:HEADS]), (1, self.node[:, :, 0:HEADS])):
            link(nc.vector.tensor_tensor(self.prod, self.h16, across(n), ALU.mult))
            link(nc.vector.tensor_reduce(to, by_head(self.prod), AX.X, ALU.add))
        nc.vector.tensor_copy(self.row[:, :, HEADS:AW], self.h16).then_inc(self.rows_ready, 1)
        for a in range(HEADS):
            link(nc.vector.tensor_scalar(self.off[:, a, :], sh.ident, -BIG, None, ALU.mult))
        link(nc.vector.memset(self.top, -3e38))
        link(nc.vector.memset(self.sums, 0.0))
        nc.vector.sem_inc(self.reduced, 3)
        with dve.Fori(0, self.iters) as i:
            for h in range(2):
                dve.wait_ge(self.spread, i * (2 * U) + h * U)
                for u in range(U):
                    ins = nc.vector.tensor_scalar(self.cold[h][:, u, :], sh.iota,
                                                  self.edges[:, ds((i * 2 + h) * U + u, 1), 1], None, ALU.not_equal)
                ins.then_inc(self.cold_ready, 1)
                for u in range(U):
                    c = (i * 2 + h) * U + u
                    b = u % 4
                    w = dve.value_load(self.cw[0:1, ds(c, 1)], min_val=0, max_val=NT - 1)
                    dve.wait_ge(self.spread, i * (2 * U) + (h * U + u + 1 + U))
                    nc.vector.tensor_reduce(self.red[:, b, :], self.bank[b].rearrange("p (a n) -> p a n", a=HEADS),
                                            AX.X, ALU.max).then_inc(self.reduced, 1)
                    dve.wait_ge(self.reduced, i * (2 * U) + (h * U + u + 1 + 3))
                    dve.wait_ge(self.maxed, i * (2 * U) + (h * U + u))
                    to = self.top[:, ds(w, 1), :]
                    nc.vector.tensor_tensor(to, to, self.red[:, b:b + 1, :], ALU.max).then_inc(self.maxed, 1)
        dve.wait_ge(self.maxed, NC2)
        link(nc.vector.tensor_tensor(self.top, self.top, self.node[:, :, 0:HEADS], ALU.add))
        link(nc.vector.tensor_scalar(self.low, self.top, 0.2, None, ALU.mult))
        link(nc.vector.tensor_tensor(self.node[:, :, HEADS:2 * HEADS], self.top, self.low, ALU.max))
        dve.wait_ge(self.kept, self.iters * 2)
        hold(dve)
        with dve.Fori(0, self.iters) as i:
            for h in range(2):
                k = i * 2 + h
                rows = self.all[:, ds(k * U, U), :]
                pn = self.pn[:, 0:U * 2 * HEADS].rearrange("p (u c) -> p u c", u=U)
                dve.wait_ge(self.summed, i * (2 * U) + h * U)
                for u in range(U):
                    ins = nc.vector.tensor_scalar(self.hot[h][:, u, :], sh.iota, self.edges[:, ds(k * U + u, 1), 1],
                                                  None, ALU.is_equal)
                ins.then_inc(self.hot2, 1)
                dve.wait_ge(self.nodes_done, i * 2 + (h + 1))
                dve.wait_ge(self.ex_done, i * 2 + h)
                nc.vector.tensor_tensor(self.z, rows[:, :, 0:HEADS], pn[:, :, 0:HEADS], ALU.add).then_inc(self.z_done, 1)
                dve.wait_ge(self.z_done, k * 3 + 1)
                nc.vector.scalar_tensor_tensor(self.z2, self.z, 0.2, self.z, ALU.mult, ALU.max).then_inc(self.z_done, 1)
                dve.wait_ge(self.z_done, k * 3 + 2)
                nc.vector.tensor_tensor(self.z, self.z2, pn[:, :, HEADS:2 * HEADS], ALU.subtract).then_inc(self.z_done, 1)
                dve.wait_ge(self.ex_done, i * 2 + (h + 1))
                pay = self.pay[h][:, :, HEADS:AW].rearrange("p u (a x) -> p u a x", a=HEADS)
                ex = self.pay[h][:, :, 0:HEADS].rearrange("p u (a o) -> p u a o", o=1).to_broadcast([P, U, HEADS, XD])
                nc.vector.tensor_tensor(pay, rows[:, :, HEADS:AW].rearrange("p u (a x) -> p u a x", a=HEADS), ex,
                                        ALU.mult).then_inc(self.pay_done, 1)
                for u in range(U):
                    w = dve.value_load(self.cw[0:1, ds(k * U + u, 1)], min_val=0, max_val=NT - 1)
                    if u == 0:
                        dve.wait_ge(self.paid, i * 2 + (h + 1))
                    dve.wait_ge(self.summed, i * (2 * U) + (h * U + u))
                    to = self.sums[:, ds(w, 1), :].rearrange("p o c -> p (o c)")
                    nc.vector.tensor_tensor(to, to, self.pd[:, u * 32:u * 32 + AW], ALU.add).then_inc(self.summed, 1)
        dve.wait_ge(self.summed, NC2)
        den, out = self.sums[:, :, 0:HEADS], self.sums[:, :, HEADS:AW]
        link(nc.vector.tensor_scalar(den, den, 1e-16, None, ALU.add))
        link(nc.vector.reciprocal(self.low, den))
        wide = self.low.rearrange("p t (a o) -> p t a o", o=1).to_broadcast([P, NT, HEADS, XD])
        link(nc.vector.tensor_tensor(by_head(self.prod), by_head(out), wide, ALU.mult))
        link(nc.vector.tensor_tensor(self.prod, self.prod, across(2), ALU.add))
        mean = self.top[:, :, 0]
        over = self.top[:, :, 0:1].to_broadcast([P, NT, HX])
        link(nc.vector.tensor_reduce(mean, self.prod, AX.X, ALU.add))
        link(nc.vector.tensor_scalar(mean, mean, 1.0 / HX, None, ALU.mult))
        link(nc.vector.tensor_tensor(self.prod, self.prod, over, ALU.subtract))
        link(nc.vector.tensor_tensor(out, self.prod, self.prod, ALU.mult))
        link(nc.vector.tensor_reduce(mean, out, AX.X, ALU.add))
        nc.vector.tensor_scalar(mean, mean, 1.0 / HX, LN_EPS, ALU.mult, ALU.add).then_inc(self.var_done, 1)
        dve.wait_ge(self.root_done, 1)
        link(nc.vector.reciprocal(mean, mean))
        link(nc.vector.tensor_tensor(self.prod, self.prod, over, ALU.mult))
        link(nc.vector.tensor_tensor(self.prod, self.prod, across(3), ALU.mult))
        link(nc.vector.tensor_tensor(self.prod, self.prod, across(4), ALU.add))
        link(nc.vector.tensor_reduce(self.gate.v, self.prod.rearrange("p t (h x) -> p t x h", h=HEADS), AX.X, ALU.add))
        link(nc.vector.tensor_scalar(self.gate.v, self.gate.v, 1.0 / HEADS, None, ALU.mult))
        self.gate.dve(nc, dve, link)


class AddTurned:

    def __init__(self, sp, sh, table):
        self.sh, self.table = sh, table
        self.x = [sp.sb(f"x{j}", [P, D]) for j in range(2)]
        self.turn = [sp.ps(f"turn{j}", [P, 512]) for j in range(2)]
        self.here = [sp.sem(f"here{j}") for j in range(2)]
        self.turned = [sp.sem(f"turned{j}") for j in range(2)]
        self.added = [sp.sem(f"added{j}") for j in range(2)]

    def tiles(self, eng, body):
        with eng.Fori(0, NT // 2) as i:
            for j in range(2):
                body(i * 2 + j, j, i)
        body(NT - 1, 0, NT // 2)

    def sp(self, nc, sp):
        def load(t, j, n):
            sp.wait_ge(self.turned[j], n)
            hold(sp)
            sp.dma_start(self.x[j], self.table[ds(t * P, P), :]).then_inc(self.here[j], 16)
        self.tiles(sp, load)

    def pe(self, nc, pe):
        def turn(t, j, n):
            pe.wait_ge(self.here[j], n * 16 + 16)
            pe.wait_ge(self.added[j], n)
            for f in range(FB):
                ins = nc.tensor.transpose(self.turn[j][:, f * P:(f + 1) * P], self.x[j][:, f * P:(f + 1) * P],
                                          self.sh.ident)
            ins.then_inc(self.turned[j], 1)
        self.tiles(pe, turn)

    def dve(self, nc, dve):
        def add(t, j, n):
            dve.wait_ge(self.turned[j], n + 1)
            to = self.sh.agg[:, :, ds(t * P, P)]
            nc.vector.tensor_tensor(to, to, self.turn[j][:, 0:D].rearrange("p (f n) -> p f n", f=FB),
                                    ALU.add).then_inc(self.added[j], 1)
        self.tiles(dve, add)


def program(nc, x, src, dst, edge_attr_4, edge_weight, L0_gnn_W1, L0_gnn_b1, L0_gnn_W2, L0_gnn_b2, L0_ffn_router_w,
            L0_ffn_w1, L0_ffn_b1, L0_ffn_w2, L0_ffn_b2, L1_gnn_mlp_w, L1_gnn_mlp_b, L1_gnn_ew1, L1_gnn_ew2,
            L1_gnn_bn_g, L1_gnn_bn_b, L1_ffn_W_gat, L1_ffn_att_src, L1_ffn_att_dst, L1_ffn_b_gat, L1_ffn_ln_gamma,
            L1_ffn_ln_beta, L1_ffn_W1, L1_ffn_b1, L1_ffn_W2, L1_ffn_b2, L1_ffn_edge_index, out, last_phase=99):
    table = lambda name, shape: nc.dram_tensor(name, shape, F32, kind="Internal").ap()
    x0, xn0, x1, both1, x2, x3 = (table(n, [NP, D]) for n in ("x0", "xn0", "x1", "both1", "x2", "x3"))
    listA, listC, listD = (table(n, [P * c, r]) for n, c, r in
                           (("listA", NC1, RA), ("listC", NC1, RC), ("listD", NC2, RD)))
    nodesC, nodesD = table("nodesC", [NP, TW]), table("nodesD", [NP, AW])
    lanes = lambda lst: lst.rearrange("(p c) w -> p (c w)", p=P)

    with ExitStack() as whole:
        sb = lambda name, shape, dt=F32: whole.enter_context(nc.sbuf_tensor(name, shape, dt))[:]
        sh = Shared()
        sh.h, sh.agg = sb("h", [P, FB, NP]), sb("agg", [P, FB, NP])
        sh.ident, sh.iota, sh.ones, sh.below = (sb(n, [P, P]) for n in ("ident", "iota", "ones", "below"))
        sh.wincol = sb("wincol", [P, NT])
        sh.scale, sh.shift, sh.dinv_col = sb("scale", [P, FB]), sb("shift", [P, FB]), sb("dinv_col", [P, NT])
        cwC, cwD = sb("cwC", [1, NC1], I32), sb("cwD", [1, NC2], I32)

        def cut(whole_tile):
            flat, at = whole_tile.rearrange("p f n -> p (f n)"), [0]

            def take(parts, *shape):
                n = 1
                for d in shape:
                    n *= d
                piece = flat[0:parts, at[0]:at[0] + n]
                at[0] += n
                return piece if len(shape) == 1 else piece.rearrange("p (t w) -> p t w", w=shape[1])
            return take
        take = cut(sh.h)
        recA, recC, recD = take(E1P, E1T, RA), take(E1P, E1T, RC), take(P, E2T, RD)
        cwA = take(1, NC1).bitcast(I32)
        rowA, rowC, rowD = (take(p, t).bitcast(I32) for p, t in ((E1P, E1T), (E1P, E1T), (P, E2T)))
        take = cut(sh.agg)
        src_sb, dst_sb = take(E1P, E1T).bitcast(I32), take(E1P, E1T).bitcast(I32)
        sh.chunkrow = take(P, NC1)
        wt_sb, attr_sb = take(E1P, E1T), take(E1P, E1T, 4)
        from_sb, to_sb = take(P, E2T).bitcast(I32), take(P, E2T).bitcast(I32)

        def phase(name, build):
            sems = []
            with ExitStack() as mem:
                build(lambda part: Space(nc, mem, sems, f"{name}_{part}"))
            numbers = sorted(s.num for s in sems)
            while numbers:
                n = next((i for i in range(1, len(numbers)) if numbers[i] != numbers[0] + i), len(numbers))
                nc.sync.sem_clear(range(numbers[0], numbers[n - 1] + 1))
                numbers = numbers[n:]
            nc.all_engine_barrier()
            for s in sems:
                nc.release_semaphore(s)

        def setup(space):
            sp_ = space("in")
            sort = Sort(space("sort"), sh, E1P, E1T, NC1, src_sb, recA, rowA, cwA)
            pads = [sp_.sb(f"pad{n}", [P, c, r]) for n, c, r in ((0, NC1, RA), (1, NC1, RC), (2, NC2, RD))]
            zero = sp_.sb("zero", [NP - N, D])
            loaded, const, padded, stored, recs, ready = (sp_.sem(n) for n in
                                                          ("loaded", "const", "padded", "stored", "recs", "ready"))
            cut1 = lambda a: a.rearrange("(p t) -> p t", p=E1P)
            with nc.Block() as block:
                @block.sync
                def _(sp):
                    sp.dma_start(src_sb, cut1(src)).then_inc(loaded, 16)
                    sp.dma_start(dst_sb, cut1(dst)).then_inc(loaded, 16)
                    sp.dma_start(wt_sb, cut1(edge_weight)).then_inc(loaded, 16)
                    sp.dma_start(attr_sb, edge_attr_4.rearrange("(p t) w -> p t w", p=E1P)).then_inc(loaded, 16)
                    for n, to in ((0, from_sb), (1, to_sb)):
                        sp.dma_start(to[:, 0:E2T - NT], L1_ffn_edge_index[n].rearrange("(p t) -> p t",
                                                                                      p=P)).then_inc(loaded, 16)
                    sp.dma_start(x0[0:N, :], x).then_inc(stored, 16)
                    sp.wait_ge(padded, 4)
                    hold(sp)
                    sp.dma_start(x0[N:NP, :], zero).then_inc(stored, 16)
                    for pad, lst in zip(pads, (listA, listC, listD)):
                        sp.dma_start(lanes(lst), pad.rearrange("p c w -> p (c w)")).then_inc(stored, 16)
                    sp.wait_ge(stored, 5 * 16)
                    sp.wait_ge(recs, 1)

                @block.gpsimd
                def _(pool):
                    nc.gpsimd.iota(sh.iota, [[1, P]], base=0, channel_multiplier=0,
                                   allow_small_or_imprecise_dtypes=True)
                    nc.gpsimd.iota(sh.wincol, [[1, NT]], base=0, channel_multiplier=0,
                                   allow_small_or_imprecise_dtypes=True)
                    nc.gpsimd.iota(sh.chunkrow, [[P, NC1]], base=0, channel_multiplier=0,
                                   allow_small_or_imprecise_dtypes=True)
                    nc.gpsimd.memset(sh.ones, 1.0)
                    nc.gpsimd.memset(sh.below, 1.0)
                    nc.gpsimd.memset(sh.ident, 0.0).then_inc(const, 1)
                    for to in (from_sb, to_sb):
                        nc.gpsimd.iota(to[:, E2T - NT:E2T], [[P, NT]], base=0, channel_multiplier=1)
                    pool.wait_ge(const, 1)
                    nc.gpsimd.affine_select(out=sh.below, in_=sh.below, compare_op=ALU.is_gt, fill=0.0, base=0,
                                            pattern=[[1, P]], channel_multiplier=-1)
                    nc.gpsimd.affine_select(out=sh.ident, in_=sh.ident, compare_op=ALU.not_equal, fill=1.0, base=0,
                                            pattern=[[-1, P]], channel_multiplier=1).then_inc(ready, 1)
                    nc.gpsimd.memset(zero, 0.0).then_inc(padded, 1)
                    for n, pad in enumerate(pads):
                        nc.gpsimd.memset(pad, 0.0).then_inc(const, 1)
                        pool.wait_ge(const, n * 2 + 2)
                        nc.gpsimd.memset(pad[:, :, 1], -1.0).then_inc(const, 1)
                        nc.gpsimd.memset(pad.bitcast(I32)[:, :, 0], N).then_inc(padded, 1)

                @block.scalar
                def _(act):
                    act.wait_ge(loaded, 6 * 16)
                    act.wait_ge(ready, 1)
                    nc.scalar.copy(recA.bitcast(I32)[:, :, 0], dst_sb)
                    nc.scalar.copy(recA[:, :, 2], wt_sb)
                    nc.scalar.copy(recC.bitcast(I32)[:, :, 0], src_sb)
                    nc.scalar.copy(recC[:, :, 2:6], attr_sb)
                    nc.scalar.copy(recD.bitcast(I32)[:, :, 0], from_sb).then_inc(recs, 1)

                @block.vector
                def _(dve):
                    dve.wait_ge(loaded, 6 * 16)
                    dve.wait_ge(ready, 1)
                    sort.dve(nc, dve)

                @block.tensor
                def _(pe):
                    pe.wait_ge(ready, 1)
                    sort.pe(nc, pe)

        def place_first(space):
            norm = Norm(space("norm"), sh, x0, normed=xn0)
            scat = Scatter(space("scat"), E1P, E1T, NC1, rowA, recA, listA, RA)
            with ExitStack() as psum:
                sortC = Sort(space("sortC"), sh, E1P, E1T, NC1, dst_sb, recC, rowC, cwC)
                sortD = Sort(space("sortD"), sh, P, E2T, NC2, to_sb, recD, rowD, cwD)
                with nc.Block() as block:
                    @block.sync
                    def _(sp):
                        norm.sp(nc, sp)

                    @block.scalar
                    def _(act):
                        norm.act(nc, act)

                    @block.gpsimd
                    def _(pool):
                        scat.pool(nc, pool)

                    @block.vector
                    def _(dve):
                        norm.dve(nc, dve)
                        sortC.dve(nc, dve)
                        sortD.dve(nc, dve)

                    @block.tensor
                    def _(pe):
                        sortC.pe(nc, pe)
                        sortD.pe(nc, pe)

        def first_sums(space):
            sp_ = space("sums")
            edges = sp_.sb("edges", [P, NC1, RA])
            g = Gather(space("gather"), NC1, edges, RA, xn0, D)
            a = Aggregate(space("agg"), sh, g, edges, cwA, sh.agg, True)
            here, zeroed = sp_.sem("here"), sp_.sem("zeroed")
            with nc.Block() as block:
                @block.sync
                def _(sp):
                    sp.dma_start(edges.rearrange("p c w -> p (c w)"), lanes(listA)).then_inc(here, 16)

                @block.scalar
                def _(act):
                    act.wait_ge(here, 16)
                    hold(act)
                    with act.Fori(0, g.iters) as i:
                        for h in range(2):
                            g.act_set(nc, act, i, i, h)

                @block.gpsimd
                def _(pool):
                    with pool.Fori(0, g.iters) as i:
                        for h in range(2):
                            g.pool_set(nc, pool, i, h)

                @block.vector
                def _(dve):
                    nc.vector.memset(sh.agg, 0.0).then_inc(zeroed, 1)
                    dve.wait_ge(zeroed, 1)
                    dve.wait_ge(here, 16)
                    hold(dve)
                    with dve.Fori(0, g.iters) as i:
                        for h in range(2):
                            a.dve_set(nc, dve, i, i, h, False)

                @block.tensor
                def _(pe):
                    nc.tensor.sem_inc(g.used, U)
                    with pe.Fori(0, g.iters) as i:
                        for h in range(2):
                            a.pe_set(nc, pe, i, h, False)

        def first_add(space):
            add = AddTurned(space("add"), sh, xn0)
            with nc.Block() as block:
                @block.sync
                def _(sp):
                    add.sp(nc, sp)

                @block.tensor
                def _(pe):
                    add.pe(nc, pe)

                @block.vector
                def _(dve):
                    add.dve(nc, dve)

        def dense(space, ffn, scat=None, ones=None):
            with nc.Block() as block:
                @block.sync
                def _(sp):
                    ffn.sp_load(nc, sp)
                    ffn.sp(nc, sp)

                @block.scalar
                def _(act):
                    ffn.act(nc, act)

                @block.tensor
                def _(pe):
                    ffn.pe(nc, pe)

                @block.vector
                def _(dve):
                    if ones is not None:
                        tile, done = ones
                        nc.vector.memset(tile, 1.0).then_inc(done, 1)
                        dve.wait_ge(done, 1)
                    ffn.dve(nc, dve)

                if scat is not None:
                    @block.gpsimd
                    def _(pool):
                        scat.pool(nc, pool)

        def first_ffn(space):
            sp_ = space("one")
            share = sp_.sb("share", [P, NT, 1])
            one = lambda a: a.rearrange("(o k) m -> o k m", o=1)
            row = lambda a: a.rearrange("(o m) -> o m", o=1)
            ffn = Ffn(space("ffn"), sh, sh.agg, 1, 4, one(L0_gnn_W1), row(L0_gnn_b1), one(L0_gnn_W2), row(L0_gnn_b2),
                      ACT.Relu, share, x0, x1)
            dense(space, ffn, Scatter(space("scat"), P, E2T, NC2, rowD, recD, listD, RD), (share, sp_.sem("done")))

        def first_mixture(space):
            sp_ = space("mix")
            share = sp_.sb("share", [P, NT, XB])
            with ExitStack() as part:
                space2 = lambda n: Space(nc, part, sp_.sems, "mix_" + n)
                q = space2("router")
                head, logits = q.sb("head", [P, FB, XB]), q.sb("logits", [P, NT, XB])
                norm = Norm(space2("norm"), sh, x1, both=both1, tok=sh.agg, head=head, head_out=logits)
                gate = Shares(space2("gate"), logits, XB, True, share)
                head_here, link, done = q.sem("head_here"), q.sem("link"), q.sem("done")
                with nc.Block() as block:
                    @block.sync
                    def _(sp):
                        for f in range(FB):
                            sp.dma_start(head[:, f, :], L0_ffn_router_w[:, f * P:(f + 1) * P].rearrange(
                                "e p -> p e"), allow_slow_non_contiguous=True).then_inc(head_here, 16)
                        norm.sp(nc, sp)

                    @block.scalar
                    def _(act):
                        norm.act(nc, act)
                        gate.act(nc, act)

                    @block.tensor
                    def _(pe):
                        pe.wait_ge(head_here, 16 * FB)
                        norm.pe(nc, pe)

                    @block.vector
                    def _(dve):
                        norm.dve(nc, dve)
                        dve.wait_ge(norm.head_used, NG)
                        gate.dve(nc, dve, Chain(dve, link))
            ffn = Ffn(space("ffn"), sh, sh.agg, XB, 2, L0_ffn_w1, L0_ffn_b1, L0_ffn_w2, L0_ffn_b2, ACT.Gelu, share,
                      both1, x2)
            dense(space, ffn, Scatter(space("scat"), E1P, E1T, NC1, rowC, recC, listC, RC))

        def messages(space):
            sp_ = space("msg")
            edges = sp_.sb("edges", [P, NC1, RC])
            sh.dinv_row = sp_.sb("dinv_row", [P, NP])
            here = sp_.sem("here")
            with ExitStack() as part:
                space2 = lambda n: Space(nc, part, sp_.sems, "msg_" + n)
                norm = Norm(space2("norm"), sh, x2, tok=sh.h)
                deg = Degree(space2("deg"), sh, edges, cwC)
                with nc.Block() as block:
                    @block.sync
                    def _(sp):
                        sp.dma_start(edges.rearrange("p c w -> p (c w)"), lanes(listC)).then_inc(here, 16)
                        norm.sp(nc, sp)

                    @block.scalar
                    def _(act):
                        norm.act(nc, act)
                        deg.act(nc, act)

                    @block.tensor
                    def _(pe):
                        norm.pe(nc, pe)
                        deg.pe(nc, pe)

                    @block.vector
                    def _(dve):
                        norm.dve(nc, dve)
                        dve.wait_ge(here, 16)
                        deg.dve(nc, dve)
            layers = Layers(space("layers"), sh, edges, cwC, nodesC, L1_gnn_mlp_w, L1_gnn_mlp_b, L1_gnn_ew1,
                            L1_gnn_ew2, L1_gnn_bn_g, L1_gnn_bn_b)
            with nc.Block() as block:
                @block.sync
                def _(sp):
                    layers.sp(nc, sp)

                @block.scalar
                def _(act):
                    layers.act(nc, act)

                @block.gpsimd
                def _(pool):
                    layers.pool(nc, pool)

                @block.tensor
                def _(pe):
                    layers.pe(nc, pe)

                @block.vector
                def _(dve):
                    layers.dve(nc, dve)

        def last_mixture(space):
            sp_ = space("gat")
            share = sp_.sb("share", [P, NT, XD])
            with ExitStack() as part:
                space2 = lambda n: Space(nc, part, sp_.sems, "gat_" + n)
                q = space2("in")
                h16, edges = q.sb("h16", [P, NT, HX]), q.sb("edges", [P, NC2 + 2 * U, RD])
                here = q.sem("here")
                with ExitStack() as part1:
                    space3 = lambda n: Space(nc, part1, sp_.sems, "gat_" + n)
                    head = space3("head").sb("w", [P, FB, HX])
                    norm = Norm(space3("norm"), sh, x2, tok=sh.h, head=head, head_out=h16, add=sh.h, summed=x3)
                    with nc.Block() as block:
                        @block.sync
                        def _(sp):
                            sp.dma_start(head, L1_ffn_W_gat.rearrange("(f p) m -> p f m", p=P)).then_inc(here, 16)
                            sp.dma_start(edges[:, 0:NC2, :].rearrange("p c w -> p (c w)"),
                                         lanes(listD)).then_inc(here, 16)
                            norm.sp(nc, sp)
                            sp.wait_ge(here, 32)

                        @block.gpsimd
                        def _(pool):
                            nc.gpsimd.memset(edges[:, NC2:NC2 + 2 * U, :].bitcast(I32), N)

                        @block.scalar
                        def _(act):
                            norm.act(nc, act)

                        @block.tensor
                        def _(pe):
                            pe.wait_ge(here, 32)
                            norm.pe(nc, pe)

                        @block.vector
                        def _(dve):
                            norm.dve(nc, dve)
                att = Attention(space2("att"), sh, h16, nodesD, edges, cwD, share,
                                [L1_ffn_att_src.rearrange("h x -> (h x)"), L1_ffn_att_dst.rearrange("h x -> (h x)"),
                                 L1_ffn_b_gat, L1_ffn_ln_gamma, L1_ffn_ln_beta])
                with nc.Block() as block:
                    @block.sync
                    def _(sp):
                        att.sp(nc, sp)

                    @block.gpsimd
                    def _(pool):
                        att.pool(nc, pool)

                    @block.scalar
                    def _(act):
                        att.act(nc, act)

                    @block.tensor
                    def _(pe):
                        att.pe(nc, pe)

                    @block.vector
                    def _(dve):
                        att.dve(nc, dve)
            ffn = Ffn(space("ffn"), sh, sh.h, XD, 4, L1_ffn_W1, L1_ffn_b1, L1_ffn_W2, L1_ffn_b2, ACT.Gelu, share, x3,
                      out)
            dense(space, ffn)

        phases = [("p1", setup), ("p2", place_first), ("p3", first_sums), ("p4", first_add), ("p5", first_ffn),
                  ("p6", first_mixture), ("p7", messages), ("p8", last_mixture)]
        for name, build in phases[:last_phase]:
            phase(name, build)


_INS = ['x', 'src', 'dst', 'edge_attr_4', 'edge_weight', 'L0_gnn_W1', 'L0_gnn_b1', 'L0_gnn_W2', 'L0_gnn_b2',
        'L0_ffn_router_w', 'L0_ffn_w1', 'L0_ffn_b1', 'L0_ffn_w2', 'L0_ffn_b2', 'L1_gnn_mlp_w', 'L1_gnn_mlp_b',
        'L1_gnn_ew1', 'L1_gnn_ew2', 'L1_gnn_bn_g', 'L1_gnn_bn_b', 'L1_ffn_W_gat', 'L1_ffn_att_src', 'L1_ffn_att_dst',
        'L1_ffn_b_gat', 'L1_ffn_ln_gamma', 'L1_ffn_ln_beta', 'L1_ffn_W1', 'L1_ffn_b1', 'L1_ffn_W2', 'L1_ffn_b2',
        'L1_ffn_edge_index']


def kernel(**inputs):
    import numpy as _np
    import concourse.bacc as _bacc
    from concourse import mybir as _mybir
    from concourse.bass_utils import run_bass_kernel_spmd as _run

    nc = _bacc.Bacc("TRN2", target_bir_lowering=False, num_devices=1)
    arrays, args = {}, []
    for name in _INS:
        a = _np.ascontiguousarray(inputs[name])
        arrays[f"in_{name}_dram"] = a
        args.append(nc.dram_tensor(f"in_{name}_dram", a.shape, _mybir.dt.from_np(a.dtype), kind="ExternalInput").ap())
    out = nc.dram_tensor("out_0_dram", (N, D), F32, kind="ExternalOutput").ap()
    program(nc, *args, out)
    r = _run(nc, [arrays], core_ids=[0])
    return r.results[0]["out_0_dram"]
```

```python
from contextlib import ExitStack

import concourse.bass as bass
from concourse import mybir

F32 = mybir.dt.float32
I32 = mybir.dt.int32
ALU = mybir.AluOpType
ACT = mybir.ActivationFunctionType
AX = mybir.AxisListType
ds = bass.ds

P = 128
N, D = 6250, 256
NT = -(-N // P)
NP = NT * P
FB = D // P
E1 = 100000
E1P, E1T = 125, 800
E2 = 65536
E2T = E2 // P + NT
GT = 7
NG = NT // GT
GW = GT * P
HW = GW // 2
U = 4
S = 4
SU = S * U
AHEAD = SU - U
V = 8
LAYERS = 5
HEADS, XD = 4, 4
HX = HEADS * XD
XB = 8
LN_EPS = 1e-5
BN_EPS = 1e-5
BIG = 1e30
START = 1
TW = D + 4
AW = HEADS + HX


def chunks_of(edges):
    most = (edges + NT * (P - 1)) // P
    return -(-most // SU) * SU


NC1 = chunks_of(E1)
NC2 = chunks_of(E2 + NP)
PARTS_C = (4, 16, 10)
RA, RC, RD = 3, 6, 2


class Chain:

    def __init__(self, eng, sem, base=0):
        self.eng, self.sem, self.n = eng, sem, base

    def __call__(self, ins, wait=True):
        self.n = self.n + 1
        ins.then_inc(self.sem, 1)
        if wait:
            self.eng.wait_ge(self.sem, START + self.n)


def hold(eng):
    eng.nop(nofuse=True)


class Shared:
    pass


class Space:

    def __init__(self, nc, ctx, sems, name):
        self.nc, self.ctx, self.sems, self.name = nc, ctx, sems, name

    def sb(self, name, shape, dt=F32):
        return self.ctx.enter_context(self.nc.sbuf_tensor(f"{self.name}_{name}", shape, dt))[:]

    def ps(self, name, shape):
        return self.ctx.enter_context(self.nc.psum_tensor(f"{self.name}_{name}", shape, F32))[:]

    def sem(self, name, dma=False, pool_dma=False):
        handle = self.nc.alloc_semaphore(f"{self.name}_{name}")
        if not pool_dma:
            self.sems.append(handle)
        if not (dma or pool_dma):
            self.nc.sync.sem_inc(handle, START)
        return handle




class Sort:

    def __init__(self, sp, sh, parts, T, nchunks, key, rec, row, cw):
        self.sh, self.parts, self.T, self.nchunks = sh, parts, T, nchunks
        self.key, self.rec, self.row, self.cw = key, rec, row, cw
        self.tmp_i, self.tmp_j = sp.sb("tmp_i", [parts, T], I32), sp.sb("tmp_j", [parts, T], I32)
        self.win, self.mask = sp.sb("win", [parts, T]), sp.sb("mask", [parts, T])
        self.rank, self.pos = sp.sb("rank", [parts, T]), sp.sb("pos", [parts, T])
        self.count = sp.sb("count", [parts, 1])
        self.start, self.endcol = sp.sb("start", [P, 1]), sp.sb("endcol", [NT, 1])
        self.ends = sp.sb("ends", [P, NT + 1])
        self.len_i, self.len_j = sp.sb("len_i", [P, 1], I32), sp.sb("len_j", [P, 1], I32)
        self.len_f = sp.sb("len_f", [P, 1])
        self.after = sp.sb("after", [NT, nchunks])
        self.sums = sp.ps("sums", [P, 512])
        self.endps = self.sums[0:NT, 64:65]
        self.cwps = sp.ps("cwps", [P, 1024])[0:1, :]
        self.link, self.summed, self.turned = sp.sem("link"), sp.sem("summed"), sp.sem("turned")
        self.after_done, self.winsum, self.rows_done = sp.sem("after_done"), sp.sem("winsum"), sp.sem("rows_done")

    BEFORE, PER = 6, 8

    def dve(self, nc, dve):
        sh, parts = self.sh, self.parts
        link = Chain(dve, self.link)
        link(nc.vector.tensor_scalar(self.tmp_i, self.key, 7, None, ALU.arith_shift_right))
        link(nc.vector.tensor_copy(self.win, self.tmp_i))
        link(nc.vector.tensor_scalar(self.tmp_j, self.key, P - 1, None, ALU.bitwise_and))
        link(nc.vector.tensor_copy(self.rec[:, :, 1], self.tmp_j))
        link(nc.vector.memset(self.pos, 0.0))
        link(nc.vector.memset(self.ends[:, 0:1], 0.0))
        before, per = self.BEFORE, self.PER
        assert link.n == before
        with dve.Fori(0, NT) as w:
            link = Chain(dve, self.link, w * per + before)
            link(nc.vector.tensor_scalar(self.mask, self.win, sh.wincol[0:parts, ds(w, 1)], 0.0, ALU.is_equal,
                                         ALU.add, accum_out=self.count))
            dve.wait_ge(self.summed, START + w + 1)
            link(nc.vector.tensor_tensor(self.start[0:parts, :], self.sums[0:parts, 0:1],
                                         self.ends[0:parts, ds(w, 1)], ALU.add))
            link(nc.vector.tensor_tensor_scan(self.rank, sh.ones[0:parts, 0:1].to_broadcast([parts, self.T]),
                                              self.mask, self.start[0:parts, 0:1], ALU.mult, ALU.add))
            link(nc.vector.tensor_scalar(self.len_i, self.sums[:, 1:2], float(P - 1), None, ALU.add))
            link(nc.vector.tensor_scalar(self.len_j, self.len_i, 7, 7, ALU.arith_shift_right,
                                         ALU.arith_shift_left))
            link(nc.vector.tensor_copy(self.len_f, self.len_j))
            nc.vector.tensor_tensor(self.ends[:, ds(w + 1, 1)], self.ends[:, ds(w, 1)], self.len_f,
                                    ALU.add).then_inc(self.link, 1)
            link.n = link.n + 1
            link(nc.vector.copy_predicated(self.pos, self.mask.bitcast(I32), self.rank))
        link = Chain(dve, self.link, NT * per + before)
        link(nc.vector.tensor_scalar(self.pos, self.pos, -1.0, None, ALU.add))
        link(nc.vector.tensor_copy(self.tmp_i, self.pos))
        link(nc.vector.tensor_scalar(self.tmp_j, self.tmp_i, P - 1, None, ALU.bitwise_and))
        link(nc.vector.tensor_copy(self.rank, self.tmp_j))
        link(nc.vector.tensor_scalar(self.tmp_j, self.tmp_i, 7, None, ALU.arith_shift_right))
        link(nc.vector.tensor_copy(self.pos, self.tmp_j))
        nc.vector.scalar_tensor_tensor(self.row, self.rank, float(self.nchunks), self.pos, ALU.mult,
                                       ALU.add).then_inc(self.rows_done, 1)
        dve.wait_ge(self.turned, START + 1)
        link(nc.vector.tensor_copy(self.endcol, self.endps))
        nc.vector.tensor_scalar(self.after, sh.chunkrow[0:NT, 0:self.nchunks], self.endcol[:, 0:1], None,
                                ALU.is_ge).then_inc(self.after_done, 1)
        for n, b in enumerate(range(0, self.nchunks, 512)):
            m = min(512, self.nchunks - b)
            dve.wait_ge(self.winsum, START + n + 1)
            nc.vector.tensor_scalar(self.cw[:, b:b + m], self.cwps[:, b:b + m], float(NT - 1), None,
                                    ALU.min).then_inc(self.rows_done, 1)

    def pe(self, nc, pe):
        sh, parts = self.sh, self.parts
        with pe.Fori(0, NT) as w:
            pe.wait_ge(self.link, START + w * self.PER + (self.BEFORE + 1))
            nc.tensor.matmul(self.sums[:, 0:1], sh.below[0:parts, :], self.count, start=True, stop=True)
            nc.tensor.matmul(self.sums[:, 1:2], sh.ones[0:parts, :], self.count, start=True,
                             stop=True).then_inc(self.summed, 1)
        pe.wait_ge(self.link, START + NT * self.PER + self.BEFORE)
        nc.tensor.matmul(self.endps, self.ends[0:1, 1:NT + 1], sh.ones[0:1, 0:1], start=True,
                         stop=True).then_inc(self.turned, 1)
        pe.wait_ge(self.after_done, START + 1)
        for b in range(0, self.nchunks, 512):
            m = min(512, self.nchunks - b)
            nc.tensor.matmul(self.cwps[:, b:b + m], sh.ones[0:NT, 0:1], self.after[:, b:b + m], start=True,
                             stop=True).then_inc(self.winsum, 1)


class Scatter:

    def __init__(self, sp, parts, T, nchunks, row, rec, table, words):
        self.parts, self.T, self.row, self.rec, self.table, self.words = parts, T, row, rec, table, words
        self.sets = T // (2 * V)
        self.rest = T - self.sets * 2 * V
        self.at = [sp.sb(f"at{h}", [P, V], I32) for h in range(2)]
        self.what = [sp.sb(f"what{h}", [P, V * words]) for h in range(2)]
        self.ready = sp.sem("ready")
        self.written = [sp.sem(f"written{h}", pool_dma=True) for h in range(2)]

    def pool(self, nc, pool, begin, count, first):
        if first:
            for h in range(2):
                self._send(nc, pool, h, h * V, V, h * 2 + 2)
        with pool.Fori(1 if first else 0, count) as i:
            for h in range(2):
                k = begin + i
                pool.wait_ge(self.written[h], k * (16 * V))
                self._send(nc, pool, h, (k * 2 + h) * V, V, k * 4 + (h * 2 + 2))

    def pool_rest(self, nc, pool):
        if self.rest:
            pool.wait_ge(self.written[0], self.sets * 16 * V)
            self._send(nc, pool, 0, self.sets * 2 * V, self.rest, self.sets * 4 + 2)
        pool.wait_ge(self.written[0], self.sets * 16 * V + 16 * self.rest)
        pool.wait_ge(self.written[1], self.sets * 16 * V)

    def _send(self, nc, pool, h, t, n, ready):
        p, w = self.parts, self.words
        flat = self.rec.rearrange("p t w -> p (t w)")
        nc.gpsimd.tensor_copy(self.at[h][0:p, 0:n], self.row[:, ds(t, n)]).then_inc(self.ready, 1)
        nc.gpsimd.tensor_copy(self.what[h][0:p, 0:n * w], flat[:, ds(t * w, n * w)]).then_inc(self.ready, 1)
        pool.wait_ge(self.ready, START + ready)
        hold(pool)
        for u in range(n):
            nc.gpsimd.indirect_dma_start(
                out=self.table, out_offset=bass.IndirectOffsetOnAxis(ap=self.at[h][0:p, u:u + 1], axis=0),
                in_=self.what[h][0:p, u * w:(u + 1) * w], in_offset=None).then_inc(self.written[h], 16)




def windows_of(nc, engine, cw, chunk, n):
    loads = [nc.values_load_multi_w_load_instructions(
        cw[0:1, ds(chunk + k, 4)], engines=[engine], min_val=0, max_val=NT - 1,
        skip_runtime_bounds_check_because="a count of windows, which Sort limits to NT - 1")[1]
        for k in range(0, n, 4)]
    return [w for four in loads for w in four]


class Gather:

    def __init__(self, sp, nchunks, edges, words, table, width, tracked=True, place=True):
        self.edges, self.words, self.table, self.width = edges, words, table, width
        self.turns = nchunks // SU
        self.idx = [sp.sb(f"idx{s}", [P, U], I32) for s in range(S)]
        self.rows = [sp.sb(f"rows{s}", [P, U, width]) for s in range(S)] if place else None
        self.ready = [sp.sem(f"ready{s}") for s in range(S)]
        self.here = [sp.sem(f"here{s}", pool_dma=True) for s in range(S)]
        self.used = sp.sem("used") if tracked else None

    def act_set(self, nc, act, it, i, s):
        act.wait_ge(self.used, START + it * SU + s * U)
        nodes = self.edges[:, ds(i * SU + s * U, U), 0].bitcast(I32)
        nc.scalar.copy(self.idx[s], nodes).then_inc(self.ready[s], 1)

    def pool_set(self, nc, pool, it, s):
        pool.wait_ge(self.ready[s], START + it + 1)
        hold(pool)
        for u in range(U):
            nc.gpsimd.indirect_dma_start(
                out=self.rows[s][:, u, :], out_offset=None, in_=self.table,
                in_offset=bass.IndirectOffsetOnAxis(ap=self.idx[s][:, u:u + 1], axis=0)).then_inc(self.here[s], 16)


class Aggregate:

    def __init__(self, sp, sh, g, edges, cw, agg, weighted, agge=None, place=True):
        self.sh, self.g, self.edges, self.cw, self.agg, self.weighted, self.agge = sh, g, edges, cw, agg, weighted, agge
        self.hot = [sp.sb(f"hot{s}", [P, U, P]) for s in range(S)] if place else None
        self.hot_ready = sp.sem("hot_ready")
        self.bank = [sp.ps(f"bank{u}", [P, 512]) for u in range(U)]
        self.added = [sp.sem(f"added{u}") for u in range(U)]
        if agge is not None:
            self.attr = [sp.sb(f"attr{s}", [P, U, 4]) for s in range(S)]

    def dve(self, nc, dve, it0, edge_terms):
        turns = self.g.turns

        def turn(i, last):
            for s in range(S):
                if s + 1 < S:
                    self._matrices(nc, dve, it0 + i, i, s + 1, edge_terms)
                elif not last:
                    self._matrices(nc, dve, it0 + i + 1, i + 1, 0, edge_terms)
                self._sums(nc, dve, it0 + i, i, s, edge_terms)

        self._matrices(nc, dve, it0, 0, 0, edge_terms)
        with dve.Fori(0, turns - 1) as i:
            turn(i, False)
        turn(turns - 1, True)

    def _matrices(self, nc, dve, it, i, s, edge_terms):
        dve.wait_ge(self.g.used, START + it * SU + s * U)
        hold(dve)
        for u in range(U):
            c = i * SU + s * U + u
            place = self.edges[:, ds(c, 1), 1]
            if self.weighted:
                ins = nc.vector.tensor_scalar(self.hot[s][:, u, :], self.sh.iota, place, self.edges[:, ds(c, 1), 2],
                                              ALU.is_equal, ALU.mult)
            else:
                ins = nc.vector.tensor_scalar(self.hot[s][:, u, :], self.sh.iota, place, None, ALU.is_equal)
        if edge_terms:
            dve.wait_ge(self.g.here[s], it * (16 * U) + 16 * U)
            ins = nc.vector.tensor_tensor(self.attr[s], self.edges[:, ds(i * SU + s * U, U), 2:6],
                                          self.g.rows[s][:, :, D:D + 1].to_broadcast([P, U, 4]), ALU.mult)
        ins.then_inc(self.hot_ready, 1)

    def _sums(self, nc, dve, it, i, s, edge_terms):
        for u, w in enumerate(windows_of(nc, mybir.EngineType.DVE, self.cw, i * SU + s * U, U)):
            dve.wait_ge(self.g.used, START + it * SU + (s * U + u + 1 + AHEAD))
            dve.wait_ge(self.added[(u - 1) % U], START + it * S + s + (u > 0))
            to = self.agg[:, :, ds(w * P, P)]
            prod = self.bank[u][:, 0:D].rearrange("p (f n) -> p f n", f=FB)
            if edge_terms:
                te = self.agge[:, ds(w * P, P)]
                nc.vector.tensor_tensor(te, te, self.bank[u][0:4, D:D + P], ALU.add)
            nc.vector.tensor_tensor(to, to, prod, ALU.add).then_inc(self.added[u], 1)

    def pe_set(self, nc, pe, it, s, edge_terms):
        pe.wait_ge(self.hot_ready, START + it * S + (s + 1))
        pe.wait_ge(self.g.here[s], it * (16 * U) + 16 * U)
        for u in range(U):
            pe.wait_ge(self.added[u], START + it * S + s)
            for f in range(FB):
                ins = nc.tensor.matmul(self.bank[u][:, f * P:(f + 1) * P], self.g.rows[s][:, u, f * P:(f + 1) * P],
                                       self.hot[s][:, u, :], start=True, stop=True)
            if edge_terms:
                ins = nc.tensor.matmul(self.bank[u][0:4, D:D + P], self.attr[s][:, u, :], self.hot[s][:, u, :],
                                       start=True, stop=True)
            ins.then_inc(self.g.used, 1)




def group_rows(table, g):
    return table[ds(g * GW, GW), :].rearrange("(t p) d -> p t d", p=P)


class Ffn:

    def __init__(self, sp, sh, tok, E, HB, w1, b1, w2, b2, func, share, base, out):
        self.sh, self.tok, self.E, self.HB, self.func, self.share = sh, tok, E, HB, func, share
        self.base, self.out = base, out
        self.d = (w1, b1, w2, b2)
        self.w1, self.b1 = sp.sb("w1", [P, E, FB, HB * P]), sp.sb("b1", [P, E * HB])
        self.w2, self.b2 = sp.sb("w2", [P, E * HB, D]), sp.sb("b2", [P, E, D])
        self.nh = min(2, E)
        self.hid = [sp.sb(f"hid{j}", [P, HB, GW]) for j in range(self.nh)]
        self.acc = sp.sb("acc", [P, GT, D])
        self.pre = [sp.ps(f"pre{j}", [P, 2, 512]) for j in range(2)]
        self.y = [sp.ps(f"y{j}", [P, 512]) for j in range(4)]
        self.loaded, self.pre_done = sp.sem("loaded", dma=True), sp.sem("pre_done")
        self.act_done = [sp.sem(f"act_done{j}") for j in range(2)]
        self.y_done = sp.sem("y_done")
        self.y_used = [sp.sem(f"y_used{j}") for j in range(4)]
        self.base_here, self.link, self.stored = sp.sem("base_here", dma=True), sp.sem("link"), sp.sem("stored")

    def sp_load(self, nc, sp):
        w1, b1, w2, b2 = self.d
        for e in range(self.E):
            sp.dma_start(self.w1[:, e], w1[e].rearrange("(f p) h -> p f h", p=P)).then_inc(self.loaded, 16)
            sp.dma_start(self.w2[:, e * self.HB:(e + 1) * self.HB],
                         w2[e].rearrange("(b p) d -> p b d", p=P)).then_inc(self.loaded, 16)
        sp.dma_start(self.b1, b1.rearrange("e (b p) -> p (e b)", p=P),
                     allow_slow_non_contiguous=True).then_inc(self.loaded, 16)
        sp.dma_start(self.b2, b2.partition_broadcast(P)).then_inc(self.loaded, 16)

    LOADS = property(lambda self: 16 * (2 * self.E + 2))

    def sp(self, nc, sp):
        def group(g):
            sp.wait_ge(self.stored, START + g * 16)
            hold(sp)
            sp.dma_start(self.acc, group_rows(self.base, g)).then_inc(self.base_here, 16)
            for j in range(4):
                sp.wait_ge(self.y_used[j], START + (g + 1) * (self.E * len(range(j, GT, 4))))
                hold(sp)

        with sp.Fori(0, NG - 1) as g:
            group(g)
            sp.dma_start(group_rows(self.out, g), self.acc).then_inc(self.stored, 16)
        group(NG - 1)
        rows = self.out.shape[0] - (NG - 1) * GW
        whole, rest = rows // P, rows % P
        at = (NG - 1) * GW
        sp.dma_start(self.out[at:at + whole * P, :].rearrange("(t p) d -> p t d", p=P),
                     self.acc[:, 0:whole, :]).then_inc(self.stored, 16)
        if rest:
            sp.dma_start(self.out[at + whole * P:at + rows, :], self.acc[0:rest, whole, :]).then_inc(self.stored, 16)
        sp.wait_ge(self.stored, START + NG * 16 + (16 if rest else 0))

    def pe(self, nc, pe):
        E, HB = self.E, self.HB
        pe.wait_ge(self.loaded, self.LOADS)

        def up(g, e):
            for b in range(HB):
                j = b % 2
                pe.wait_ge(self.act_done[j], START + (g * E + e) * (HB // 2) + b // 2)
                for m in range(2):
                    for f in range(FB):
                        ins = nc.tensor.matmul(self.pre[j][:, m, 0:HW], self.w1[:, e, f, b * P:(b + 1) * P],
                                               self.tok[:, f, ds(g * GW + m * HW, HW)], start=(f == 0),
                                               stop=(f == FB - 1))
                ins.then_inc(self.pre_done, 1)

        def down(g, e):
            for j in range(2):
                pe.wait_ge(self.act_done[j], START + (g * E + e + 1) * (HB // 2))
            for s in range(GT):
                j = s % 4
                n = len(range(j, GT, 4))
                pe.wait_ge(self.y_used[j], START + (g * E + e) * n + s // 4)
                for b in range(HB):
                    ins = nc.tensor.matmul(self.y[j][:, 0:D], self.hid[e % self.nh][:, b, s * P:(s + 1) * P],
                                           self.w2[:, e * HB + b, :], start=(b == 0), stop=(b == HB - 1))
                ins.then_inc(self.y_done, 1)

        nc.tensor.sem_inc(self.y_done, self.nh * GT)
        with pe.Fori(0, NG) as g:
            up(g, 0)
            for e in range(E):
                if e + 1 < E:
                    up(g, e + 1)
                down(g, e)

    def act(self, nc, act):
        E, HB, nh = self.E, self.HB, self.nh
        act.wait_ge(self.loaded, self.LOADS)
        hold(act)
        with act.Fori(0, NG) as g:
            for e in range(E):
                act.wait_ge(self.y_done, START + (g * E + e + 1) * GT)
                for b in range(HB):
                    act.wait_ge(self.pre_done, START + (g * E + e) * HB + b + 1)
                    nc.scalar.activation(self.hid[e % nh][:, b, :].rearrange("p (m n) -> p m n", m=2),
                                         self.pre[b % 2][:, :, 0:HW], self.func,
                                         bias=self.b1[:, e * HB + b:e * HB + b + 1]).then_inc(self.act_done[b % 2], 1)

    def dve(self, nc, dve):
        E = self.E
        dve.wait_ge(self.loaded, self.LOADS)
        hold(dve)
        with dve.Fori(0, NG) as g:
            dve.wait_ge(self.base_here, (g + 1) * 16)
            for e in range(E):
                for s in range(GT):
                    j = s % 4
                    n = len(range(j, GT, 4))
                    share = self.share[:, ds(g * GT + s, 1), e]
                    a = self.acc[:, s, :]
                    dve.wait_ge(self.y_used[j], START + (g * E + e) * n + s // 4)
                    nc.vector.scalar_tensor_tensor(a, self.b2[:, e, :], share, a, ALU.mult,
                                                   ALU.add).then_inc(self.link, 1)
                    dve.wait_ge(self.link, START + (g * E + e) * GT + s + 1)
                    dve.wait_ge(self.y_done, START + (g * E + e + self.nh) * GT + s + 1)
                    nc.vector.scalar_tensor_tensor(a, self.y[j][:, 0:D], share, a, ALU.mult,
                                                   ALU.add).then_inc(self.y_used[j], 1)


class Norm:

    def __init__(self, sp, sh, src, normed=None, both=None, tok=None, head=None, head_out=None, add=None,
                 summed=None):
        self.sh, self.src, self.normed, self.both, self.tok = sh, src, normed, both, tok
        self.head, self.head_out, self.add, self.summed = head, head_out, add, summed
        self.x, self.xn = sp.sb("x", [P, GT, D]), sp.sb("xn", [P, GT, D])
        self.sum = sp.sb("sum", [P, GT, D]) if both is not None else None
        self.stats, self.mv, self.rstd = sp.sb("stats", [P, GT, 6]), sp.sb("mv", [P, GT, 2]), sp.sb("rstd", [P, GT])
        if tok is not None:
            self.turn = [sp.ps(f"turn{j}", [P, 512]) for j in range(4)]
        self.here, self.link, self.stored = sp.sem("here", dma=True), sp.sem("link"), sp.sem("stored")
        self.var_done, self.root_done = sp.sem("var_done"), sp.sem("root_done")
        self.turned, self.xn_done, self.out_done = sp.sem("turned"), sp.sem("xn_done"), sp.sem("out_done")
        self.stores = (normed is not None) + (both is not None) + (summed is not None)
        if tok is not None:
            self.slot = sp.sb("slot", [P, GT, D])
            self.copied = [sp.sem(f"copied{j}") for j in range(2)]
            self.slotted = sp.sem("slotted")
        if head is not None:
            self.M = head_out.shape[2]
            self.prod = sp.ps("prod", [P, 512])
            self.head_done, self.head_used = sp.sem("head_done"), sp.sem("head_used")
        if add is not None:
            self.raw = sp.sb("raw", [P, FB, GW])
            self.applied = sp.sem("applied")
            self.added = [sp.sem(f"added{j}") for j in range(2)]
            self.add_turned = sp.sem("add_turned")

    def sp(self, nc, sp):
        with sp.Fori(0, NG) as g:
            sp.wait_ge(self.stored, START + g * (16 * self.stores))
            hold(sp)
            sp.wait_ge(self.out_done, START + g)
            hold(sp)
            sp.dma_start(self.x, group_rows(self.src, g)).then_inc(self.here, 16)
            if self.summed is not None:
                sp.wait_ge(self.added[0], START + (g + 1) * 4)
                hold(sp)
                sp.wait_ge(self.added[1], START + (g + 1) * 3)
                hold(sp)
                sp.dma_start(group_rows(self.summed, g), self.x).then_inc(self.stored, 16)
            sp.wait_ge(self.out_done, START + g + 1)
            hold(sp)
            if self.normed is not None:
                sp.dma_start(group_rows(self.normed, g), self.xn).then_inc(self.stored, 16)
            if self.both is not None:
                sp.dma_start(group_rows(self.both, g), self.sum).then_inc(self.stored, 16)
        sp.wait_ge(self.stored, START + NG * 16 * self.stores)

    PER = 3

    def dve(self, nc, dve):
        with dve.Fori(0, NG) as g:
            link = Chain(dve, self.link, g * self.PER)
            dve.wait_ge(self.here, (g + 1) * 16)
            if self.add is not None:
                for t in range(GT):
                    dve.wait_ge(self.add_turned, START + g * GT + t + 1)
                    nc.vector.tensor_tensor(self.x[:, t, :], self.x[:, t, :], self.turn[t % 2][:, 0:D],
                                            ALU.add).then_inc(self.added[t % 2], 1)
                dve.wait_ge(self.added[0], START + (g + 1) * 4)
                dve.wait_ge(self.added[1], START + (g + 1) * 3)
            for t in range(GT):
                ins = nc.vector.bn_stats(self.stats[:, t, :], self.x[:, t, :])
            link(ins)
            hold(dve)
            for t in range(GT):
                ins = nc.vector.bn_aggr(self.mv[:, t, :], self.stats[:, t, :])
            link(ins)
            nc.vector.tensor_scalar(self.rstd, self.mv[:, :, 1], LN_EPS, None, ALU.add).then_inc(self.var_done, 1)
            dve.wait_ge(self.root_done, START + g + 1)
            link(nc.vector.reciprocal(self.rstd, self.rstd))
            if self.tok is not None:
                dve.wait_ge(self.turned, START + g * GT)
            for t in range(GT):
                ins = nc.vector.tensor_scalar(self.xn[:, t, :], self.x[:, t, :], self.mv[:, t, 0:1],
                                              self.rstd[:, t:t + 1], ALU.subtract, ALU.mult)
                ins.then_inc(self.xn_done, 1)
            dve.wait_ge(self.xn_done, START + (g + 1) * GT)
            if self.both is not None:
                nc.vector.tensor_tensor(self.sum, self.x, self.xn, ALU.add).then_inc(self.out_done, 1)
            else:
                nc.vector.sem_inc(self.out_done, 1)
            if self.head is not None:
                dve.wait_ge(self.head_done, START + (g + 1) * GT)
                nc.vector.tensor_copy(self.head_out[:, ds(g * GT, GT), :],
                                      self.prod[:, 0:GT * 64].rearrange("p (t m) -> p t m", t=GT)[:, :, 0:self.M]
                                      ).then_inc(self.head_used, 1)

    def pe(self, nc, pe):
        if self.add is None and self.tok is None:
            return
        with pe.Fori(0, NG) as g:
            if self.add is not None:
                pe.wait_ge(self.applied, START + g + 1)
                for t in range(GT):
                    j = t % 2
                    pe.wait_ge(self.added[j], START + g * (4 - j) + t // 2)
                    for f in range(FB):
                        ins = nc.tensor.transpose(self.turn[j][:, f * P:(f + 1) * P],
                                                  self.raw[:, f, t * P:(t + 1) * P], self.sh.ident)
                    ins.then_inc(self.add_turned, 1)

            def head(t):
                pe.wait_ge(self.slotted, START + g * GT + t + 1)
                if t == 0:
                    pe.wait_ge(self.head_used, START + g)
                for f in range(FB):
                    ins = nc.tensor.matmul(self.prod[:, t * 64:t * 64 + self.M], self.slot[:, t, f * P:(f + 1) * P],
                                           self.head[:, f, :], start=(f == 0), stop=(f == FB - 1))
                ins.then_inc(self.head_done, 1)

            for t in range(GT):
                j = t % 2
                pe.wait_ge(self.xn_done, START + g * GT + t + 1)
                pe.wait_ge(self.copied[j], START + g * (4 - j) + t // 2)
                for f in range(FB):
                    ins = nc.tensor.transpose(self.turn[2 + j][:, f * P:(f + 1) * P],
                                              self.xn[:, t, f * P:(f + 1) * P], self.sh.ident)
                ins.then_inc(self.turned, 1)
                if self.head is not None and t:
                    head(t - 1)
            if self.head is not None:
                head(GT - 1)

    def act(self, nc, act):
        with act.Fori(0, NG) as g:
            if self.add is not None:
                act.wait_ge(self.add_turned, START + g * GT)
                for f in range(FB):
                    ins = nc.scalar.activation(self.raw[:, f, :], self.add[:, f, ds(g * GW, GW)], ACT.Identity,
                                               bias=self.sh.shift[:, f:f + 1], scale=self.sh.scale[:, f:f + 1])
                ins.then_inc(self.applied, 1)
            act.wait_ge(self.var_done, START + g + 1)
            nc.scalar.activation(self.rstd, self.rstd, ACT.Sqrt).then_inc(self.root_done, 1)
            for t in range(GT if self.tok is not None else 0):
                j = t % 2
                act.wait_ge(self.turned, START + g * GT + t + 1)
                if self.head is not None:
                    act.wait_ge(self.head_done, START + g * GT)
                    nc.scalar.copy(self.slot[:, t, :], self.turn[2 + j][:, 0:D]).then_inc(self.slotted, 1)
                nc.scalar.copy(self.tok[:, :, ds((g * GT + t) * P, P)],
                               self.turn[2 + j][:, 0:D].rearrange("p (f n) -> p f n", f=FB)).then_inc(self.copied[j], 1)


class Degree:

    COLS = 16

    def __init__(self, sp, sh, win, place, out):
        self.sh, self.win, self.place, self.out = sh, win, place, out
        self.pairs = E1T // (2 * self.COLS)
        bf = mybir.dt.bfloat16
        self.in_win = [sp.sb(f"in_win{j}", [E1P, self.COLS, NT], bf) for j in range(2)]
        self.in_place = [sp.sb(f"in_place{j}", [E1P, self.COLS, P], bf) for j in range(2)]
        self.low, self.dinv = sp.sb("low", [NT, P]), sp.sb("dinv", [NT, P])
        bank = sp.ps("bank", [P, 512])
        self.deg, self.col = bank[0:NT, 0:P], bank[:, P:P + NT]
        self.made, self.link = sp.sem("made"), sp.sem("link")
        self.counted = sp.sem("counted")
        self.some_done, self.root_done = sp.sem("some_done"), sp.sem("root_done")
        self.dinv_done, self.turned = sp.sem("dinv_done"), sp.sem("turned")
        self.stored = sp.sem("stored", dma=True)

    def dve(self, nc, dve):
        sh, n = self.sh, self.COLS
        with dve.Fori(0, self.pairs) as i:
            for j in range(2):
                t = i * (2 * n) + j * n
                dve.wait_ge(self.counted, START + i * 2 + (j + 1))
                hold(dve)
                for to, numbers, of in ((self.in_win[j], sh.wincol, self.win), (self.in_place[j], sh.iota, self.place)):
                    m = to.shape[2]
                    ins = nc.vector.tensor_tensor(
                        to, numbers[0:E1P, :].rearrange("p (o m) -> p o m", o=1).to_broadcast([E1P, n, m]),
                        of[:, ds(t, n)].rearrange("p (t o) -> p t o", o=1).to_broadcast([E1P, n, m]), ALU.is_equal)
                ins.then_inc(self.made, 1)
        dve.wait_ge(self.counted, START + self.pairs * 2 + 2)
        link = Chain(dve, self.link)
        link(nc.vector.tensor_scalar(self.low, self.deg, 1.0, None, ALU.min))
        nc.vector.tensor_scalar(self.dinv, self.deg, 1.0, None, ALU.max).then_inc(self.some_done, 1)
        dve.wait_ge(self.root_done, START + 1)
        link(nc.vector.reciprocal(self.dinv, self.dinv))
        nc.vector.tensor_tensor(self.dinv, self.dinv, self.low, ALU.mult).then_inc(self.dinv_done, 1)
        dve.wait_ge(self.turned, START + 1)
        link(nc.vector.tensor_copy(sh.dinv_col, self.col))

    def pe(self, nc, pe):
        n = self.COLS
        nc.tensor.sem_inc(self.counted, 2)

        def pair(i, first, last):
            for j in range(2):
                pe.wait_ge(self.made, START + i * 2 + (j + 1))
                for c in range(n):
                    ins = nc.tensor.matmul(self.deg, self.in_win[j][:, c, :], self.in_place[j][:, c, :],
                                           start=first and j == 0 and c == 0, stop=last and j == 1 and c == n - 1)
                ins.then_inc(self.counted, 1)
        pair(0, True, False)
        with pe.Fori(1, self.pairs - 1) as i:
            pair(i, False, False)
        pair(self.pairs - 1, False, True)
        pe.wait_ge(self.dinv_done, START + 1)
        nc.tensor.transpose(self.col, self.dinv, self.sh.ident[0:NT, 0:NT]).then_inc(self.turned, 1)

    def act(self, nc, act):
        act.wait_ge(self.some_done, START + 1)
        nc.scalar.activation(self.dinv, self.dinv, ACT.Sqrt).then_inc(self.root_done, 1)

    def sp(self, nc, sp):
        sp.wait_ge(self.dinv_done, START + 1)
        sp.dma_start(self.out, self.dinv).then_inc(self.stored, 16)
        sp.wait_ge(self.stored, 16)


class Layers:

    TILES = NP // HW
    LAST = N - (NP // HW - 1) * HW

    def __init__(self, sp, sh, scat, edges, cw, table, mlp_w, mlp_b, ew1, ew2, bn_g, bn_b):
        self.sh, self.scat, self.d, self.table = sh, scat, (mlp_w, mlp_b, ew1, ew2, bn_g, bn_b), table
        self.g = Gather(sp, NC1, edges, RC, table, TW, place=False)
        self.agge = sh.agge
        self.a = Aggregate(sp, sh, self.g, edges, cw, sh.agg, False, self.agge, place=False)
        both = FB * GW
        place = sp.sb("place", [P, S * U * TW])
        self.g.rows = [place[:, s * U * TW:(s + 1) * U * TW].rearrange("p (u w) -> p u w", u=U) for s in range(S)]
        by_block = lambda a: a.rearrange("p (f n) -> p f n", f=FB)
        self.slot = [by_block(place[:, j * both:(j + 1) * both]) for j in range(2)]
        self.full = [by_block(place[:, j * both // 2:(j + 1) * both // 2]) for j in range(2)]
        hots = sp.sb("hots", [P, S * U * P])
        self.a.hot = [hots[:, s * U * P:(s + 1) * U * P].rearrange("p (u n) -> p u n", u=U) for s in range(S)]
        self.rows = hots[:, 0:GT * TW].rearrange("p (t w) -> p t w", t=GT)
        self.w, self.ew = sp.sb("w", [P, 2 * FB, D]), sp.sb("ew", [4, D])
        self.b, self.bn_g, self.bn_b = (sp.sb(n, [P, LAYERS * FB]) for n in ("b", "bn_g", "bn_b"))
        self.stats, self.mv = sp.sb("stats", [P, FB, self.TILES, 6]), sp.sb("mv", [P, FB, 2])
        self.rstd, self.part = sp.sb("rstd", [P, FB]), sp.sb("part", [P, FB])
        self.turn = [sp.ps(f"turn{j}", [P, 512]) for j in range(2)]
        self.edge = sp.ps("edge", [P, 2, 512])
        self.link, self.var_done, self.root_done = sp.sem("link"), sp.sem("var_done"), sp.sem("root_done")
        self.loaded, self.w_here = sp.sem("loaded", dma=True), sp.sem("w_here", dma=True)
        self.normed, self.back = sp.sem("normed"), sp.sem("back")
        self.turned = sp.sem("turned")
        self.row_done = [sp.sem(f"row_done{j}") for j in range(2)]
        self.stored, self.zeroed = [sp.sem(f"stored{n}") for n in range(2)], sp.sem("zeroed")
        self.edge_done, self.edge_used, self.full_done = sp.sem("edge_done"), sp.sem("edge_used"), sp.sem("full_done")
        self.mixed, self.relu_done = sp.sem("mixed"), sp.sem("relu_done")
        self.bn_ready = sp.sem("bn_ready")

    def each(self, eng, layer):
        layer(0, True)
        with eng.Fori(1, LAYERS) as l:
            layer(l, False)

    def groups(self, eng, group):
        with eng.Fori(0, NG // 2) as i:
            for j in range(2):
                group(i * 2 + j, j)
        group(NG - 1, 0)

    def sp(self, nc, sp):
        mlp_w, mlp_b, ew1, ew2, bn_g, bn_b = self.d
        for to, src in ((self.b, mlp_b), (self.bn_g, bn_g), (self.bn_b, bn_b)):
            sp.dma_start(to, src.rearrange("l (f p) -> p (l f)", p=P),
                         allow_slow_non_contiguous=True).then_inc(self.loaded, 16)

        def layer(l, first):
            sp.wait_ge(self.bn_ready, START + l + 1)
            hold(sp)
            sp.dma_start(self.w, mlp_w[ds(l, 1)].rearrange("l (k p) d -> p (l k) d", p=P)).then_inc(self.w_here, 16)
            sp.dma_start(self.ew[3:4, 0:P], ew1[ds(l, 1)].rearrange("l k d -> (l k) d")).then_inc(self.w_here, 16)
            sp.dma_start(self.ew[0:3, P:D], ew2[ds(l, 1)].rearrange("l k d -> (l k) d")).then_inc(self.w_here, 16)
            with sp.Fori(0, NG) as g:
                it = l * NG + g
                for n, (t0, t1) in enumerate(self.PARTS):
                    for j in range(2):
                        sp.wait_ge(self.row_done[j], START + it * (4 - j) + (t1 + 1 - j) // 2)
                        hold(sp)
                    sp.dma_start(group_rows(self.table, g)[:, t0:t1, :],
                                 self.rows[:, t0:t1, :]).then_inc(self.stored[n], 16)
        self.each(sp, layer)

    PARTS = ((0, GT // 2 + 1), (GT // 2 + 1, GT))

    def act(self, nc, act):
        sh = self.sh
        act.wait_ge(self.loaded, 48)
        nc.scalar.sem_inc(self.relu_done, 1)

        def layer(l, first):
            act.wait_ge(self.bn_ready, START + l + 1)
            hold(act)

            def group(g, j):
                it = l * NG + g
                func = ACT.Identity if first else ACT.Relu
                act.wait_ge(self.turned, START + it * GT)
                hold(act)
                for f in range(FB):
                    ins = nc.scalar.activation(self.slot[j][:, f, :], sh.h[:, f, ds(g * GW, GW)], func,
                                               bias=sh.shift[:, f:f + 1], scale=sh.scale[:, f:f + 1])
                ins.then_inc(self.normed, 1)
                if not first:
                    for f in range(FB):
                        here = sh.h[:, f, ds(g * GW, GW)]
                        ins = nc.scalar.activation(here, here, func, bias=sh.shift[:, f:f + 1],
                                                   scale=sh.scale[:, f:f + 1])
                    ins.then_inc(self.back, 1)
            self.groups(act, group)
            with act.Fori(0, self.g.turns) as i:
                for s in range(S):
                    self.g.act_set(nc, act, l * self.g.turns + i, i, s)
            with act.Fori(0, self.TILES // 2) as m2:
                for j in range(2):
                    act.wait_ge(self.mixed, START + l * self.TILES + m2 * 2 + (j + 2))
                    for o in range(FB):
                        ins = nc.scalar.activation(sh.h[:, o, ds((m2 * 2 + j) * HW, HW)],
                                                   self.a.bank[2 * j + o][:, 0:HW], ACT.Relu,
                                                   bias=self.b[:, ds(l * FB + o, 1)])
                    ins.then_inc(self.relu_done, 1)
            act.wait_ge(self.var_done, START + l + 1)
            nc.scalar.activation(self.rstd, self.rstd, ACT.Sqrt).then_inc(self.root_done, 1)
        self.each(act, layer)

    def pool(self, nc, pool):
        def layer(l, first):
            if first:
                nc.gpsimd.memset(self.agge, 0.0).then_inc(self.zeroed, 1)
            else:
                pool.wait_ge(self.full_done, START + l * self.TILES)
            hold(pool)
            nc.gpsimd.memset(self.sh.agg, 0.0).then_inc(self.zeroed, 1)
            for n in range(2):
                pool.wait_ge(self.stored[n], START + (l + 1) * (NG * 16))
                hold(pool)
            with pool.Fori(0, self.g.turns) as i:
                for s in range(S):
                    self.g.pool_set(nc, pool, l * self.g.turns + i, s)
            per = self.scat.sets // LAYERS
            self.scat.pool(nc, pool, l * per, per, first)
        self.each(pool, layer)
        self.scat.pool_rest(nc, pool)

    def pe(self, nc, pe):
        sh = self.sh
        nc.tensor.sem_inc(self.g.used, AHEAD)
        nc.tensor.sem_inc(self.turned, GT)
        nc.tensor.sem_inc(self.mixed, 1)

        def layer(l, first):
            def group(g, j):
                it = l * NG + g
                pe.wait_ge(self.normed, START + it + 1)
                for t in range(GT):
                    b = t % 2
                    pe.wait_ge(self.row_done[b], START + it * (4 - b) + t // 2)
                    for f in range(FB):
                        ins = nc.tensor.transpose(self.turn[b][:, f * P:(f + 1) * P],
                                                  self.slot[j][:, f, t * P:(t + 1) * P], sh.ident)
                    ins.then_inc(self.turned, 1)
            self.groups(pe, group)
            if not first:
                pe.wait_ge(self.relu_done, START + l * self.TILES + 1)
            hold(pe)
            with pe.Fori(0, self.g.turns) as i:
                for s in range(S):
                    self.a.pe_set(nc, pe, l * self.g.turns + i, s, first)
            pe.wait_ge(self.w_here, (l + 1) * 48)
            if not first:
                pe.wait_ge(self.back, START + l * NG)
            for b in range(U):
                pe.wait_ge(self.a.added[b], START + (l + 1) * (NC1 // U))
            hold(pe)

            def edge(m):
                it = l * self.TILES + m
                pe.wait_ge(self.edge_used, START + it)
                for f in range(FB):
                    ins = nc.tensor.matmul(self.edge[:, f, 0:HW], self.ew[:, f * P:(f + 1) * P],
                                           self.agge[:, ds(m * HW, HW)], start=True, stop=True)
                ins.then_inc(self.edge_done, 1)

            def mix(m, j):
                it = l * self.TILES + m
                pe.wait_ge(self.full_done, START + it + 1)
                pe.wait_ge(self.relu_done, START + it)
                for o in range(FB):
                    for kk in range(2 * FB):
                        rhs = sh.h[:, kk, ds(m * HW, HW)] if kk < FB else self.full[j][:, kk - FB, :]
                        ins = nc.tensor.matmul(self.a.bank[2 * j + o][:, 0:HW], self.w[:, kk, o * P:(o + 1) * P],
                                               rhs, start=(kk == 0), stop=(kk == 2 * FB - 1))
                ins.then_inc(self.mixed, 1)
            edge(0)
            with pe.Fori(0, self.TILES // 2 - 1) as m2:
                for j in range(2):
                    edge(m2 * 2 + (j + 1))
                    mix(m2 * 2 + j, j)
            edge(self.TILES - 1)
            for j in range(2):
                mix(self.TILES - 2 + j, j)
        self.each(pe, layer)

    PER = 5

    def dve(self, nc, dve):
        sh = self.sh
        link0 = Chain(dve, self.link)
        link0(nc.vector.memset(sh.scale, 1.0))
        link0(nc.vector.memset(sh.shift, 0.0))
        link0(nc.vector.memset(self.ew, 0.0))
        nc.vector.sem_inc(self.bn_ready, 1)
        dve.wait_ge(self.loaded, 48)
        before = link0.n

        def layer(l, first):
            with dve.Fori(0, NG) as g:
                it = l * NG + g
                for n, (t0, t1) in enumerate(self.PARTS):
                    dve.wait_ge(self.stored[n], START + it * 16)
                    nc.vector.tensor_copy(self.rows[:, t0:t1, D:TW], sh.dinv_col[:, ds(g * GT + t0, t1 - t0)].rearrange(
                        "p (t o) -> p t o", o=1).to_broadcast([P, t1 - t0, TW - D]))
                    for t in range(t0, t1):
                        dve.wait_ge(self.turned, START + it * GT + (t + 1 + GT))
                        nc.vector.tensor_scalar(self.rows[:, t, 0:D], self.turn[t % 2][:, 0:D],
                                                sh.dinv_col[:, ds(g * GT + t, 1)], None,
                                                ALU.mult).then_inc(self.row_done[t % 2], 1)
            dve.wait_ge(self.zeroed, START + l + 2)
            for n in range(2):
                dve.wait_ge(self.stored[n], START + (l + 1) * (NG * 16))
                hold(dve)
            self.a.dve(nc, dve, l * self.g.turns, first)
            for b in range(U):
                dve.wait_ge(self.a.added[b], START + (l + 1) * (NC1 // U))
            hold(dve)

            def full(m, j):
                it = l * self.TILES + m
                dve.wait_ge(self.edge_done, START + it + 1)
                dve.wait_ge(self.mixed, START + it)
                hold(dve)
                nc.vector.tensor_tensor(self.full[j], self.edge[:, :, 0:HW], sh.agg[:, :, ds(m * HW, HW)],
                                        ALU.add).then_inc(self.edge_used, 1)
                dve.wait_ge(self.edge_used, START + it + 1)
                for f in range(FB):
                    ins = nc.vector.tensor_tensor(self.full[j][:, f, :], self.full[j][:, f, :],
                                                  sh.dinv_row[:, ds(m * HW, HW)], ALU.mult)
                ins.then_inc(self.full_done, 1)

            def spread(m, n, ins=None):
                dve.wait_ge(self.relu_done, START + l * self.TILES + m + 2)
                hold(dve)
                for o in range(FB):
                    ins = nc.vector.bn_stats(self.stats[:, o, ds(m, 1), :].rearrange("p m s -> p (m s)"),
                                             sh.h[:, o, ds(m * HW, n)])
                return ins
            for j in range(2):
                full(j, j)
            with dve.Fori(1, self.TILES // 2) as m2:
                for j in range(2):
                    full(m2 * 2 + j, j)
                    spread(m2 * 2 + (j - 2), HW)
            link = Chain(dve, self.link, l * self.PER + before)
            spread(self.TILES - 2, HW)
            link(spread(self.TILES - 1, self.LAST))
            hold(dve)
            for o in range(FB):
                ins = nc.vector.bn_aggr(self.mv[:, o, :], self.stats[:, o].rearrange("p m s -> p (m s)"))
            link(ins)
            nc.vector.tensor_scalar(self.rstd, self.mv[:, :, 1], BN_EPS, None, ALU.add).then_inc(self.var_done, 1)
            dve.wait_ge(self.root_done, START + l + 1)
            link(nc.vector.reciprocal(self.rstd, self.rstd))
            link(nc.vector.tensor_tensor(sh.scale, self.bn_g[:, ds(l * FB, FB)], self.rstd, ALU.mult))
            link(nc.vector.tensor_tensor(self.part, self.mv[:, :, 0], sh.scale, ALU.mult))
            nc.vector.tensor_tensor(sh.shift, self.bn_b[:, ds(l * FB, FB)], self.part,
                                    ALU.subtract).then_inc(self.bn_ready, 1)
        self.each(dve, layer)


def top2(nc, link, v, rank, cmp, E):
    link(nc.vector.memset(rank, 0.0))
    for j in range(E):
        for lo, hi, op in ((0, j, ALU.is_gt), (j + 1, E, ALU.is_ge)):
            if lo < hi:
                link(nc.vector.tensor_tensor(cmp[:, :, lo:hi], v[:, :, j:j + 1].to_broadcast([P, NT, hi - lo]),
                                             v[:, :, lo:hi], op))
                link(nc.vector.tensor_tensor(rank[:, :, lo:hi], rank[:, :, lo:hi], cmp[:, :, lo:hi], ALU.add))


class Shares:

    def __init__(self, sp, v, E, all_first, share):
        self.v, self.E, self.all_first, self.share = v, E, all_first, share
        self.rank, self.cmp, self.ex = (sp.sb(n, [P, NT, E]) for n in ("rank", "cmp", "ex"))
        self.most, self.total = sp.sb("most", [P, NT]), sp.sb("total", [P, NT])
        self.low_done, self.ex_done = sp.sem("gate_low"), sp.sem("gate_ex")

    def dve(self, nc, dve, link):
        E = self.E
        wide = lambda x: x.rearrange("p (t o) -> p t o", o=1).to_broadcast([P, NT, E])
        link(nc.vector.tensor_reduce(self.most, self.v, AX.X, ALU.max))
        nc.vector.tensor_tensor(self.ex, self.v, wide(self.most), ALU.subtract).then_inc(self.low_done, 1)
        dve.wait_ge(self.ex_done, START + 1)
        if self.all_first:
            link(nc.vector.tensor_reduce(self.total, self.ex, AX.X, ALU.add))
            link(nc.vector.reciprocal(self.total, self.total))
            link(nc.vector.tensor_tensor(self.ex, self.ex, wide(self.total), ALU.mult))
        top2(nc, link, self.ex if self.all_first else self.v, self.rank, self.cmp, E)
        link(nc.vector.scalar_tensor_tensor(self.share, self.rank, 1.5, self.ex, ALU.is_lt, ALU.mult))
        link(nc.vector.tensor_reduce(self.total, self.share, AX.X, ALU.add))
        link(nc.vector.tensor_scalar(self.total, self.total, 1e-12, None, ALU.max))
        link(nc.vector.reciprocal(self.total, self.total))
        link(nc.vector.tensor_tensor(self.share, self.share, wide(self.total), ALU.mult))

    def act(self, nc, act):
        act.wait_ge(self.low_done, START + 1)
        nc.scalar.activation(self.ex, self.ex, ACT.Exp).then_inc(self.ex_done, 1)


class Attention:

    def __init__(self, sp, sh, h16, table, edges, cw, share, d):
        self.sh, self.h16, self.table, self.edges, self.cw, self.d = sh, h16, table, edges, cw, d
        self.share = share
        self.g = Gather(sp, NC2, edges, RD, table, AW, tracked=False)
        self.turns, self.pairs = NC2 // SU, NC2 // (2 * V)
        self.all = sh.agg.rearrange("p f n -> p (f n)")[:, 0:NC2 * AW].rearrange("p (c w) -> p c w", w=AW)
        self.att = sp.sb("att", [P, 5, HX])
        self.row = sp.sb("row", [P, NT, AW])
        self.prod = sp.sb("prod", [P, NT, HX])
        self.node = sp.sb("node", [P, NT, 2 * HEADS])
        self.top, self.low = sp.sb("top", [P, NT, HEADS]), sp.sb("low", [P, NT, HEADS])
        self.sums = sp.sb("sums", [P, NT, AW])
        bf = mybir.dt.bfloat16
        self.cold = [sp.sb(f"cold{s}", [P, U, P], bf) for s in range(S)]
        self.off = sp.sb("off", [P, HEADS, P], bf)
        self.diag = [sp.sb(f"diag{s}", [P, U, HEADS, P]) for s in range(S)]
        halves = [d.rearrange("p u a n -> p (u a) n") for d in self.diag]
        self.hot, self.turned = ([halves[n][:, h * V:(h + 1) * V, :] for h in range(2)] for n in range(2))
        self.red = [sp.sb(f"red{h}", [P, U, HEADS]) for h in range(2)]
        self.z, self.z2 = sp.sb("z", [P, V, HEADS]), sp.sb("z2", [P, V, HEADS])
        self.pay = [sp.sb(f"pay{h}", [P, V, AW]) for h in range(2)]
        self.banks = [sp.ps(f"banks{h}", [P, U, 512]) for h in range(2)]
        self.pt, self.pn = self.banks[0][:, 0:2, :], [self.banks[0][:, 2 + h, :] for h in range(2)]
        self.pd = [self.banks[1][:, h, :] for h in range(2)]
        self.loaded, self.stored = sp.sem("loaded", dma=True), sp.sem("stored", dma=True)
        names = ("link", "rows_ready", "kept", "diag_done", "cold_ready", "maxed", "hot2", "turn_done", "turn_kept",
                 "nodes_done", "z_done", "ex_done", "pay_done", "paid", "summed")
        (self.link, self.rows_ready, self.kept, self.diag_done, self.cold_ready, self.maxed, self.hot2, self.turn_done,
         self.turn_kept, self.nodes_done, self.z_done, self.ex_done, self.pay_done, self.paid,
         self.summed) = (sp.sem(n) for n in names)
        self.spread = sp.sem("spread")
        self.reduced = sp.sem("reduced")
        self.var_done, self.root_done = sp.sem("var_done"), sp.sem("root_done")
        self.gate = Shares(sp, sp.sb("scores", [P, NT, XD]), XD, False, share)

    def sp(self, nc, sp):
        for n, src in enumerate(self.d):
            sp.dma_start(self.att[:, n, :], src.partition_broadcast(P)).then_inc(self.loaded, 16)
        sp.wait_ge(self.rows_ready, START + 1)
        hold(sp)
        sp.dma_start(self.table.rearrange("(t p) w -> p t w", p=P), self.row).then_inc(self.stored, 16)

    def pool(self, nc, pool):
        pool.wait_ge(self.stored, 16)
        hold(pool)
        with pool.Fori(0, self.turns) as i:
            for s in range(S):
                self.g.pool_set(nc, pool, i, s)

    def act(self, nc, act):
        sh = self.sh
        nodes = lambda c: self.edges[:, ds(c, U), 0].bitcast(I32)
        for s in range(S):
            nc.scalar.copy(self.g.idx[s], nodes(s * U)).then_inc(self.g.ready[s], 1)
        with act.Fori(0, self.turns) as i:
            for s in range(S):
                act.wait_ge(self.g.here[s], i * (16 * U) + 16 * U)
                c = i * SU + s * U
                hold(act)
                nc.scalar.copy(self.all[:, ds(c, U), :], self.g.rows[s]).then_inc(self.kept, 1)
                act.wait_ge(self.spread, START + i * S + (s + 1))
                for u in range(U):
                    for a in range(HEADS):
                        ins = nc.scalar.activation(self.diag[s][:, u, a, :], sh.ident, ACT.Copy,
                                                   scale=self.g.rows[s][:, u, a:a + 1])
                ins.then_inc(self.diag_done, 1)
                nc.scalar.copy(self.g.idx[s], nodes(c + SU)).then_inc(self.g.ready[s], 1)

        def keep_turned(k, h):
            act.wait_ge(self.turn_done, START + k + 1)
            nc.scalar.copy(self.turned[h].rearrange("p u n -> p (u n)").rearrange("p (b n) -> p b n", b=2),
                           self.pt).then_inc(self.turn_kept, 1)

        def step(k, h, last):
            act.wait_ge(self.z_done, START + k * 3 + 3)
            nc.scalar.activation(self.pay[h][:, :, 0:HEADS], self.z, ACT.Exp).then_inc(self.ex_done, 1)
            if not last:
                keep_turned(k + 1, 1 - h)
        keep_turned(0, 0)
        self.steps(act, step)
        act.wait_ge(self.var_done, START + 1)
        nc.scalar.activation(self.top[:, :, 0], self.top[:, :, 0], ACT.Sqrt).then_inc(self.root_done, 1)
        self.gate.act(nc, act)

    def steps(self, eng, step):
        with eng.Fori(0, self.pairs - 1) as i:
            for h in range(2):
                step(i * 2 + h, h, False)
        for h in range(2):
            step(self.pairs * 2 - 2 + h, h, h == 1)

    def pe(self, nc, pe):
        sh = self.sh
        nc.tensor.sem_inc(self.spread, S)
        with pe.Fori(0, self.turns) as i:
            for s in range(S):
                pe.wait_ge(self.diag_done, START + i * S + (s + 1))
                pe.wait_ge(self.cold_ready, START + i * S + (s + 1))
                pe.wait_ge(self.reduced, START + i * S + (s + 1))
                for u in range(U):
                    bank = self.banks[s % 2][:, u, :]
                    nc.tensor.matmul(bank, sh.ones, self.diag[s][:, u].rearrange("p a n -> p (a n)"), start=True,
                                     stop=False)
                    ins = nc.tensor.matmul(bank, self.cold[s][:, u, :], self.off.rearrange("p a n -> p (a n)"),
                                           start=False, stop=True)
                ins.then_inc(self.spread, 1)

        def look_up(k, h):
            pe.wait_ge(self.hot2, START + k + 1)
            pe.wait_ge(self.turn_kept, START + k)
            for u in range(V):
                ins = nc.tensor.transpose(self.pt[:, u // 4, (u % 4) * P:(u % 4 + 1) * P], self.hot[h][:, u, :],
                                          sh.ident)
            ins.then_inc(self.turn_done, 1)
            windows = windows_of(nc, mybir.EngineType.PE, self.cw, k * V, V)
            pe.wait_ge(self.turn_kept, START + k + 1)
            hold(pe)
            for u, w in enumerate(windows):
                ins = nc.tensor.matmul(self.pn[h][:, u * 2 * HEADS:(u + 1) * 2 * HEADS], self.turned[h][:, u, :],
                                       self.node[:, ds(w, 1), :].rearrange("p o c -> p (o c)"), start=True, stop=True)
            ins.then_inc(self.nodes_done, 1)

        def pay(k, h):
            pe.wait_ge(self.pay_done, START + k + 1)
            for u in range(V):
                ins = nc.tensor.matmul(self.pd[h][:, u * 32:u * 32 + AW], self.hot[h][:, u, :], self.pay[h][:, u, :],
                                       start=True, stop=True)
            ins.then_inc(self.paid, 1)

        def step(k, h, last):
            if not last:
                look_up(k + 1, 1 - h)
            pay(k, h)
        pe.wait_ge(self.reduced, START + self.turns * S + 2)
        look_up(0, 0)
        self.steps(pe, step)

    def dve(self, nc, dve):
        sh = self.sh
        link = Chain(dve, self.link)
        dve.wait_ge(self.loaded, 5 * 16)
        across = lambda n: self.att[:, n:n + 1, :].to_broadcast([P, NT, HX])
        by_head = lambda x: x.rearrange("p t (h x) -> p t h x", h=HEADS)
        for n, to in ((0, self.row[:, :, 0:HEADS]), (1, self.node[:, :, 0:HEADS])):
            link(nc.vector.tensor_tensor(self.prod, self.h16, across(n), ALU.mult))
            link(nc.vector.tensor_reduce(to, by_head(self.prod), AX.X, ALU.add))
        nc.vector.tensor_copy(self.row[:, :, HEADS:AW], self.h16).then_inc(self.rows_ready, 1)
        for a in range(HEADS):
            link(nc.vector.tensor_scalar(self.off[:, a, :], sh.ident, -BIG, None, ALU.mult))
        link(nc.vector.memset(self.top, -3e38))
        link(nc.vector.memset(self.sums, 0.0))
        nc.vector.sem_inc(self.reduced, 2)

        def matrices(k, c, s):
            dve.wait_ge(self.spread, START + k + 1)
            hold(dve)
            for u in range(U):
                ins = nc.vector.tensor_scalar(self.cold[s][:, u, :], sh.iota, self.edges[:, ds(c + u, 1), 1], None,
                                              ALU.not_equal)
            ins.then_inc(self.cold_ready, 1)

        def largest(i, last):
            for s in range(S):
                k, c = i * S + s, i * SU + s * U
                if not (last and s == S - 1):
                    matrices(k + 1, c + U, (s + 1) % S)
                red = self.red[s % 2]
                dve.wait_ge(self.spread, START + k + (1 + S))
                nc.vector.tensor_reduce(red, self.banks[s % 2].rearrange("p u (a n) -> p u a n", a=HEADS), AX.X,
                                        ALU.max).then_inc(self.reduced, 1)
                windows = windows_of(nc, mybir.EngineType.DVE, self.cw, c, U)
                dve.wait_ge(self.reduced, START + k + 3)
                for u, w in enumerate(windows):
                    dve.wait_ge(self.maxed, START + c + u)
                    to = self.top[:, ds(w, 1), :]
                    nc.vector.tensor_tensor(to, to, red[:, u:u + 1, :], ALU.max).then_inc(self.maxed, 1)
        matrices(0, 0, 0)
        with dve.Fori(0, self.turns - 1) as i:
            largest(i, False)
        largest(self.turns - 1, True)
        dve.wait_ge(self.maxed, START + NC2)
        link(nc.vector.tensor_tensor(self.top, self.top, self.node[:, :, 0:HEADS], ALU.add))
        link(nc.vector.tensor_scalar(self.low, self.top, 0.2, None, ALU.mult))
        link(nc.vector.tensor_tensor(self.node[:, :, HEADS:2 * HEADS], self.top, self.low, ALU.max))
        dve.wait_ge(self.kept, START + NC2 // U)
        hold(dve)

        def edge_matrices(k, h):
            if not isinstance(k, int) or k:
                dve.wait_ge(self.paid, START + k - 1)
                hold(dve)
            for u in range(V):
                ins = nc.vector.tensor_scalar(self.hot[h][:, u, :], sh.iota, self.edges[:, ds(k * V + u, 1), 1], None,
                                              ALU.is_equal)
            ins.then_inc(self.hot2, 1)

        def add(k, h):
            windows = windows_of(nc, mybir.EngineType.DVE, self.cw, k * V, V)
            dve.wait_ge(self.paid, START + k + 1)
            for u, w in enumerate(windows):
                dve.wait_ge(self.summed, START + k * V + u)
                to = self.sums[:, ds(w, 1), :].rearrange("p o c -> p (o c)")
                nc.vector.tensor_tensor(to, to, self.pd[h][:, u * 32:u * 32 + AW], ALU.add).then_inc(self.summed, 1)

        def step(k, h, last, first=False):
            rows = self.all[:, ds(k * V, V), :]
            pn = self.pn[h][:, 0:V * 2 * HEADS].rearrange("p (u c) -> p u c", u=V)
            dve.wait_ge(self.nodes_done, START + k + 1)
            dve.wait_ge(self.ex_done, START + k)
            hold(dve)
            nc.vector.tensor_tensor(self.z, rows[:, :, 0:HEADS], pn[:, :, 0:HEADS], ALU.add).then_inc(self.z_done, 1)
            dve.wait_ge(self.z_done, START + k * 3 + 1)
            nc.vector.scalar_tensor_tensor(self.z2, self.z, 0.2, self.z, ALU.mult, ALU.max).then_inc(self.z_done, 1)
            dve.wait_ge(self.z_done, START + k * 3 + 2)
            nc.vector.tensor_tensor(self.z, self.z2, pn[:, :, HEADS:2 * HEADS], ALU.subtract).then_inc(self.z_done, 1)
            if not last:
                edge_matrices(k + 1, 1 - h)
            if not first:
                add(k - 1, 1 - h)
            dve.wait_ge(self.ex_done, START + k + 1)
            pay = self.pay[h][:, :, HEADS:AW].rearrange("p u (a x) -> p u a x", a=HEADS)
            ex = self.pay[h][:, :, 0:HEADS].rearrange("p u (a o) -> p u a o", o=1).to_broadcast([P, V, HEADS, XD])
            nc.vector.tensor_tensor(pay, rows[:, :, HEADS:AW].rearrange("p u (a x) -> p u a x", a=HEADS), ex,
                                    ALU.mult).then_inc(self.pay_done, 1)
        edge_matrices(0, 0)
        for h in range(2):
            step(h, h, False, h == 0)
        with dve.Fori(1, self.pairs - 1) as i:
            for h in range(2):
                step(i * 2 + h, h, False)
        for h in range(2):
            step(self.pairs * 2 - 2 + h, h, h == 1)
        add(self.pairs * 2 - 1, 1)
        dve.wait_ge(self.summed, START + NC2)
        den, out = self.sums[:, :, 0:HEADS], self.sums[:, :, HEADS:AW]
        link(nc.vector.tensor_scalar(den, den, 1e-16, None, ALU.add))
        link(nc.vector.reciprocal(self.low, den))
        wide = self.low.rearrange("p t (a o) -> p t a o", o=1).to_broadcast([P, NT, HEADS, XD])
        link(nc.vector.tensor_tensor(by_head(self.prod), by_head(out), wide, ALU.mult))
        link(nc.vector.tensor_tensor(self.prod, self.prod, across(2), ALU.add))
        mean = self.top[:, :, 0]
        over = self.top[:, :, 0:1].to_broadcast([P, NT, HX])
        link(nc.vector.tensor_reduce(mean, self.prod, AX.X, ALU.add))
        link(nc.vector.tensor_scalar(mean, mean, 1.0 / HX, None, ALU.mult))
        link(nc.vector.tensor_tensor(self.prod, self.prod, over, ALU.subtract))
        link(nc.vector.tensor_tensor(out, self.prod, self.prod, ALU.mult))
        link(nc.vector.tensor_reduce(mean, out, AX.X, ALU.add))
        nc.vector.tensor_scalar(mean, mean, 1.0 / HX, LN_EPS, ALU.mult, ALU.add).then_inc(self.var_done, 1)
        dve.wait_ge(self.root_done, START + 1)
        link(nc.vector.reciprocal(mean, mean))
        link(nc.vector.tensor_tensor(self.prod, self.prod, over, ALU.mult))
        link(nc.vector.tensor_tensor(self.prod, self.prod, across(3), ALU.mult))
        link(nc.vector.tensor_tensor(self.prod, self.prod, across(4), ALU.add))
        link(nc.vector.tensor_reduce(self.gate.v, self.prod.rearrange("p t (h x) -> p t x h", h=HEADS), AX.X, ALU.add))
        link(nc.vector.tensor_scalar(self.gate.v, self.gate.v, 1.0 / HEADS, None, ALU.mult))
        self.gate.dve(nc, dve, link)


class AddTurned:

    def __init__(self, sp, sh, table):
        self.sh, self.table = sh, table
        self.x = [sp.sb(f"x{j}", [P, D]) for j in range(2)]
        self.turn = [sp.ps(f"turn{j}", [P, 512]) for j in range(2)]
        self.here = [sp.sem(f"here{j}", dma=True) for j in range(2)]
        self.turned = [sp.sem(f"turned{j}") for j in range(2)]
        self.added = [sp.sem(f"added{j}") for j in range(2)]

    def tiles(self, eng, body):
        with eng.Fori(0, NT // 2) as i:
            for j in range(2):
                body(i * 2 + j, j, i)
        body(NT - 1, 0, NT // 2)

    def sp(self, nc, sp):
        def load(t, j, n):
            sp.wait_ge(self.turned[j], START + n)
            hold(sp)
            sp.dma_start(self.x[j], self.table[ds(t * P, P), :]).then_inc(self.here[j], 16)
        self.tiles(sp, load)

    def pe(self, nc, pe):
        def turn(t, j, n):
            pe.wait_ge(self.here[j], n * 16 + 16)
            pe.wait_ge(self.added[j], START + n)
            for f in range(FB):
                ins = nc.tensor.transpose(self.turn[j][:, f * P:(f + 1) * P], self.x[j][:, f * P:(f + 1) * P],
                                          self.sh.ident)
            ins.then_inc(self.turned[j], 1)
        self.tiles(pe, turn)

    def dve(self, nc, dve):
        def add(t, j, n):
            dve.wait_ge(self.turned[j], START + n + 1)
            to = self.sh.agg[:, :, ds(t * P, P)]
            nc.vector.tensor_tensor(to, to, self.turn[j][:, 0:D].rearrange("p (f n) -> p f n", f=FB),
                                    ALU.add).then_inc(self.added[j], 1)
        self.tiles(dve, add)


def program(nc, x, src, dst, edge_attr_4, edge_weight, L0_gnn_W1, L0_gnn_b1, L0_gnn_W2, L0_gnn_b2, L0_ffn_router_w,
            L0_ffn_w1, L0_ffn_b1, L0_ffn_w2, L0_ffn_b2, L1_gnn_mlp_w, L1_gnn_mlp_b, L1_gnn_ew1, L1_gnn_ew2,
            L1_gnn_bn_g, L1_gnn_bn_b, L1_ffn_W_gat, L1_ffn_att_src, L1_ffn_att_dst, L1_ffn_b_gat, L1_ffn_ln_gamma,
            L1_ffn_ln_beta, L1_ffn_W1, L1_ffn_b1, L1_ffn_W2, L1_ffn_b2, L1_ffn_edge_index, out, last_phase=99):
    table = lambda name, shape: nc.dram_tensor(name, shape, F32, kind="Internal").ap()
    x0, xn0, x1, both1, x2, x3 = (table(n, [NP, D]) for n in ("x0", "xn0", "x1", "both1", "x2", "x3"))
    listA, listC, listD = (table(n, [P * c, r]) for n, c, r in
                           (("listA", NC1, RA), ("listC", NC1, RC), ("listD", NC2, RD)))
    dinv = table("dinv", [NT, P])
    nodesC, nodesD = table("nodesC", [NP, TW]), table("nodesD", [NP, AW])
    lanes = lambda lst: lst.rearrange("(p c) w -> p (c w)", p=P)

    with ExitStack() as whole:
        sb = lambda name, shape, dt=F32: whole.enter_context(nc.sbuf_tensor(name, shape, dt))[:]
        sh = Shared()
        rows = sb("rows", [P, NP])
        cwC, cwD = rows[32:33, 0:NC1].bitcast(I32), rows[64:65, 0:NC2].bitcast(I32)
        sh.agge = rows[0:4, :]
        sh.h, sh.agg = sb("h", [P, FB, NP]), sb("agg", [P, FB, NP])
        sh.ident, sh.iota, sh.ones, sh.below = (sb(n, [P, P]) for n in ("ident", "iota", "ones", "below"))
        sh.wincol = sb("wincol", [P, NT])
        sh.scale, sh.shift, sh.dinv_col = sb("scale", [P, FB]), sb("shift", [P, FB]), sb("dinv_col", [P, NT])

        def cut(whole_tile):
            flat, at = whole_tile.rearrange("p f n -> p (f n)"), [0]

            def take(parts, *shape):
                n = 1
                for d in shape:
                    n *= d
                piece = flat[0:parts, at[0]:at[0] + n]
                at[0] += n
                return piece if len(shape) == 1 else piece.rearrange("p (t w) -> p t w", w=shape[1])
            return take
        take = cut(sh.h)
        cwA = take(1, NC1).bitcast(I32)
        recA, recC = take(E1P, E1T, RA), take(E1P, E1T, RC)
        rowA, rowC = take(E1P, E1T).bitcast(I32), take(E1P, E1T).bitcast(I32)
        recD, rowD = sb("recD", [P, E2T, RD]), sb("rowD", [P, E2T], I32)
        scatC = Scatter(Space(nc, whole, [], "scatC"), E1P, E1T, NC1, rowC, recC, listC, RC)
        scatD = Scatter(Space(nc, whole, [], "scatD"), P, E2T, NC2, rowD, recD, listD, RD)
        take = cut(sh.agg)
        src_sb, dst_sb = take(E1P, E1T).bitcast(I32), take(E1P, E1T).bitcast(I32)
        sh.chunkrow = take(P, NC1)
        wt_sb, attr_sb = take(E1P, E1T), take(E1P, E1T, 4)
        from_sb, to_sb = take(P, E2T).bitcast(I32), take(P, E2T).bitcast(I32)

        def phase(name, build):
            sems = []
            with ExitStack() as mem:
                build(lambda part: Space(nc, mem, sems, f"{name}_{part}"))
            numbers = sorted(s.num for s in sems)
            while numbers:
                n = next((i for i in range(1, len(numbers)) if numbers[i] != numbers[0] + i), len(numbers))
                nc.sync.sem_clear(range(numbers[0], numbers[n - 1] + 1))
                numbers = numbers[n:]
            nc.all_engine_barrier()
            for s in sems:
                nc.release_semaphore(s)

        def setup(space):
            sp_ = space("in")
            sort = Sort(space("sort"), sh, E1P, E1T, NC1, src_sb, recA, rowA, cwA)
            pads = [sp_.sb(f"pad{n}", [P, c, r]) for n, c, r in ((0, NC1, RA), (1, NC1, RC), (2, NC2, RD))]
            zero = sp_.sb("zero", [NP - N, D])
            loaded, stored = sp_.sem("loaded", dma=True), sp_.sem("stored", dma=True)
            const, padded, recs, ready = (sp_.sem(n) for n in ("const", "padded", "recs", "ready"))
            cut1 = lambda a: a.rearrange("(p t) -> p t", p=E1P)
            with nc.Block() as block:
                @block.sync
                def _(sp):
                    sp.dma_start(src_sb, cut1(src)).then_inc(loaded, 16)
                    sp.dma_start(dst_sb, cut1(dst)).then_inc(loaded, 16)
                    sp.dma_start(wt_sb, cut1(edge_weight)).then_inc(loaded, 16)
                    sp.dma_start(attr_sb, edge_attr_4.rearrange("(p t) w -> p t w", p=E1P)).then_inc(loaded, 16)
                    for n, to in ((0, from_sb), (1, to_sb)):
                        sp.dma_start(to[:, 0:E2T - NT], L1_ffn_edge_index[n].rearrange("(p t) -> p t",
                                                                                      p=P)).then_inc(loaded, 16)
                    sp.dma_start(x0[0:N, :], x).then_inc(stored, 16)
                    sp.wait_ge(padded, START + 4)
                    hold(sp)
                    sp.dma_start(x0[N:NP, :], zero).then_inc(stored, 16)
                    for pad, lst in zip(pads, (listA, listC, listD)):
                        sp.dma_start(lanes(lst), pad.rearrange("p c w -> p (c w)")).then_inc(stored, 16)
                    sp.wait_ge(stored, 5 * 16)
                    sp.wait_ge(recs, START + 1)

                @block.gpsimd
                def _(pool):
                    nc.gpsimd.iota(sh.iota, [[1, P]], base=0, channel_multiplier=0,
                                   allow_small_or_imprecise_dtypes=True)
                    nc.gpsimd.iota(sh.wincol, [[1, NT]], base=0, channel_multiplier=0,
                                   allow_small_or_imprecise_dtypes=True)
                    nc.gpsimd.iota(sh.chunkrow, [[P, NC1]], base=0, channel_multiplier=0,
                                   allow_small_or_imprecise_dtypes=True)
                    nc.gpsimd.memset(sh.ones, 1.0)
                    nc.gpsimd.memset(sh.below, 1.0)
                    nc.gpsimd.memset(sh.ident, 0.0).then_inc(const, 1)
                    for to in (from_sb, to_sb):
                        nc.gpsimd.iota(to[:, E2T - NT:E2T], [[P, NT]], base=0, channel_multiplier=1)
                    pool.wait_ge(const, START + 1)
                    nc.gpsimd.affine_select(out=sh.below, in_=sh.below, compare_op=ALU.is_gt, fill=0.0, base=0,
                                            pattern=[[1, P]], channel_multiplier=-1)
                    nc.gpsimd.affine_select(out=sh.ident, in_=sh.ident, compare_op=ALU.not_equal, fill=1.0, base=0,
                                            pattern=[[-1, P]], channel_multiplier=1).then_inc(ready, 1)
                    nc.gpsimd.memset(zero, 0.0).then_inc(padded, 1)
                    for n, pad in enumerate(pads):
                        nc.gpsimd.memset(pad, 0.0).then_inc(const, 1)
                        pool.wait_ge(const, START + n * 2 + 2)
                        nc.gpsimd.memset(pad[:, :, 1], -1.0).then_inc(const, 1)
                        nc.gpsimd.memset(pad.bitcast(I32)[:, :, 0], N).then_inc(padded, 1)

                @block.scalar
                def _(act):
                    act.wait_ge(loaded, 6 * 16)
                    act.wait_ge(ready, START + 1)
                    nc.scalar.copy(recA.bitcast(I32)[:, :, 0], dst_sb)
                    nc.scalar.copy(recA[:, :, 2], wt_sb)
                    nc.scalar.copy(recC.bitcast(I32)[:, :, 0], src_sb)
                    nc.scalar.copy(recC[:, :, 2:6], attr_sb)
                    nc.scalar.copy(recD.bitcast(I32)[:, :, 0], from_sb).then_inc(recs, 1)

                @block.vector
                def _(dve):
                    dve.wait_ge(loaded, 6 * 16)
                    dve.wait_ge(ready, START + 1)
                    sort.dve(nc, dve)

                @block.tensor
                def _(pe):
                    pe.wait_ge(ready, START + 1)
                    sort.pe(nc, pe)

        def place_first(space):
            norm = Norm(space("norm"), sh, x0, normed=xn0)
            scat = Scatter(space("scat"), E1P, E1T, NC1, rowA, recA, listA, RA)
            with ExitStack() as psum:
                sortC = Sort(space("sortC"), sh, E1P, E1T, NC1, dst_sb, recC, rowC, cwC)
                deg = Degree(space("deg"), sh, sortC.win, recC[:, :, 1], dinv)
                sortD = Sort(space("sortD"), sh, P, E2T, NC2, to_sb, recD, rowD, cwD)
                with nc.Block() as block:
                    @block.sync
                    def _(sp):
                        norm.sp(nc, sp)
                        deg.sp(nc, sp)

                    @block.scalar
                    def _(act):
                        norm.act(nc, act)
                        deg.act(nc, act)

                    @block.gpsimd
                    def _(pool):
                        scat.pool(nc, pool, 0, scat.sets, True)
                        scat.pool_rest(nc, pool)

                    @block.vector
                    def _(dve):
                        norm.dve(nc, dve)
                        sortC.dve(nc, dve)
                        deg.dve(nc, dve)
                        sortD.dve(nc, dve)

                    @block.tensor
                    def _(pe):
                        sortC.pe(nc, pe)
                        deg.pe(nc, pe)
                        sortD.pe(nc, pe)

        def first_sums(space):
            sp_ = space("sums")
            edges = sp_.sb("edges", [P, NC1, RA])
            g = Gather(space("gather"), NC1, edges, RA, xn0, D)
            a = Aggregate(space("agg"), sh, g, edges, cwA, sh.agg, True)
            here, zeroed = sp_.sem("here", dma=True), sp_.sem("zeroed")
            with nc.Block() as block:
                @block.sync
                def _(sp):
                    sp.dma_start(edges.rearrange("p c w -> p (c w)"), lanes(listA)).then_inc(here, 16)

                @block.scalar
                def _(act):
                    act.wait_ge(here, 16)
                    hold(act)
                    with act.Fori(0, g.turns) as i:
                        for s in range(S):
                            g.act_set(nc, act, i, i, s)

                @block.gpsimd
                def _(pool):
                    with pool.Fori(0, g.turns) as i:
                        for s in range(S):
                            g.pool_set(nc, pool, i, s)

                @block.vector
                def _(dve):
                    nc.vector.memset(sh.agg, 0.0).then_inc(zeroed, 1)
                    dve.wait_ge(zeroed, START + 1)
                    dve.wait_ge(here, 16)
                    hold(dve)
                    a.dve(nc, dve, 0, False)

                @block.tensor
                def _(pe):
                    nc.tensor.sem_inc(g.used, AHEAD)
                    with pe.Fori(0, g.turns) as i:
                        for s in range(S):
                            a.pe_set(nc, pe, i, s, False)

        def first_add(space):
            add = AddTurned(space("add"), sh, xn0)
            with nc.Block() as block:
                @block.gpsimd
                def _(pool):
                    scatC.pool(nc, pool, 0, PARTS_C[0], True)

                @block.sync
                def _(sp):
                    add.sp(nc, sp)

                @block.tensor
                def _(pe):
                    add.pe(nc, pe)

                @block.vector
                def _(dve):
                    add.dve(nc, dve)

        def dense(space, ffn, pool_part=None, ones=None):
            with nc.Block() as block:
                @block.sync
                def _(sp):
                    ffn.sp_load(nc, sp)
                    ffn.sp(nc, sp)

                @block.scalar
                def _(act):
                    ffn.act(nc, act)

                @block.tensor
                def _(pe):
                    ffn.pe(nc, pe)

                @block.vector
                def _(dve):
                    if ones is not None:
                        tile, done = ones
                        nc.vector.memset(tile, 1.0).then_inc(done, 1)
                        dve.wait_ge(done, START + 1)
                    ffn.dve(nc, dve)

                if pool_part is not None:
                    @block.gpsimd
                    def _(pool):
                        pool_part(pool)

        def first_ffn(space):
            sp_ = space("one")
            share = sp_.sb("share", [P, NT, 1])
            one = lambda a: a.rearrange("(o k) m -> o k m", o=1)
            row = lambda a: a.rearrange("(o m) -> o m", o=1)
            ffn = Ffn(space("ffn"), sh, sh.agg, 1, 4, one(L0_gnn_W1), row(L0_gnn_b1), one(L0_gnn_W2), row(L0_gnn_b2),
                      ACT.Relu, share, x0, x1)
            dense(space, ffn, lambda pool: scatC.pool(nc, pool, sum(PARTS_C[:1]), PARTS_C[1], False),
                  (share, sp_.sem("done")))

        def first_mixture(space):
            sp_ = space("mix")
            share = sp_.sb("share", [P, NT, XB])
            with ExitStack() as part:
                space2 = lambda n: Space(nc, part, sp_.sems, "mix_" + n)
                q = space2("router")
                head, logits = q.sb("head", [P, FB, XB]), q.sb("logits", [P, NT, XB])
                norm = Norm(space2("norm"), sh, x1, both=both1, tok=sh.agg, head=head, head_out=logits)
                gate = Shares(space2("gate"), logits, XB, True, share)
                head_here, link, done = q.sem("head_here", dma=True), q.sem("link"), q.sem("done")
                with nc.Block() as block:
                    @block.sync
                    def _(sp):
                        for f in range(FB):
                            sp.dma_start(head[:, f, :], L0_ffn_router_w[:, f * P:(f + 1) * P].rearrange(
                                "e p -> p e"), allow_slow_non_contiguous=True).then_inc(head_here, 16)
                        norm.sp(nc, sp)

                    @block.scalar
                    def _(act):
                        norm.act(nc, act)
                        gate.act(nc, act)

                    @block.gpsimd
                    def _(pool):
                        scatC.pool(nc, pool, sum(PARTS_C[:2]), PARTS_C[2], False)

                    @block.tensor
                    def _(pe):
                        pe.wait_ge(head_here, 16 * FB)
                        norm.pe(nc, pe)

                    @block.vector
                    def _(dve):
                        norm.dve(nc, dve)
                        dve.wait_ge(norm.head_used, START + NG)
                        gate.dve(nc, dve, Chain(dve, link))
            ffn = Ffn(space("ffn"), sh, sh.agg, XB, 2, L0_ffn_w1, L0_ffn_b1, L0_ffn_w2, L0_ffn_b2, ACT.Gelu, share,
                      both1, x2)
            def rest_of_list(pool):
                scatC.pool(nc, pool, sum(PARTS_C[:3]), scatC.sets - sum(PARTS_C[:3]), False)
                scatC.pool_rest(nc, pool)
            dense(space, ffn, rest_of_list)

        def messages(space):
            sp_ = space("msg")
            edges = sp_.sb("edges", [P, NC1, RC])
            sh.dinv_row = sp_.sb("dinv_row", [P, NP])
            here = sp_.sem("here", dma=True)
            with ExitStack() as part:
                space2 = lambda n: Space(nc, part, sp_.sems, "msg_" + n)
                norm = Norm(space2("norm"), sh, x2, tok=sh.h)
                with nc.Block() as block:
                    @block.sync
                    def _(sp):
                        sp.dma_start(edges.rearrange("p c w -> p (c w)"), lanes(listC)).then_inc(here, 16)
                        sp.dma_start(sh.dinv_row, dinv.rearrange("t p -> (t p)").partition_broadcast(P)).then_inc(here, 16)
                        norm.sp(nc, sp)
                        sp.wait_ge(here, 32)

                    @block.scalar
                    def _(act):
                        norm.act(nc, act)

                    @block.tensor
                    def _(pe):
                        norm.pe(nc, pe)

                    @block.vector
                    def _(dve):
                        norm.dve(nc, dve)
            layers = Layers(space("layers"), sh, scatD, edges, cwC, nodesC, L1_gnn_mlp_w, L1_gnn_mlp_b, L1_gnn_ew1,
                            L1_gnn_ew2, L1_gnn_bn_g, L1_gnn_bn_b)
            with nc.Block() as block:
                @block.sync
                def _(sp):
                    layers.sp(nc, sp)

                @block.scalar
                def _(act):
                    layers.act(nc, act)

                @block.gpsimd
                def _(pool):
                    layers.pool(nc, pool)

                @block.tensor
                def _(pe):
                    layers.pe(nc, pe)

                @block.vector
                def _(dve):
                    layers.dve(nc, dve)

        def last_mixture(space):
            sp_ = space("gat")
            share = sp_.sb("share", [P, NT, XD])
            with ExitStack() as part:
                space2 = lambda n: Space(nc, part, sp_.sems, "gat_" + n)
                q = space2("in")
                h16, edges = q.sb("h16", [P, NT, HX]), q.sb("edges", [P, NC2 + SU, RD])
                here = q.sem("here", dma=True)
                with ExitStack() as part1:
                    space3 = lambda n: Space(nc, part1, sp_.sems, "gat_" + n)
                    head = space3("head").sb("w", [P, FB, HX])
                    norm = Norm(space3("norm"), sh, x2, tok=sh.h, head=head, head_out=h16, add=sh.h, summed=x3)
                    with nc.Block() as block:
                        @block.sync
                        def _(sp):
                            sp.dma_start(head, L1_ffn_W_gat.rearrange("(f p) m -> p f m", p=P)).then_inc(here, 16)
                            sp.dma_start(edges[:, 0:NC2, :].rearrange("p c w -> p (c w)"),
                                         lanes(listD)).then_inc(here, 16)
                            norm.sp(nc, sp)
                            sp.wait_ge(here, 32)

                        @block.gpsimd
                        def _(pool):
                            nc.gpsimd.memset(edges[:, NC2:NC2 + SU, :].bitcast(I32), N)

                        @block.scalar
                        def _(act):
                            norm.act(nc, act)

                        @block.tensor
                        def _(pe):
                            pe.wait_ge(here, 32)
                            norm.pe(nc, pe)

                        @block.vector
                        def _(dve):
                            norm.dve(nc, dve)
                att = Attention(space2("att"), sh, h16, nodesD, edges, cwD, share,
                                [L1_ffn_att_src.rearrange("h x -> (h x)"), L1_ffn_att_dst.rearrange("h x -> (h x)"),
                                 L1_ffn_b_gat, L1_ffn_ln_gamma, L1_ffn_ln_beta])
                with nc.Block() as block:
                    @block.sync
                    def _(sp):
                        att.sp(nc, sp)

                    @block.gpsimd
                    def _(pool):
                        att.pool(nc, pool)

                    @block.scalar
                    def _(act):
                        att.act(nc, act)

                    @block.tensor
                    def _(pe):
                        att.pe(nc, pe)

                    @block.vector
                    def _(dve):
                        att.dve(nc, dve)
            ffn = Ffn(space("ffn"), sh, sh.h, XD, 4, L1_ffn_W1, L1_ffn_b1, L1_ffn_W2, L1_ffn_b2, ACT.Gelu, share, x3,
                      out)
            dense(space, ffn)

        phases = [("p1", setup), ("p2", place_first), ("p3", first_sums), ("p4", first_add), ("p5", first_ffn),
                  ("p6", first_mixture), ("p7", messages), ("p8", last_mixture)]
        for name, build in phases[:last_phase]:
            phase(name, build)


_INS = ['x', 'src', 'dst', 'edge_attr_4', 'edge_weight', 'L0_gnn_W1', 'L0_gnn_b1', 'L0_gnn_W2', 'L0_gnn_b2',
        'L0_ffn_router_w', 'L0_ffn_w1', 'L0_ffn_b1', 'L0_ffn_w2', 'L0_ffn_b2', 'L1_gnn_mlp_w', 'L1_gnn_mlp_b',
        'L1_gnn_ew1', 'L1_gnn_ew2', 'L1_gnn_bn_g', 'L1_gnn_bn_b', 'L1_ffn_W_gat', 'L1_ffn_att_src', 'L1_ffn_att_dst',
        'L1_ffn_b_gat', 'L1_ffn_ln_gamma', 'L1_ffn_ln_beta', 'L1_ffn_W1', 'L1_ffn_b1', 'L1_ffn_W2', 'L1_ffn_b2',
        'L1_ffn_edge_index']


def kernel(**inputs):
    import numpy as _np
    import concourse.bacc as _bacc
    from concourse import mybir as _mybir
    from concourse.bass_utils import run_bass_kernel_spmd as _run

    nc = _bacc.Bacc("TRN2", target_bir_lowering=False, num_devices=1)
    arrays, args = {}, []
    for name in _INS:
        a = _np.ascontiguousarray(inputs[name])
        arrays[f"in_{name}_dram"] = a
        args.append(nc.dram_tensor(f"in_{name}_dram", a.shape, _mybir.dt.from_np(a.dtype), kind="ExternalInput").ap())
    out = nc.dram_tensor("out_0_dram", (N, D), F32, kind="ExternalOutput").ap()
    program(nc, *args, out)
    r = _run(nc, [arrays], core_ids=[0])
    return r.results[0]["out_0_dram"]
```

```python
from contextlib import ExitStack

import concourse.bass as bass
from concourse import mybir

F32 = mybir.dt.float32
I32 = mybir.dt.int32
BF16 = mybir.dt.bfloat16
ALU = mybir.AluOpType
ACT = mybir.ActivationFunctionType
AX = mybir.AxisListType
ds = bass.ds

P = 128
N, D = 6250, 256
NT = -(-N // P)
NP = NT * P
FB = D // P
E1 = 100000
E1P, E1T = 125, 800
E2 = 65536
E2T = E2 // P + NT
GT = 7
NG = NT // GT
GW = GT * P
HW = GW // 2
U = 4
S = 4
SU = S * U
AHEAD = SU - U
V = 8
LAYERS = 5
HEADS, XD = 4, 4
HX = HEADS * XD
XB = 8
LN_EPS = 1e-5
BN_EPS = 1e-5
BIG = 1e30
START = 1
TW = D + 4
AW = HEADS + HX


def chunks_of(edges):
    most = (edges + NT * (P - 1)) // P
    return -(-most // SU) * SU


NC1 = chunks_of(E1)
NC2 = chunks_of(E2 + NP)
PARTS_C = (4, 11, 6)
PART_D = 10
RA, RC, RD = 3, 6, 2


class Chain:

    def __init__(self, eng, sem, base=0):
        self.eng, self.sem, self.n = eng, sem, base

    def __call__(self, ins, wait=True):
        self.n = self.n + 1
        ins.then_inc(self.sem, 1)
        if wait:
            self.eng.wait_ge(self.sem, START + self.n)


def hold(eng):
    eng.nop(nofuse=True)


class Shared:
    pass


class Space:

    def __init__(self, nc, ctx, sems, name):
        self.nc, self.ctx, self.sems, self.name = nc, ctx, sems, name

    def sb(self, name, shape, dt=F32):
        return self.ctx.enter_context(self.nc.sbuf_tensor(f"{self.name}_{name}", shape, dt))[:]

    def ps(self, name, shape):
        return self.ctx.enter_context(self.nc.psum_tensor(f"{self.name}_{name}", shape, F32))[:]

    def sem(self, name, dma=False, pool_dma=False):
        handle = self.nc.alloc_semaphore(f"{self.name}_{name}")
        if not pool_dma:
            self.sems.append(handle)
        if not (dma or pool_dma):
            self.nc.sync.sem_inc(handle, START)
        return handle




class Sort:

    def __init__(self, sp, sh, parts, T, nchunks, key, rec, row, cw):
        self.sh, self.parts, self.T, self.nchunks = sh, parts, T, nchunks
        self.key, self.rec, self.row, self.cw = key, rec, row, cw
        self.win, self.pos = sp.sb("win", [parts, T]), sp.sb("pos", [parts, T])
        self.mask = [sp.sb(f"mask{j}", [parts, T]) for j in range(2)]
        self.rank = [sp.sb(f"rank{j}", [parts, T]) for j in range(2)]
        self.tmp_i, self.tmp_j = self.mask[1].bitcast(I32), self.rank[1].bitcast(I32)
        self.count, self.start = sp.sb("count", [parts, NT]), sp.sb("start", [P, NT])
        self.endcol, self.ends = sp.sb("endcol", [NT, 1]), sp.sb("ends", [P, NT + 1])
        self.len_i, self.len_j = sp.sb("len_i", [P, NT], I32), sp.sb("len_j", [P, NT], I32)
        self.len_f = sp.sb("len_f", [P, NT])
        self.after = sp.sb("after", [NT, nchunks])
        self.sums = sp.ps("sums", [P, 512])
        self.earlier, self.all = self.sums[:, 0:NT], self.sums[:, 64:64 + NT]
        self.endps = self.sums[0:NT, 128:129]
        self.cwps = sp.ps("cwps", [P, 1024])[0:1, :]
        self.counted, self.ends_done = sp.sem("counted"), sp.sem("ends_done")
        self.link, self.summed, self.turned = sp.sem("link"), sp.sem("summed"), sp.sem("turned")
        self.after_done, self.winsum, self.rows_done = sp.sem("after_done"), sp.sem("winsum"), sp.sem("rows_done")

    def dve(self, nc, dve):
        sh, parts = self.sh, self.parts
        link = Chain(dve, self.link)
        link(nc.vector.tensor_scalar(self.tmp_i, self.key, 7, None, ALU.arith_shift_right))
        link(nc.vector.tensor_copy(self.win, self.tmp_i))
        link(nc.vector.tensor_scalar(self.tmp_j, self.key, P - 1, None, ALU.bitwise_and))
        link(nc.vector.tensor_copy(self.rec[:, :, 1], self.tmp_j))
        link(nc.vector.memset(self.pos, 0.0))
        link(nc.vector.memset(self.ends[:, 0:1], 0.0))
        before = link.n

        def counted(w, j):
            dve.wait_ge(self.link, START + before + w - 1)
            nc.vector.tensor_scalar(self.mask[j], self.win, sh.wincol[0:parts, ds(w, 1)], 0.0, ALU.is_equal, ALU.add,
                                    accum_out=self.count[:, ds(w, 1)]).then_inc(self.link, 1)
        with dve.Fori(0, NT // 2) as i:
            for j in range(2):
                counted(i * 2 + j, j)
        counted(NT - 1, 0)
        dve.wait_ge(self.link, START + before + NT)
        nc.vector.sem_inc(self.counted, 1)
        dve.wait_ge(self.summed, START + 1)
        link = Chain(dve, self.link, before + NT)
        link(nc.vector.tensor_scalar(self.len_i, self.all, float(P - 1), None, ALU.add))
        link(nc.vector.tensor_scalar(self.len_j, self.len_i, 7, 7, ALU.arith_shift_right, ALU.arith_shift_left))
        link(nc.vector.tensor_copy(self.len_f, self.len_j))
        link(nc.vector.tensor_tensor_scan(self.ends[:, 1:NT + 1], sh.ones[:, 0:1].to_broadcast([P, NT]), self.len_f,
                                          self.ends[:, 0:1], ALU.mult, ALU.add))
        link(nc.vector.tensor_tensor(self.start, self.earlier, self.ends[:, 0:NT], ALU.add))
        nc.vector.sem_inc(self.ends_done, 1)
        before = link.n

        def placed(w, n):
            done = before + w * 3
            for j in range(n):
                dve.wait_ge(self.link, START + done - n + 1 + j)
                nc.vector.tensor_scalar(self.mask[j], self.win, sh.wincol[0:parts, ds(w + j, 1)], None,
                                        ALU.is_equal).then_inc(self.link, 1)
            for j in range(n):
                dve.wait_ge(self.link, START + done + 1 + j)
                hold(dve)
                nc.vector.tensor_tensor_scan(self.rank[j], sh.ones[0:parts, 0:1].to_broadcast([parts, self.T]),
                                             self.mask[j], self.start[0:parts, ds(w + j, 1)], ALU.mult,
                                             ALU.add).then_inc(self.link, 1)
            for j in range(n):
                dve.wait_ge(self.link, START + done + (2 * n + j if j else n + 1))
                hold(dve)
                nc.vector.copy_predicated(self.pos, self.mask[j].bitcast(I32), self.rank[j]).then_inc(self.link, 1)
        with dve.Fori(0, NT // 2) as i:
            placed(i * 2, 2)
        placed(NT - 1, 1)
        dve.wait_ge(self.link, START + before + NT * 3)
        link = Chain(dve, self.link, before + NT * 3)
        link(nc.vector.tensor_scalar(self.pos, self.pos, -1.0, None, ALU.add))
        link(nc.vector.tensor_copy(self.tmp_i, self.pos))
        link(nc.vector.tensor_scalar(self.tmp_j, self.tmp_i, P - 1, None, ALU.bitwise_and))
        link(nc.vector.tensor_copy(self.rank[0], self.tmp_j))
        link(nc.vector.tensor_scalar(self.tmp_j, self.tmp_i, 7, None, ALU.arith_shift_right))
        link(nc.vector.tensor_copy(self.pos, self.tmp_j))
        nc.vector.scalar_tensor_tensor(self.row, self.rank[0], float(self.nchunks), self.pos, ALU.mult,
                                       ALU.add).then_inc(self.rows_done, 1)
        dve.wait_ge(self.turned, START + 1)
        link(nc.vector.tensor_copy(self.endcol, self.endps))
        nc.vector.tensor_scalar(self.after, sh.chunkrow[0:NT, 0:self.nchunks], self.endcol[:, 0:1], None,
                                ALU.is_ge).then_inc(self.after_done, 1)
        for n, b in enumerate(range(0, self.nchunks, 512)):
            m = min(512, self.nchunks - b)
            dve.wait_ge(self.winsum, START + n + 1)
            nc.vector.tensor_scalar(self.cw[:, b:b + m], self.cwps[:, b:b + m], float(NT - 1), None,
                                    ALU.min).then_inc(self.rows_done, 1)

    def pe(self, nc, pe):
        sh, parts = self.sh, self.parts
        pe.wait_ge(self.counted, START + 1)
        nc.tensor.matmul(self.earlier, sh.below[0:parts, :], self.count, start=True, stop=True)
        nc.tensor.matmul(self.all, sh.ones[0:parts, :], self.count, start=True, stop=True).then_inc(self.summed, 1)
        pe.wait_ge(self.ends_done, START + 1)
        nc.tensor.matmul(self.endps, self.ends[0:1, 1:NT + 1], sh.ones[0:1, 0:1], start=True,
                         stop=True).then_inc(self.turned, 1)
        pe.wait_ge(self.after_done, START + 1)
        for b in range(0, self.nchunks, 512):
            m = min(512, self.nchunks - b)
            nc.tensor.matmul(self.cwps[:, b:b + m], sh.ones[0:NT, 0:1], self.after[:, b:b + m], start=True,
                             stop=True).then_inc(self.winsum, 1)


class Scatter:

    def __init__(self, sp, parts, T, nchunks, row, rec, table, words):
        self.parts, self.T, self.row, self.rec, self.table, self.words = parts, T, row, rec, table, words
        self.sets = T // (2 * V)
        self.rest = T - self.sets * 2 * V
        self.at = [sp.sb(f"at{h}", [P, V], I32) for h in range(2)]
        self.what = [sp.sb(f"what{h}", [P, V * words]) for h in range(2)]
        self.ready = sp.sem("ready")
        self.written = [sp.sem(f"written{h}", pool_dma=True) for h in range(2)]

    def pool(self, nc, pool, begin, count, first):
        if first:
            for h in range(2):
                self._send(nc, pool, h, h * V, V, h * 2 + 2)
        with pool.Fori(1 if first else 0, count) as i:
            for h in range(2):
                k = begin + i
                pool.wait_ge(self.written[h], k * (16 * V))
                self._send(nc, pool, h, (k * 2 + h) * V, V, k * 4 + (h * 2 + 2))

    def pool_rest(self, nc, pool):
        if self.rest:
            pool.wait_ge(self.written[0], self.sets * 16 * V)
            self._send(nc, pool, 0, self.sets * 2 * V, self.rest, self.sets * 4 + 2)
        pool.wait_ge(self.written[0], self.sets * 16 * V + 16 * self.rest)
        pool.wait_ge(self.written[1], self.sets * 16 * V)

    def _send(self, nc, pool, h, t, n, ready):
        p, w = self.parts, self.words
        flat = self.rec.rearrange("p t w -> p (t w)")
        nc.gpsimd.tensor_copy(self.at[h][0:p, 0:n], self.row[:, ds(t, n)]).then_inc(self.ready, 1)
        nc.gpsimd.tensor_copy(self.what[h][0:p, 0:n * w], flat[:, ds(t * w, n * w)]).then_inc(self.ready, 1)
        pool.wait_ge(self.ready, START + ready)
        hold(pool)
        for u in range(n):
            nc.gpsimd.indirect_dma_start(
                out=self.table, out_offset=bass.IndirectOffsetOnAxis(ap=self.at[h][0:p, u:u + 1], axis=0),
                in_=self.what[h][0:p, u * w:(u + 1) * w], in_offset=None).then_inc(self.written[h], 16)




def windows_of(nc, engine, cw, chunk, n):
    loads = [nc.values_load_multi_w_load_instructions(
        cw[0:1, ds(chunk + k, 4)], engines=[engine], min_val=0, max_val=NT - 1,
        skip_runtime_bounds_check_because="a count of windows, which Sort limits to NT - 1")[1]
        for k in range(0, n, 4)]
    return [w for four in loads for w in four]


class Gather:

    def __init__(self, sp, nchunks, edges, words, table, width, tracked=True, place=True):
        self.edges, self.words, self.table, self.width = edges, words, table, width
        self.turns = nchunks // SU
        self.idx = [sp.sb(f"idx{s}", [P, U], I32) for s in range(S)]
        self.rows = [sp.sb(f"rows{s}", [P, U, width]) for s in range(S)] if place else None
        self.ready = [sp.sem(f"ready{s}") for s in range(S)]
        self.here = [sp.sem(f"here{s}", pool_dma=True) for s in range(S)]
        self.used = sp.sem("used") if tracked else None

    def act_set(self, nc, act, it, i, s):
        act.wait_ge(self.used, START + it * SU + s * U)
        nodes = self.edges[:, ds(i * SU + s * U, U), 0].bitcast(I32)
        nc.scalar.copy(self.idx[s], nodes).then_inc(self.ready[s], 1)

    def pool_set(self, nc, pool, it, s):
        pool.wait_ge(self.ready[s], START + it + 1)
        hold(pool)
        for u in range(U):
            nc.gpsimd.indirect_dma_start(
                out=self.rows[s][:, u, :], out_offset=None, in_=self.table,
                in_offset=bass.IndirectOffsetOnAxis(ap=self.idx[s][:, u:u + 1], axis=0)).then_inc(self.here[s], 16)


class Aggregate:

    def __init__(self, sp, sh, g, edges, cw, agg, weighted, agge=None, place=True):
        self.sh, self.g, self.edges, self.cw, self.agg, self.weighted, self.agge = sh, g, edges, cw, agg, weighted, agge
        self.hot = [sp.sb(f"hot{s}", [P, U, P]) for s in range(S)] if place else None
        self.hot_ready = sp.sem("hot_ready")
        self.bank = [sp.ps(f"bank{u}", [P, 512]) for u in range(U)]
        self.added = [sp.sem(f"added{u}") for u in range(U)]
        if agge is not None:
            self.attr = [sp.sb(f"attr{s}", [P, U, 4]) for s in range(S)]
            self.edge_added = sp.sem("edge_added")

    def dve(self, nc, dve, it0, edge_terms):
        turns = self.g.turns

        def turn(i, last):
            for s in range(S):
                if s + 1 < S:
                    self._matrices(nc, dve, it0 + i, i, s + 1, edge_terms)
                elif not last:
                    self._matrices(nc, dve, it0 + i + 1, i + 1, 0, edge_terms)
                self._sums(nc, dve, it0 + i, i, s, edge_terms)

        self._matrices(nc, dve, it0, 0, 0, edge_terms)
        with dve.Fori(0, turns - 1) as i:
            turn(i, False)
        turn(turns - 1, True)

    def _matrices(self, nc, dve, it, i, s, edge_terms):
        dve.wait_ge(self.g.used, START + it * SU + s * U)
        hold(dve)
        for u in range(U):
            c = i * SU + s * U + u
            place = self.edges[:, ds(c, 1), 1]
            if self.weighted:
                ins = nc.vector.tensor_scalar(self.hot[s][:, u, :], self.sh.iota, place, self.edges[:, ds(c, 1), 2],
                                              ALU.is_equal, ALU.mult)
            else:
                ins = nc.vector.tensor_scalar(self.hot[s][:, u, :], self.sh.iota, place, None, ALU.is_equal)
        if edge_terms:
            dve.wait_ge(self.g.here[s], it * (16 * U) + 16 * U)
            ins = nc.vector.tensor_tensor(self.attr[s], self.edges[:, ds(i * SU + s * U, U), 2:6],
                                          self.g.rows[s][:, :, D:D + 1].to_broadcast([P, U, 4]), ALU.mult)
        ins.then_inc(self.hot_ready, 1)

    def _sums(self, nc, dve, it, i, s, edge_terms):
        for u, w in enumerate(windows_of(nc, mybir.EngineType.DVE, self.cw, i * SU + s * U, U)):
            dve.wait_ge(self.g.used, START + it * SU + (s * U + u + 1 + AHEAD))
            dve.wait_ge(self.added[(u - 1) % U], START + it * S + s + (u > 0))
            to = self.agg[:, :, ds(w * P, P)]
            prod = self.bank[u][:, 0:D].rearrange("p (f n) -> p f n", f=FB)
            nc.vector.tensor_tensor(to, to, prod, ALU.add).then_inc(self.added[u], 1)
            if edge_terms:
                dve.wait_ge(self.edge_added, START + it * SU + (s * U + u + U))
                te = self.agge[:, ds(w * P, P)]
                nc.vector.tensor_tensor(te, te, self.bank[u][0:4, D:D + P], ALU.add).then_inc(self.edge_added, 1)

    def pe_set(self, nc, pe, it, s, edge_terms):
        pe.wait_ge(self.hot_ready, START + it * S + (s + 1))
        pe.wait_ge(self.g.here[s], it * (16 * U) + 16 * U)
        for u in range(U):
            pe.wait_ge(self.added[u], START + it * S + s)
            if edge_terms:
                pe.wait_ge(self.edge_added, START + it * SU + (s * U + u + 1))
            for f in range(FB):
                ins = nc.tensor.matmul(self.bank[u][:, f * P:(f + 1) * P], self.g.rows[s][:, u, f * P:(f + 1) * P],
                                       self.hot[s][:, u, :], start=True, stop=True)
            if edge_terms:
                ins = nc.tensor.matmul(self.bank[u][0:4, D:D + P], self.attr[s][:, u, :], self.hot[s][:, u, :],
                                       start=True, stop=True)
            ins.then_inc(self.g.used, 1)




def group_rows(table, g):
    return table[ds(g * GW, GW), :].rearrange("(t p) d -> p t d", p=P)


class Ffn:

    def __init__(self, sp, sh, tok, E, HB, w1, b1, w2, b2, func, share, base, out):
        self.sh, self.tok, self.E, self.HB, self.func, self.share = sh, tok, E, HB, func, share
        self.base, self.out = base, out
        self.d = (w1, b1, w2, b2)
        self.w1, self.b1 = sp.sb("w1", [P, E, FB, HB * P]), sp.sb("b1", [P, E * HB])
        self.w2, self.b2 = sp.sb("w2", [P, E * HB, D]), sp.sb("b2", [P, E, D])
        self.nh = min(2, E)
        self.hid = [sp.sb(f"hid{j}", [P, HB, GW]) for j in range(self.nh)]
        self.acc = sp.sb("acc", [P, GT, D])
        self.pre = [sp.ps(f"pre{j}", [P, 2, 512]) for j in range(2)]
        self.y = [sp.ps(f"y{j}", [P, 512]) for j in range(4)]
        self.loaded = [sp.sem(f"loaded{e}", dma=True) for e in range(E)]
        self.pre_done = sp.sem("pre_done")
        self.act_done = [sp.sem(f"act_done{j}") for j in range(2)]
        self.y_done = sp.sem("y_done")
        self.y_used = [sp.sem(f"y_used{j}") for j in range(4)]
        self.base_here, self.link, self.stored = sp.sem("base_here", dma=True), sp.sem("link"), sp.sem("stored")

    def sp_load(self, nc, sp):
        w1, b1, w2, b2 = self.d
        sp.dma_start(self.b1, b1.rearrange("e (b p) -> p (e b)", p=P),
                     allow_slow_non_contiguous=True).then_inc(self.loaded[0], 16)
        sp.dma_start(self.b2, b2.partition_broadcast(P)).then_inc(self.loaded[0], 16)
        for e in range(self.E):
            sp.dma_start(self.w1[:, e], w1[e].rearrange("(f p) h -> p f h", p=P)).then_inc(self.loaded[e], 16)
            sp.dma_start(self.w2[:, e * self.HB:(e + 1) * self.HB],
                         w2[e].rearrange("(b p) d -> p b d", p=P)).then_inc(self.loaded[e], 16)

    FIRST, OTHER = 4 * 16, 2 * 16

    def sp(self, nc, sp):
        def group(g):
            sp.wait_ge(self.stored, START + g * 16)
            hold(sp)
            sp.dma_start(self.acc, group_rows(self.base, g)).then_inc(self.base_here, 16)
            for j in range(4):
                sp.wait_ge(self.y_used[j], START + (g + 1) * (self.E * len(range(j, GT, 4))))
                hold(sp)

        with sp.Fori(0, NG - 1) as g:
            group(g)
            sp.dma_start(group_rows(self.out, g), self.acc).then_inc(self.stored, 16)
        group(NG - 1)
        rows = self.out.shape[0] - (NG - 1) * GW
        whole, rest = rows // P, rows % P
        at = (NG - 1) * GW
        sp.dma_start(self.out[at:at + whole * P, :].rearrange("(t p) d -> p t d", p=P),
                     self.acc[:, 0:whole, :]).then_inc(self.stored, 16)
        if rest:
            sp.dma_start(self.out[at + whole * P:at + rows, :], self.acc[0:rest, whole, :]).then_inc(self.stored, 16)
        sp.wait_ge(self.stored, START + NG * 16 + (16 if rest else 0))

    def pe(self, nc, pe):
        E, HB = self.E, self.HB

        def up(g, e):
            pe.wait_ge(self.loaded[e], self.OTHER if e else self.FIRST)
            for b in range(HB):
                j = b % 2
                pe.wait_ge(self.act_done[j], START + (g * E + e) * (HB // 2) + b // 2)
                for m in range(2):
                    for f in range(FB):
                        ins = nc.tensor.matmul(self.pre[j][:, m, 0:HW], self.w1[:, e, f, b * P:(b + 1) * P],
                                               self.tok[:, f, ds(g * GW + m * HW, HW)], start=(f == 0),
                                               stop=(f == FB - 1))
                ins.then_inc(self.pre_done, 1)

        def down(g, e):
            for j in range(2):
                pe.wait_ge(self.act_done[j], START + (g * E + e + 1) * (HB // 2))
            for s in range(GT):
                j = s % 4
                n = len(range(j, GT, 4))
                pe.wait_ge(self.y_used[j], START + (g * E + e) * n + s // 4)
                for b in range(HB):
                    ins = nc.tensor.matmul(self.y[j][:, 0:D], self.hid[e % self.nh][:, b, s * P:(s + 1) * P],
                                           self.w2[:, e * HB + b, :], start=(b == 0), stop=(b == HB - 1))
                ins.then_inc(self.y_done, 1)

        nc.tensor.sem_inc(self.y_done, self.nh * GT)
        with pe.Fori(0, NG) as g:
            up(g, 0)
            for e in range(E):
                if e + 1 < E:
                    up(g, e + 1)
                down(g, e)

    def act(self, nc, act):
        E, HB, nh = self.E, self.HB, self.nh
        act.wait_ge(self.loaded[0], self.FIRST)
        hold(act)
        with act.Fori(0, NG) as g:
            for e in range(E):
                act.wait_ge(self.y_done, START + (g * E + e + 1) * GT)
                for b in range(HB):
                    act.wait_ge(self.pre_done, START + (g * E + e) * HB + b + 1)
                    nc.scalar.activation(self.hid[e % nh][:, b, :].rearrange("p (m n) -> p m n", m=2),
                                         self.pre[b % 2][:, :, 0:HW], self.func,
                                         bias=self.b1[:, e * HB + b:e * HB + b + 1]).then_inc(self.act_done[b % 2], 1)

    def dve(self, nc, dve):
        E = self.E
        dve.wait_ge(self.loaded[0], self.FIRST)
        hold(dve)
        with dve.Fori(0, NG) as g:
            dve.wait_ge(self.base_here, (g + 1) * 16)
            for e in range(E):
                for s in range(GT):
                    j = s % 4
                    n = len(range(j, GT, 4))
                    share = self.share[:, ds(g * GT + s, 1), e]
                    a = self.acc[:, s, :]
                    dve.wait_ge(self.y_used[j], START + (g * E + e) * n + s // 4)
                    nc.vector.scalar_tensor_tensor(a, self.b2[:, e, :], share, a, ALU.mult,
                                                   ALU.add).then_inc(self.link, 1)
                    dve.wait_ge(self.link, START + (g * E + e) * GT + s + 1)
                    dve.wait_ge(self.y_done, START + (g * E + e + self.nh) * GT + s + 1)
                    nc.vector.scalar_tensor_tensor(a, self.y[j][:, 0:D], share, a, ALU.mult,
                                                   ALU.add).then_inc(self.y_used[j], 1)


class Norm:

    def __init__(self, sp, sh, src, normed=None, both=None, tok=None, head=None, head_out=None, add=None,
                 summed=None, depth=2):
        self.sh, self.src, self.normed, self.both, self.tok = sh, src, normed, both, tok
        self.head, self.head_out, self.add, self.summed = head, head_out, add, summed
        self.depth = depth
        self.x, self.xn = [sp.sb(f"x{j}", [P, GT, D]) for j in range(depth)], sp.sb("xn", [P, GT, D])
        self.sum = sp.sb("sum", [P, GT, D]) if both is not None else None
        self.stats, self.mv, self.rstd = sp.sb("stats", [P, GT, 6]), sp.sb("mv", [P, GT, 2]), sp.sb("rstd", [P, GT])
        if tok is not None:
            self.turn = [sp.ps(f"turn{j}", [P, 512]) for j in range(4)]
        self.here = [sp.sem(f"here{j}", dma=True) for j in range(depth)]
        self.link, self.stored = sp.sem("link"), sp.sem("stored")
        self.var_done, self.root_done = sp.sem("var_done"), sp.sem("root_done")
        self.turned, self.xn_done, self.out_done = sp.sem("turned"), sp.sem("xn_done"), sp.sem("out_done")
        self.stores = (normed is not None) + (both is not None) + (summed is not None)
        if tok is not None:
            self.slot = sp.sb("slot", [P, GT, D])
            self.copied = [sp.sem(f"copied{j}") for j in range(2)]
            self.slotted = sp.sem("slotted")
        if head is not None:
            self.M = head_out.shape[2]
            self.prod = sp.ps("prod", [P, 512])
            self.head_done, self.head_used = sp.sem("head_done"), sp.sem("head_used")
        if add is not None:
            self.raw = sp.sb("raw", [P, FB, GW])
            self.applied = sp.sem("applied")
            self.added = [sp.sem(f"added{j}") for j in range(2)]
            self.add_turned = sp.sem("add_turned")

    def groups(self, eng, group):
        with eng.Fori(0, NG // 2) as i:
            for j in range(2):
                group(i * 2 + j, j, i, False)
        group(NG - 1, 0, NG // 2, True)

    def sp(self, nc, sp):
        def load(g, j):
            sp.dma_start(self.x[j % self.depth], group_rows(self.src, g)).then_inc(self.here[j % self.depth], 16)

        def load_next(g, j):
            done = g + (2 - self.depth)
            sp.wait_ge(self.stored, START + done * (16 * self.stores))
            hold(sp)
            sp.wait_ge(self.out_done, START + done)
            hold(sp)
            load(g + 1, j + 1)

        def store(g, j):
            if self.summed is not None:
                sp.wait_ge(self.added[0], START + (g + 1) * 4)
                hold(sp)
                sp.wait_ge(self.added[1], START + (g + 1) * 3)
                hold(sp)
                sp.dma_start(group_rows(self.summed, g), self.x[j % self.depth]).then_inc(self.stored, 16)
            sp.wait_ge(self.out_done, START + g + 1)
            hold(sp)
            if self.normed is not None:
                sp.dma_start(group_rows(self.normed, g), self.xn).then_inc(self.stored, 16)
            if self.both is not None:
                sp.dma_start(group_rows(self.both, g), self.sum).then_inc(self.stored, 16)

        def group(g, j, i, last):
            if self.depth == 2 and not last:
                load_next(g, j)
            store(g, j)
            if self.depth == 1 and not last:
                load_next(g, j)
        load(0, 0)
        self.groups(sp, group)
        sp.wait_ge(self.stored, START + NG * 16 * self.stores)

    PER = 3

    def dve(self, nc, dve):
        def group(g, j, i, last):
            x = self.x[j % self.depth]
            link = Chain(dve, self.link, g * self.PER)
            dve.wait_ge(self.here[j % self.depth], (i if self.depth == 2 else g) * 16 + 16)
            if self.add is not None:
                for t in range(GT):
                    dve.wait_ge(self.add_turned, START + g * GT + t + 1)
                    nc.vector.tensor_tensor(x[:, t, :], x[:, t, :], self.turn[t % 2][:, 0:D],
                                            ALU.add).then_inc(self.added[t % 2], 1)
                dve.wait_ge(self.added[0], START + (g + 1) * 4)
                dve.wait_ge(self.added[1], START + (g + 1) * 3)
            for t in range(GT):
                ins = nc.vector.bn_stats(self.stats[:, t, :], x[:, t, :])
            link(ins)
            hold(dve)
            for t in range(GT):
                ins = nc.vector.bn_aggr(self.mv[:, t, :], self.stats[:, t, :])
            link(ins)
            nc.vector.tensor_scalar(self.rstd, self.mv[:, :, 1], LN_EPS, None, ALU.add).then_inc(self.var_done, 1)
            dve.wait_ge(self.root_done, START + g + 1)
            link(nc.vector.reciprocal(self.rstd, self.rstd))
            if self.normed is not None or self.both is not None:
                dve.wait_ge(self.stored, START + g * (16 * self.stores))
            if self.tok is not None:
                dve.wait_ge(self.turned, START + g * GT)
            for t in range(GT):
                ins = nc.vector.tensor_scalar(self.xn[:, t, :], x[:, t, :], self.mv[:, t, 0:1],
                                              self.rstd[:, t:t + 1], ALU.subtract, ALU.mult)
                ins.then_inc(self.xn_done, 1)
            dve.wait_ge(self.xn_done, START + (g + 1) * GT)
            if self.both is not None:
                nc.vector.tensor_tensor(self.sum, x, self.xn, ALU.add).then_inc(self.out_done, 1)
            else:
                nc.vector.sem_inc(self.out_done, 1)
            if self.head is not None:
                dve.wait_ge(self.head_done, START + (g + 1) * GT)
                nc.vector.tensor_copy(self.head_out[:, ds(g * GT, GT), :],
                                      self.prod[:, 0:GT * 64].rearrange("p (t m) -> p t m", t=GT)[:, :, 0:self.M]
                                      ).then_inc(self.head_used, 1)
        self.groups(dve, group)

    def pe(self, nc, pe):
        if self.add is None and self.tok is None:
            return
        with pe.Fori(0, NG) as g:
            if self.add is not None:
                pe.wait_ge(self.applied, START + g + 1)
                for t in range(GT):
                    j = t % 2
                    pe.wait_ge(self.added[j], START + g * (4 - j) + t // 2)
                    for f in range(FB):
                        ins = nc.tensor.transpose(self.turn[j][:, f * P:(f + 1) * P],
                                                  self.raw[:, f, t * P:(t + 1) * P], self.sh.ident)
                    ins.then_inc(self.add_turned, 1)

            def head(t):
                pe.wait_ge(self.slotted, START + g * GT + t + 1)
                if t == 0:
                    pe.wait_ge(self.head_used, START + g)
                for f in range(FB):
                    ins = nc.tensor.matmul(self.prod[:, t * 64:t * 64 + self.M], self.slot[:, t, f * P:(f + 1) * P],
                                           self.head[:, f, :], start=(f == 0), stop=(f == FB - 1))
                ins.then_inc(self.head_done, 1)

            for t in range(GT):
                j = t % 2
                pe.wait_ge(self.xn_done, START + g * GT + t + 1)
                pe.wait_ge(self.copied[j], START + g * (4 - j) + t // 2)
                for f in range(FB):
                    ins = nc.tensor.transpose(self.turn[2 + j][:, f * P:(f + 1) * P],
                                              self.xn[:, t, f * P:(f + 1) * P], self.sh.ident)
                ins.then_inc(self.turned, 1)
                if self.head is not None and t:
                    head(t - 1)
            if self.head is not None:
                head(GT - 1)

    def act(self, nc, act):
        with act.Fori(0, NG) as g:
            if self.add is not None:
                act.wait_ge(self.add_turned, START + g * GT)
                for f in range(FB):
                    ins = nc.scalar.activation(self.raw[:, f, :], self.add[:, f, ds(g * GW, GW)], ACT.Identity,
                                               bias=self.sh.shift[:, f:f + 1], scale=self.sh.scale[:, f:f + 1])
                ins.then_inc(self.applied, 1)
            act.wait_ge(self.var_done, START + g + 1)
            nc.scalar.activation(self.rstd, self.rstd, ACT.Sqrt).then_inc(self.root_done, 1)
            for t in range(GT if self.tok is not None else 0):
                j = t % 2
                act.wait_ge(self.turned, START + g * GT + t + 1)
                if self.head is not None:
                    act.wait_ge(self.head_done, START + g * GT)
                    nc.scalar.copy(self.slot[:, t, :], self.turn[2 + j][:, 0:D]).then_inc(self.slotted, 1)
                nc.scalar.copy(self.tok[:, :, ds((g * GT + t) * P, P)],
                               self.turn[2 + j][:, 0:D].rearrange("p (f n) -> p f n", f=FB)).then_inc(self.copied[j], 1)


class Degree:

    COLS = 16

    def __init__(self, sp, sh, win, place, out):
        self.sh, self.win, self.place, self.out = sh, win, place, out
        self.pairs = E1T // (2 * self.COLS)
        bf = mybir.dt.bfloat16
        self.in_win = [sp.sb(f"in_win{j}", [E1P, self.COLS, NT], bf) for j in range(2)]
        self.in_place = [sp.sb(f"in_place{j}", [E1P, self.COLS, P], bf) for j in range(2)]
        self.low, self.dinv = sp.sb("low", [NT, P]), sp.sb("dinv", [NT, P])
        bank = sp.ps("bank", [P, 512])
        self.deg, self.col = bank[0:NT, 0:P], bank[:, P:P + NT]
        self.made, self.link = sp.sem("made"), sp.sem("link")
        self.counted = sp.sem("counted")
        self.some_done, self.root_done = sp.sem("some_done"), sp.sem("root_done")
        self.dinv_done, self.turned = sp.sem("dinv_done"), sp.sem("turned")
        self.stored = sp.sem("stored", dma=True)

    def dve(self, nc, dve):
        sh, n = self.sh, self.COLS
        with dve.Fori(0, self.pairs) as i:
            for j in range(2):
                t = i * (2 * n) + j * n
                dve.wait_ge(self.counted, START + i * 2 + (j + 1))
                hold(dve)
                for to, numbers, of in ((self.in_win[j], sh.wincol, self.win), (self.in_place[j], sh.iota, self.place)):
                    m = to.shape[2]
                    ins = nc.vector.tensor_tensor(
                        to, numbers[0:E1P, :].rearrange("p (o m) -> p o m", o=1).to_broadcast([E1P, n, m]),
                        of[:, ds(t, n)].rearrange("p (t o) -> p t o", o=1).to_broadcast([E1P, n, m]), ALU.is_equal)
                ins.then_inc(self.made, 1)
        dve.wait_ge(self.counted, START + self.pairs * 2 + 2)
        link = Chain(dve, self.link)
        link(nc.vector.tensor_scalar(self.low, self.deg, 1.0, None, ALU.min))
        nc.vector.tensor_scalar(self.dinv, self.deg, 1.0, None, ALU.max).then_inc(self.some_done, 1)
        dve.wait_ge(self.root_done, START + 1)
        link(nc.vector.reciprocal(self.dinv, self.dinv))
        nc.vector.tensor_tensor(self.dinv, self.dinv, self.low, ALU.mult).then_inc(self.dinv_done, 1)
        dve.wait_ge(self.turned, START + 1)
        link(nc.vector.tensor_copy(sh.dinv_col, self.col))

    def pe(self, nc, pe):
        n = self.COLS
        nc.tensor.sem_inc(self.counted, 2)

        def pair(i, first, last):
            for j in range(2):
                pe.wait_ge(self.made, START + i * 2 + (j + 1))
                for c in range(n):
                    ins = nc.tensor.matmul(self.deg, self.in_win[j][:, c, :], self.in_place[j][:, c, :],
                                           start=first and j == 0 and c == 0, stop=last and j == 1 and c == n - 1)
                ins.then_inc(self.counted, 1)
        pair(0, True, False)
        with pe.Fori(1, self.pairs - 1) as i:
            pair(i, False, False)
        pair(self.pairs - 1, False, True)
        pe.wait_ge(self.dinv_done, START + 1)
        nc.tensor.transpose(self.col, self.dinv, self.sh.ident[0:NT, 0:NT]).then_inc(self.turned, 1)

    def act(self, nc, act):
        act.wait_ge(self.some_done, START + 1)
        nc.scalar.activation(self.dinv, self.dinv, ACT.Sqrt).then_inc(self.root_done, 1)

    def sp(self, nc, sp):
        sp.wait_ge(self.dinv_done, START + 1)
        sp.dma_start(self.out, self.dinv).then_inc(self.stored, 16)
        sp.wait_ge(self.stored, 16)


class Layers:

    TILES = NP // HW
    LAST = N - (NP // HW - 1) * HW

    def __init__(self, sp, sh, scat, edges, cw, table, mlp_w, mlp_b, ew1, ew2, bn_g, bn_b):
        self.sh, self.scat, self.d, self.table = sh, scat, (mlp_w, mlp_b, ew1, ew2, bn_g, bn_b), table
        self.g = Gather(sp, NC1, edges, RC, table, TW, place=False)
        self.agge = sh.agge
        self.a = Aggregate(sp, sh, self.g, edges, cw, sh.agg, False, self.agge, place=False)
        both = FB * GW
        place = sp.sb("place", [P, S * U * TW])
        self.g.rows = [place[:, s * U * TW:(s + 1) * U * TW].rearrange("p (u w) -> p u w", u=U) for s in range(S)]
        by_block = lambda a: a.rearrange("p (f n) -> p f n", f=FB)
        self.slot = [by_block(place[:, j * both:(j + 1) * both]) for j in range(2)]
        self.full = [by_block(place[:, j * both // 2:(j + 1) * both // 2]) for j in range(2)]
        hots = sp.sb("hots", [P, S * U * P])
        self.a.hot = [hots[:, s * U * P:(s + 1) * U * P].rearrange("p (u n) -> p u n", u=U) for s in range(S)]
        self.rows = hots[:, 0:GT * TW].rearrange("p (t w) -> p t w", t=GT)
        self.w, self.ew = sp.sb("w", [P, 2 * FB, D]), sp.sb("ew", [4, D])
        self.b, self.bn_g, self.bn_b = (sp.sb(n, [P, LAYERS * FB]) for n in ("b", "bn_g", "bn_b"))
        self.stats, self.mv = sp.sb("stats", [P, FB, self.TILES, 6]), sp.sb("mv", [P, FB, 2])
        self.rstd, self.part = sp.sb("rstd", [P, FB]), sp.sb("part", [P, FB])
        self.turn = [sp.ps(f"turn{j}", [P, 512]) for j in range(2)]
        self.edge = sp.ps("edge", [P, 2, 512])
        self.link, self.var_done, self.root_done = sp.sem("link"), sp.sem("var_done"), sp.sem("root_done")
        self.loaded, self.w_here = sp.sem("loaded", dma=True), sp.sem("w_here", dma=True)
        self.normed, self.back = sp.sem("normed"), sp.sem("back")
        self.turned = sp.sem("turned")
        self.row_done = [sp.sem(f"row_done{j}") for j in range(2)]
        self.stored, self.zeroed = [sp.sem(f"stored{n}") for n in range(2)], sp.sem("zeroed")
        self.edge_done, self.edge_used, self.full_done = sp.sem("edge_done"), sp.sem("edge_used"), sp.sem("full_done")
        self.mixed, self.joined = sp.sem("mixed"), sp.sem("joined")
        self.own_done, self.own_kept, self.relu_done = sp.sem("own_done"), sp.sem("own_kept"), sp.sem("relu_done")
        self.bn_ready = sp.sem("bn_ready")

    def each(self, eng, layer):
        layer(0, True)
        with eng.Fori(1, LAYERS) as l:
            layer(l, False)

    def groups(self, eng, group):
        with eng.Fori(0, NG // 2) as i:
            for j in range(2):
                group(i * 2 + j, j)
        group(NG - 1, 0)

    def sp(self, nc, sp):
        mlp_w, mlp_b, ew1, ew2, bn_g, bn_b = self.d
        for to, src in ((self.b, mlp_b), (self.bn_g, bn_g), (self.bn_b, bn_b)):
            sp.dma_start(to, src.rearrange("l (f p) -> p (l f)", p=P),
                         allow_slow_non_contiguous=True).then_inc(self.loaded, 16)

        def layer(l, first):
            sp.wait_ge(self.bn_ready, START + l + 1)
            hold(sp)
            sp.dma_start(self.w, mlp_w[ds(l, 1)].rearrange("l (k p) d -> p (l k) d", p=P)).then_inc(self.w_here, 16)
            sp.dma_start(self.ew[3:4, 0:P], ew1[ds(l, 1)].rearrange("l k d -> (l k) d")).then_inc(self.w_here, 16)
            sp.dma_start(self.ew[0:3, P:D], ew2[ds(l, 1)].rearrange("l k d -> (l k) d")).then_inc(self.w_here, 16)
            with sp.Fori(0, NG) as g:
                it = l * NG + g
                for n, (t0, t1) in enumerate(self.PARTS):
                    for j in range(2):
                        sp.wait_ge(self.row_done[j], START + it * (4 - j) + (t1 + 1 - j) // 2)
                        hold(sp)
                    sp.dma_start(group_rows(self.table, g)[:, t0:t1, :],
                                 self.rows[:, t0:t1, :]).then_inc(self.stored[n], 16)
        self.each(sp, layer)

    PARTS = ((0, GT // 2 + 1), (GT // 2 + 1, GT))

    def act(self, nc, act):
        sh = self.sh
        act.wait_ge(self.loaded, 48)

        def layer(l, first):
            act.wait_ge(self.bn_ready, START + l + 1)
            hold(act)

            def group(g, j):
                it = l * NG + g
                func = ACT.Identity if first else ACT.Relu
                act.wait_ge(self.turned, START + it * GT)
                hold(act)
                for f in range(FB):
                    ins = nc.scalar.activation(self.slot[j][:, f, :], sh.h[:, f, ds(g * GW, GW)], func,
                                               bias=sh.shift[:, f:f + 1], scale=sh.scale[:, f:f + 1])
                ins.then_inc(self.normed, 1)
                if not first:
                    for f in range(FB):
                        here = sh.h[:, f, ds(g * GW, GW)]
                        ins = nc.scalar.activation(here, here, func, bias=sh.shift[:, f:f + 1],
                                                   scale=sh.scale[:, f:f + 1])
                    ins.then_inc(self.back, 1)
            self.groups(act, group)

            def nodes(i):
                for s in range(S):
                    self.g.act_set(nc, act, l * self.g.turns + i, i, s)

            def keep_own(m):
                act.wait_ge(self.own_done, START + l * self.TILES + m + 1)
                hold(act)
                for o in range(FB):
                    ins = nc.scalar.activation(sh.h[:, o, ds(m * HW, HW)], self.turn[o][:, 0:HW], ACT.Identity,
                                               bias=self.b[:, ds(l * FB + o, 1)])
                ins.then_inc(self.own_kept, 1)
            nodes(0)
            with act.Fori(1, self.TILES + 1) as i:
                nodes(i)
                keep_own(i - 1)
            with act.Fori(self.TILES + 1, self.g.turns) as i:
                nodes(i)
            with act.Fori(0, self.TILES) as m:
                act.wait_ge(self.joined, START + l * self.TILES + m + 2)
                hold(act)
                here = sh.h[:, :, ds(m * HW, HW)]
                nc.scalar.activation(here, here, ACT.Relu).then_inc(self.relu_done, 1)
            act.wait_ge(self.var_done, START + l + 1)
            nc.scalar.activation(self.rstd, self.rstd, ACT.Sqrt).then_inc(self.root_done, 1)
        self.each(act, layer)

    def pool(self, nc, pool):
        def layer(l, first):
            if first:
                nc.gpsimd.memset(self.agge, 0.0).then_inc(self.zeroed, 1)
            else:
                pool.wait_ge(self.full_done, START + l * self.TILES)
            hold(pool)
            nc.gpsimd.memset(self.sh.agg, 0.0).then_inc(self.zeroed, 1)
            for n in range(2):
                pool.wait_ge(self.stored[n], START + (l + 1) * (NG * 16))
                hold(pool)
            with pool.Fori(0, self.g.turns) as i:
                for s in range(S):
                    self.g.pool_set(nc, pool, l * self.g.turns + i, s)
            per = (self.scat.sets - PART_D) // LAYERS
            self.scat.pool(nc, pool, l * per + PART_D, per, False)
        self.each(pool, layer)
        done = PART_D + LAYERS * ((self.scat.sets - PART_D) // LAYERS)
        if done < self.scat.sets:
            self.scat.pool(nc, pool, done, self.scat.sets - done, False)
        self.scat.pool_rest(nc, pool)

    def pe(self, nc, pe):
        sh = self.sh
        nc.tensor.sem_inc(self.g.used, AHEAD)
        nc.tensor.sem_inc(self.a.edge_added, U)
        nc.tensor.sem_inc(self.turned, GT)
        nc.tensor.sem_inc(self.mixed, 1)
        nc.tensor.sem_inc(self.joined, 1)

        def layer(l, first):
            def group(g, j):
                it = l * NG + g
                pe.wait_ge(self.normed, START + it + 1)
                for t in range(GT):
                    b = t % 2
                    pe.wait_ge(self.row_done[b], START + it * (4 - b) + t // 2)
                    for f in range(FB):
                        ins = nc.tensor.transpose(self.turn[b][:, f * P:(f + 1) * P],
                                                  self.slot[j][:, f, t * P:(t + 1) * P], sh.ident)
                    ins.then_inc(self.turned, 1)
            self.groups(pe, group)
            if not first:
                pe.wait_ge(self.joined, START + l * self.TILES + 1)
                pe.wait_ge(self.back, START + l * NG)
            hold(pe)
            for b in range(2):
                pe.wait_ge(self.row_done[b], START + (l + 1) * (NG * (4 - b)))
            pe.wait_ge(self.w_here, (l + 1) * 48)
            hold(pe)

            def own(m):
                pe.wait_ge(self.own_kept, START + l * self.TILES + m)
                hold(pe)
                for o in range(FB):
                    for kk in range(FB):
                        ins = nc.tensor.matmul(self.turn[o][:, 0:HW], self.w[:, kk, o * P:(o + 1) * P],
                                               sh.h[:, kk, ds(m * HW, HW)], start=(kk == 0), stop=(kk == FB - 1))
                ins.then_inc(self.own_done, 1)
            with pe.Fori(0, self.TILES) as i:
                for s in range(S):
                    self.a.pe_set(nc, pe, l * self.g.turns + i, s, first)
                own(i)
            with pe.Fori(self.TILES, self.g.turns) as i:
                for s in range(S):
                    self.a.pe_set(nc, pe, l * self.g.turns + i, s, first)
            if first:
                pe.wait_ge(self.a.edge_added, START + NC1 + U)
            for b in range(U):
                pe.wait_ge(self.a.added[b], START + (l + 1) * (NC1 // U))
            hold(pe)

            def edge(m):
                it = l * self.TILES + m
                pe.wait_ge(self.edge_used, START + it)
                for f in range(FB):
                    ins = nc.tensor.matmul(self.edge[:, f, 0:HW], self.ew[:, f * P:(f + 1) * P],
                                           self.agge[:, ds(m * HW, HW)], start=True, stop=True)
                ins.then_inc(self.edge_done, 1)

            def mix(m, j):
                it = l * self.TILES + m
                pe.wait_ge(self.full_done, START + it + 1)
                pe.wait_ge(self.joined, START + it)
                for o in range(FB):
                    for f in range(FB):
                        ins = nc.tensor.matmul(self.a.bank[2 * j + o][:, 0:HW], self.w[:, FB + f, o * P:(o + 1) * P],
                                               self.full[j][:, f, :], start=(f == 0), stop=(f == FB - 1))
                ins.then_inc(self.mixed, 1)
            edge(0)
            with pe.Fori(0, self.TILES // 2 - 1) as m2:
                for j in range(2):
                    edge(m2 * 2 + (j + 1))
                    mix(m2 * 2 + j, j)
            edge(self.TILES - 1)
            for j in range(2):
                mix(self.TILES - 2 + j, j)
        self.each(pe, layer)

    PER = 5

    def dve(self, nc, dve):
        sh = self.sh
        link0 = Chain(dve, self.link)
        link0(nc.vector.memset(sh.scale, 1.0))
        link0(nc.vector.memset(sh.shift, 0.0))
        link0(nc.vector.memset(self.ew, 0.0))
        nc.vector.sem_inc(self.bn_ready, 1)
        dve.wait_ge(self.loaded, 48)
        before = link0.n

        def layer(l, first):
            with dve.Fori(0, NG) as g:
                it = l * NG + g
                for n, (t0, t1) in enumerate(self.PARTS):
                    dve.wait_ge(self.stored[n], START + it * 16)
                    nc.vector.tensor_copy(self.rows[:, t0:t1, D:TW], sh.dinv_col[:, ds(g * GT + t0, t1 - t0)].rearrange(
                        "p (t o) -> p t o", o=1).to_broadcast([P, t1 - t0, TW - D]))
                    for t in range(t0, t1):
                        dve.wait_ge(self.turned, START + it * GT + (t + 1 + GT))
                        nc.vector.tensor_scalar(self.rows[:, t, 0:D], self.turn[t % 2][:, 0:D],
                                                sh.dinv_col[:, ds(g * GT + t, 1)], None,
                                                ALU.mult).then_inc(self.row_done[t % 2], 1)
            dve.wait_ge(self.zeroed, START + l + 2)
            for n in range(2):
                dve.wait_ge(self.stored[n], START + (l + 1) * (NG * 16))
                hold(dve)
            self.a.dve(nc, dve, l * self.g.turns, first)
            for b in range(U):
                dve.wait_ge(self.a.added[b], START + (l + 1) * (NC1 // U))
            hold(dve)

            def full(m, j):
                it = l * self.TILES + m
                dve.wait_ge(self.edge_done, START + it + 1)
                dve.wait_ge(self.mixed, START + it)
                hold(dve)
                nc.vector.tensor_tensor(self.full[j], self.edge[:, :, 0:HW], sh.agg[:, :, ds(m * HW, HW)],
                                        ALU.add).then_inc(self.edge_used, 1)
                dve.wait_ge(self.edge_used, START + it + 1)
                for f in range(FB):
                    ins = nc.vector.tensor_tensor(self.full[j][:, f, :], self.full[j][:, f, :],
                                                  sh.dinv_row[:, ds(m * HW, HW)], ALU.mult)
                ins.then_inc(self.full_done, 1)

            def join(m, j):
                dve.wait_ge(self.mixed, START + l * self.TILES + m + 2)
                hold(dve)
                for o in range(FB):
                    here = sh.h[:, o, ds(m * HW, HW)]
                    ins = nc.vector.tensor_tensor(here, here, self.a.bank[2 * j + o][:, 0:HW], ALU.add)
                ins.then_inc(self.joined, 1)

            def spread(m, n, ins=None):
                dve.wait_ge(self.relu_done, START + l * self.TILES + m + 1)
                hold(dve)
                for o in range(FB):
                    ins = nc.vector.bn_stats(self.stats[:, o, ds(m, 1), :].rearrange("p m s -> p (m s)"),
                                             sh.h[:, o, ds(m * HW, n)])
                return ins
            dve.wait_ge(self.own_kept, START + (l + 1) * self.TILES)
            hold(dve)
            full(0, 0)
            full(1, 1)
            join(0, 0)
            with dve.Fori(1, self.TILES // 2) as m2:
                for j in range(2):
                    full(m2 * 2 + j, j)
                    join(m2 * 2 + (j - 1), 1 - j)
                    spread(m2 * 2 + (j - 2), HW)
            join(self.TILES - 1, 1)
            link = Chain(dve, self.link, l * self.PER + before)
            spread(self.TILES - 2, HW)
            link(spread(self.TILES - 1, self.LAST))
            hold(dve)
            for o in range(FB):
                ins = nc.vector.bn_aggr(self.mv[:, o, :], self.stats[:, o].rearrange("p m s -> p (m s)"))
            link(ins)
            nc.vector.tensor_scalar(self.rstd, self.mv[:, :, 1], BN_EPS, None, ALU.add).then_inc(self.var_done, 1)
            dve.wait_ge(self.root_done, START + l + 1)
            link(nc.vector.reciprocal(self.rstd, self.rstd))
            link(nc.vector.tensor_tensor(sh.scale, self.bn_g[:, ds(l * FB, FB)], self.rstd, ALU.mult))
            link(nc.vector.tensor_tensor(self.part, self.mv[:, :, 0], sh.scale, ALU.mult))
            nc.vector.tensor_tensor(sh.shift, self.bn_b[:, ds(l * FB, FB)], self.part,
                                    ALU.subtract).then_inc(self.bn_ready, 1)
        self.each(dve, layer)


def top2(nc, link, v, rank, cmp, E):
    link(nc.vector.memset(rank, 0.0))
    for j in range(E):
        for lo, hi, op in ((0, j, ALU.is_gt), (j + 1, E, ALU.is_ge)):
            if lo < hi:
                link(nc.vector.tensor_tensor(cmp[:, :, lo:hi], v[:, :, j:j + 1].to_broadcast([P, NT, hi - lo]),
                                             v[:, :, lo:hi], op))
                link(nc.vector.tensor_tensor(rank[:, :, lo:hi], rank[:, :, lo:hi], cmp[:, :, lo:hi], ALU.add))


class Shares:

    def __init__(self, sp, v, E, all_first, share):
        self.v, self.E, self.all_first, self.share = v, E, all_first, share
        self.rank, self.cmp, self.ex = (sp.sb(n, [P, NT, E]) for n in ("rank", "cmp", "ex"))
        self.most, self.total = sp.sb("most", [P, NT]), sp.sb("total", [P, NT])
        self.low_done, self.ex_done = sp.sem("gate_low"), sp.sem("gate_ex")

    def dve(self, nc, dve, link):
        E = self.E
        wide = lambda x: x.rearrange("p (t o) -> p t o", o=1).to_broadcast([P, NT, E])
        link(nc.vector.tensor_reduce(self.most, self.v, AX.X, ALU.max))
        nc.vector.tensor_tensor(self.ex, self.v, wide(self.most), ALU.subtract).then_inc(self.low_done, 1)
        dve.wait_ge(self.ex_done, START + 1)
        if self.all_first:
            link(nc.vector.tensor_reduce(self.total, self.ex, AX.X, ALU.add))
            link(nc.vector.reciprocal(self.total, self.total))
            link(nc.vector.tensor_tensor(self.ex, self.ex, wide(self.total), ALU.mult))
        top2(nc, link, self.ex if self.all_first else self.v, self.rank, self.cmp, E)
        link(nc.vector.scalar_tensor_tensor(self.share, self.rank, 1.5, self.ex, ALU.is_lt, ALU.mult))
        link(nc.vector.tensor_reduce(self.total, self.share, AX.X, ALU.add))
        link(nc.vector.tensor_scalar(self.total, self.total, 1e-12, None, ALU.max))
        link(nc.vector.reciprocal(self.total, self.total))
        link(nc.vector.tensor_tensor(self.share, self.share, wide(self.total), ALU.mult))

    def act(self, nc, act):
        act.wait_ge(self.low_done, START + 1)
        nc.scalar.activation(self.ex, self.ex, ACT.Exp).then_inc(self.ex_done, 1)


class Attention:

    def __init__(self, sp, sh, h16, table, edges, cw, share, d):
        self.sh, self.h16, self.table, self.edges, self.cw, self.d = sh, h16, table, edges, cw, d
        self.share = share
        self.g = Gather(sp, NC2, edges, RD, table, AW, tracked=False)
        self.turns, self.pairs = NC2 // SU, NC2 // (2 * V)
        self.all = sh.agg.rearrange("p f n -> p (f n)")[:, 0:NC2 * AW].rearrange("p (c w) -> p c w", w=AW)
        self.att = sp.sb("att", [P, 5, HX])
        self.row = sp.sb("row", [P, NT, AW])
        self.prod = sp.sb("prod", [P, NT, HX])
        self.node = sp.sb("node", [P, NT, 2 * HEADS])
        self.top, self.low = sp.sb("top", [P, NT, HEADS]), sp.sb("low", [P, NT, HEADS])
        self.sums = sp.sb("sums", [P, NT, AW])
        self.cold = [sp.sb(f"cold{s}", [P, U, P], BF16) for s in range(S)]
        self.off = sp.sb("off", [P, HEADS, P], BF16)
        self.diag = [sp.sb(f"diag{s}", [P, U, HEADS, P]) for s in range(S)]
        self.hot, self.turned = ([d.rearrange("p u a n -> p (u a n)").bitcast(BF16)[:, h * V * P:(h + 1) * V * P].rearrange(
            "p (u n) -> p u n", u=V) for h in range(2)] for d in self.diag[0:2])
        self.ident = sp.sb("ident", [P, P], BF16)
        self.red = [sp.sb(f"red{h}", [P, U, HEADS]) for h in range(2)]
        self.target = sp.sb("target", [P, V, 2 * HEADS])
        self.z, self.z2 = sp.sb("z", [P, V, HEADS]), sp.sb("z2", [P, V, HEADS])
        self.pay, self.pay_rest = [sp.sb(f"pay{h}", [P, V, AW]) for h in range(2)], sp.sb("pay_rest", [P, V, AW])
        self.pay3 = [sp.sb(f"pay3_{h}", [P, 3, V, AW], BF16) for h in range(2)]
        self.node3 = sp.sb("node3", [P, NT, 3, 2 * HEADS], BF16)
        self.banks = [sp.ps(f"banks{h}", [P, U, 512]) for h in range(2)]
        self.pt, self.pn = self.banks[0][:, 0, :].bitcast(BF16), [self.banks[0][:, 2 + h, :] for h in range(2)]
        self.pd = [self.banks[1][:, h, :] for h in range(2)]
        self.loaded, self.stored = sp.sem("loaded", dma=True), sp.sem("stored", dma=True)
        names = ("link", "rows_ready", "kept", "diag_done", "cold_ready", "maxed", "hot2", "turn_done", "turn_kept",
                 "nodes_done", "z_done", "ex_done", "split", "pay_done", "paid", "summed")
        (self.link, self.rows_ready, self.kept, self.diag_done, self.cold_ready, self.maxed, self.hot2, self.turn_done,
         self.turn_kept, self.nodes_done, self.z_done, self.ex_done, self.split, self.pay_done, self.paid,
         self.summed) = (sp.sem(n) for n in names)
        self.spread = sp.sem("spread")
        self.reduced = sp.sem("reduced")
        self.var_done, self.root_done = sp.sem("var_done"), sp.sem("root_done")
        self.gate = Shares(sp, sp.sb("scores", [P, NT, XD]), XD, False, share)

    def sp(self, nc, sp):
        for n, src in enumerate(self.d):
            sp.dma_start(self.att[:, n, :], src.partition_broadcast(P)).then_inc(self.loaded, 16)
        sp.wait_ge(self.rows_ready, START + 1)
        hold(sp)
        sp.dma_start(self.table.rearrange("(t p) w -> p t w", p=P), self.row).then_inc(self.stored, 16)

    def pool(self, nc, pool):
        pool.wait_ge(self.stored, 16)
        hold(pool)
        with pool.Fori(0, self.turns) as i:
            for s in range(S):
                self.g.pool_set(nc, pool, i, s)

    def act(self, nc, act):
        sh = self.sh
        nodes = lambda c: self.edges[:, ds(c, U), 0].bitcast(I32)
        for s in range(S):
            nc.scalar.copy(self.g.idx[s], nodes(s * U)).then_inc(self.g.ready[s], 1)
        with act.Fori(0, self.turns) as i:
            for s in range(S):
                act.wait_ge(self.g.here[s], i * (16 * U) + 16 * U)
                c = i * SU + s * U
                hold(act)
                nc.scalar.copy(self.all[:, ds(c, U), :], self.g.rows[s]).then_inc(self.kept, 1)
                act.wait_ge(self.spread, START + i * S + (s + 1))
                for u in range(U):
                    for a in range(HEADS):
                        ins = nc.scalar.activation(self.diag[s][:, u, a, :], sh.ident, ACT.Copy,
                                                   scale=self.g.rows[s][:, u, a:a + 1])
                ins.then_inc(self.diag_done, 1)
                nc.scalar.copy(self.g.idx[s], nodes(c + SU)).then_inc(self.g.ready[s], 1)

        def keep_turned(k, h):
            act.wait_ge(self.turn_done, START + k + 1)
            nc.scalar.copy(self.turned[h].rearrange("p u n -> p (u n)"), self.pt).then_inc(self.turn_kept, 1)

        def step(k, h, last):
            act.wait_ge(self.z_done, START + k * 4 + 4)
            nc.scalar.activation(self.pay[h][:, :, 0:HEADS], self.z, ACT.Exp).then_inc(self.ex_done, 1)
            if not last:
                keep_turned(k + 1, 1 - h)
        keep_turned(0, 0)
        self.steps(act, step)
        act.wait_ge(self.var_done, START + 1)
        nc.scalar.activation(self.top[:, :, 0], self.top[:, :, 0], ACT.Sqrt).then_inc(self.root_done, 1)
        self.gate.act(nc, act)

    def steps(self, eng, step):
        with eng.Fori(0, self.pairs - 1) as i:
            for h in range(2):
                step(i * 2 + h, h, False)
        for h in range(2):
            step(self.pairs * 2 - 2 + h, h, h == 1)

    def pe(self, nc, pe):
        sh = self.sh
        nc.tensor.sem_inc(self.spread, S)
        with pe.Fori(0, self.turns) as i:
            for s in range(S):
                pe.wait_ge(self.diag_done, START + i * S + (s + 1))
                pe.wait_ge(self.cold_ready, START + i * S + (s + 1))
                pe.wait_ge(self.reduced, START + i * S + (s + 1))
                for u in range(U):
                    bank = self.banks[s % 2][:, u, :]
                    nc.tensor.matmul(bank, sh.ones, self.diag[s][:, u].rearrange("p a n -> p (a n)"), start=True,
                                     stop=False)
                    ins = nc.tensor.matmul(bank, self.cold[s][:, u, :], self.off.rearrange("p a n -> p (a n)"),
                                           start=False, stop=True)
                ins.then_inc(self.spread, 1)

        def look_up(k, h):
            pe.wait_ge(self.hot2, START + k + 1)
            pe.wait_ge(self.turn_kept, START + k)
            for u in range(V):
                ins = nc.tensor.transpose(self.pt[:, u * P:(u + 1) * P], self.hot[h][:, u, :], self.ident)
            ins.then_inc(self.turn_done, 1)
            windows = windows_of(nc, mybir.EngineType.PE, self.cw, k * V, V)
            pe.wait_ge(self.turn_kept, START + k + 1)
            hold(pe)
            for u, w in enumerate(windows):
                ins = nc.tensor.matmul(self.pn[h][:, u * 6 * HEADS:(u + 1) * 6 * HEADS], self.turned[h][:, u, :],
                                       self.node3[:, ds(w, 1), :, :].rearrange("p o q c -> p (o q c)"),
                                       start=True, stop=True)
            ins.then_inc(self.nodes_done, 1)

        def pay(k, h):
            pe.wait_ge(self.pay_done, START + k + 1)
            for u in range(V):
                for q in range(3):
                    ins = nc.tensor.matmul(self.pd[h][:, u * 32:u * 32 + AW], self.hot[h][:, u, :],
                                           self.pay3[h][:, q, u, :], start=(q == 0), stop=(q == 2))
            ins.then_inc(self.paid, 1)

        def step(k, h, last):
            if not last:
                look_up(k + 1, 1 - h)
            pay(k, h)
        pe.wait_ge(self.reduced, START + self.turns * S + 2)
        look_up(0, 0)
        self.steps(pe, step)

    def dve(self, nc, dve):
        sh = self.sh
        link = Chain(dve, self.link)
        dve.wait_ge(self.loaded, 5 * 16)
        across = lambda n: self.att[:, n:n + 1, :].to_broadcast([P, NT, HX])
        by_head = lambda x: x.rearrange("p t (h x) -> p t h x", h=HEADS)
        for n, to in ((0, self.row[:, :, 0:HEADS]), (1, self.node[:, :, 0:HEADS])):
            link(nc.vector.tensor_tensor(self.prod, self.h16, across(n), ALU.mult))
            link(nc.vector.tensor_reduce(to, by_head(self.prod), AX.X, ALU.add))
        nc.vector.tensor_copy(self.row[:, :, HEADS:AW], self.h16).then_inc(self.rows_ready, 1)
        for a in range(HEADS):
            link(nc.vector.tensor_scalar(self.off[:, a, :], sh.ident, -BIG, None, ALU.mult))
        link(nc.vector.memset(self.top, -3e38))
        link(nc.vector.memset(self.sums, 0.0))
        nc.vector.sem_inc(self.reduced, 2)

        def matrices(k, c, s):
            dve.wait_ge(self.spread, START + k + 1)
            hold(dve)
            for u in range(U):
                ins = nc.vector.tensor_scalar(self.cold[s][:, u, :], sh.iota, self.edges[:, ds(c + u, 1), 1], None,
                                              ALU.not_equal)
            ins.then_inc(self.cold_ready, 1)

        def largest(i, last):
            for s in range(S):
                k, c = i * S + s, i * SU + s * U
                if not (last and s == S - 1):
                    matrices(k + 1, c + U, (s + 1) % S)
                red = self.red[s % 2]
                dve.wait_ge(self.spread, START + k + (1 + S))
                nc.vector.tensor_reduce(red, self.banks[s % 2].rearrange("p u (a n) -> p u a n", a=HEADS), AX.X,
                                        ALU.max).then_inc(self.reduced, 1)
                windows = windows_of(nc, mybir.EngineType.DVE, self.cw, c, U)
                dve.wait_ge(self.reduced, START + k + 3)
                for u, w in enumerate(windows):
                    dve.wait_ge(self.maxed, START + c + u)
                    to = self.top[:, ds(w, 1), :]
                    nc.vector.tensor_tensor(to, to, red[:, u:u + 1, :], ALU.max).then_inc(self.maxed, 1)
        matrices(0, 0, 0)
        with dve.Fori(0, self.turns - 1) as i:
            largest(i, False)
        largest(self.turns - 1, True)
        dve.wait_ge(self.maxed, START + NC2)
        link(nc.vector.tensor_tensor(self.top, self.top, self.node[:, :, 0:HEADS], ALU.add))
        link(nc.vector.tensor_scalar(self.low, self.top, 0.2, None, ALU.mult))
        link(nc.vector.tensor_tensor(self.node[:, :, HEADS:2 * HEADS], self.top, self.low, ALU.max))
        node_rest = self.prod[:, :, 0:2 * HEADS]
        link(nc.vector.tensor_copy(self.ident, sh.ident))
        link(nc.vector.tensor_copy(self.node3[:, :, 0, :], self.node))
        link(nc.vector.tensor_tensor(node_rest, self.node, self.node3[:, :, 0, :], ALU.subtract))
        link(nc.vector.tensor_copy(self.node3[:, :, 1, :], node_rest))
        link(nc.vector.tensor_tensor(self.node3[:, :, 2, :], node_rest, self.node3[:, :, 1, :], ALU.subtract))
        dve.wait_ge(self.kept, START + NC2 // U)
        hold(dve)

        def edge_matrices(k, h):
            if not isinstance(k, int) or k:
                dve.wait_ge(self.paid, START + k - 1)
                hold(dve)
            for u in range(V):
                ins = nc.vector.tensor_scalar(self.hot[h][:, u, :], sh.iota, self.edges[:, ds(k * V + u, 1), 1], None,
                                              ALU.is_equal)
            ins.then_inc(self.hot2, 1)

        def cut(k, h, part):
            pay, rest, pay3 = self.pay[h], self.pay_rest, self.pay3[h]
            dve.wait_ge(self.split, START + k * 4 + (part + 1))
            if part == 0:
                nc.vector.tensor_copy(pay3[:, 0], pay).then_inc(self.split, 1)
            elif part == 1:
                nc.vector.tensor_tensor(rest, pay, pay3[:, 0], ALU.subtract).then_inc(self.split, 1)
            elif part == 2:
                nc.vector.tensor_copy(pay3[:, 1], rest).then_inc(self.split, 1)
            else:
                nc.vector.tensor_tensor(pay3[:, 2], rest, pay3[:, 1], ALU.subtract).then_inc(self.pay_done, 1)

        def add(k, h, last=False):
            windows = windows_of(nc, mybir.EngineType.DVE, self.cw, k * V, V)
            dve.wait_ge(self.paid, START + k + 1)
            hold(dve)
            for u, w in enumerate(windows):
                dve.wait_ge(self.summed, START + k * V + u)
                to = self.sums[:, ds(w, 1), :].rearrange("p o c -> p (o c)")
                nc.vector.tensor_tensor(to, to, self.pd[h][:, u * 32:u * 32 + AW], ALU.add).then_inc(self.summed, 1)
                if u < 4 and not last:
                    cut(k + 1, 1 - h, u)

        def step(k, h, last, first=False):
            rows = self.all[:, ds(k * V, V), :]
            parts = self.pn[h][:, 0:V * 6 * HEADS].rearrange("p (u q c) -> p u c q", u=V, q=3)
            dve.wait_ge(self.nodes_done, START + k + 1)
            dve.wait_ge(self.ex_done, START + k)
            hold(dve)
            nc.vector.tensor_reduce(self.target, parts, AX.X, ALU.add).then_inc(self.z_done, 1)
            dve.wait_ge(self.z_done, START + k * 4 + 1)
            nc.vector.tensor_tensor(self.z, rows[:, :, 0:HEADS], self.target[:, :, 0:HEADS],
                                    ALU.add).then_inc(self.z_done, 1)
            dve.wait_ge(self.z_done, START + k * 4 + 2)
            nc.vector.scalar_tensor_tensor(self.z2, self.z, 0.2, self.z, ALU.mult, ALU.max).then_inc(self.z_done, 1)
            dve.wait_ge(self.z_done, START + k * 4 + 3)
            nc.vector.tensor_tensor(self.z, self.z2, self.target[:, :, HEADS:2 * HEADS],
                                    ALU.subtract).then_inc(self.z_done, 1)
            if not last:
                edge_matrices(k + 1, 1 - h)
            dve.wait_ge(self.ex_done, START + k + 1)
            pay = self.pay[h][:, :, HEADS:AW].rearrange("p u (a x) -> p u a x", a=HEADS)
            ex = self.pay[h][:, :, 0:HEADS].rearrange("p u (a o) -> p u a o", o=1).to_broadcast([P, V, HEADS, XD])
            nc.vector.tensor_tensor(pay, rows[:, :, HEADS:AW].rearrange("p u (a x) -> p u a x", a=HEADS), ex,
                                    ALU.mult).then_inc(self.split, 1)
            if first:
                for part in range(4):
                    cut(k, h, part)
            else:
                add(k - 1, 1 - h)
        edge_matrices(0, 0)
        for h in range(2):
            step(h, h, False, h == 0)
        with dve.Fori(1, self.pairs - 1) as i:
            for h in range(2):
                step(i * 2 + h, h, False)
        for h in range(2):
            step(self.pairs * 2 - 2 + h, h, h == 1)
        add(self.pairs * 2 - 1, 1, True)
        dve.wait_ge(self.summed, START + NC2)
        den, out = self.sums[:, :, 0:HEADS], self.sums[:, :, HEADS:AW]
        link(nc.vector.tensor_scalar(den, den, 1e-16, None, ALU.add))
        link(nc.vector.reciprocal(self.low, den))
        wide = self.low.rearrange("p t (a o) -> p t a o", o=1).to_broadcast([P, NT, HEADS, XD])
        link(nc.vector.tensor_tensor(by_head(self.prod), by_head(out), wide, ALU.mult))
        link(nc.vector.tensor_tensor(self.prod, self.prod, across(2), ALU.add))
        mean = self.top[:, :, 0]
        over = self.top[:, :, 0:1].to_broadcast([P, NT, HX])
        link(nc.vector.tensor_reduce(mean, self.prod, AX.X, ALU.add))
        link(nc.vector.tensor_scalar(mean, mean, 1.0 / HX, None, ALU.mult))
        link(nc.vector.tensor_tensor(self.prod, self.prod, over, ALU.subtract))
        link(nc.vector.tensor_tensor(out, self.prod, self.prod, ALU.mult))
        link(nc.vector.tensor_reduce(mean, out, AX.X, ALU.add))
        nc.vector.tensor_scalar(mean, mean, 1.0 / HX, LN_EPS, ALU.mult, ALU.add).then_inc(self.var_done, 1)
        dve.wait_ge(self.root_done, START + 1)
        link(nc.vector.reciprocal(mean, mean))
        link(nc.vector.tensor_tensor(self.prod, self.prod, over, ALU.mult))
        link(nc.vector.tensor_tensor(self.prod, self.prod, across(3), ALU.mult))
        link(nc.vector.tensor_tensor(self.prod, self.prod, across(4), ALU.add))
        link(nc.vector.tensor_reduce(self.gate.v, self.prod.rearrange("p t (h x) -> p t x h", h=HEADS), AX.X, ALU.add))
        link(nc.vector.tensor_scalar(self.gate.v, self.gate.v, 1.0 / HEADS, None, ALU.mult))
        self.gate.dve(nc, dve, link)


class AddTurned:

    def __init__(self, sp, sh, table):
        self.sh, self.table = sh, table
        self.x = [sp.sb(f"x{j}", [P, D]) for j in range(2)]
        self.turn = [sp.ps(f"turn{j}", [P, 512]) for j in range(2)]
        self.here = [sp.sem(f"here{j}", dma=True) for j in range(2)]
        self.turned = [sp.sem(f"turned{j}") for j in range(2)]
        self.added = [sp.sem(f"added{j}") for j in range(2)]

    def tiles(self, eng, body):
        with eng.Fori(0, NT // 2) as i:
            for j in range(2):
                body(i * 2 + j, j, i)
        body(NT - 1, 0, NT // 2)

    def sp(self, nc, sp):
        def load(t, j, n):
            sp.wait_ge(self.turned[j], START + n)
            hold(sp)
            sp.dma_start(self.x[j], self.table[ds(t * P, P), :]).then_inc(self.here[j], 16)
        self.tiles(sp, load)

    def pe(self, nc, pe):
        def turn(t, j, n):
            pe.wait_ge(self.here[j], n * 16 + 16)
            pe.wait_ge(self.added[j], START + n)
            for f in range(FB):
                ins = nc.tensor.transpose(self.turn[j][:, f * P:(f + 1) * P], self.x[j][:, f * P:(f + 1) * P],
                                          self.sh.ident)
            ins.then_inc(self.turned[j], 1)
        self.tiles(pe, turn)

    def dve(self, nc, dve):
        def add(t, j, n):
            dve.wait_ge(self.turned[j], START + n + 1)
            to = self.sh.agg[:, :, ds(t * P, P)]
            nc.vector.tensor_tensor(to, to, self.turn[j][:, 0:D].rearrange("p (f n) -> p f n", f=FB),
                                    ALU.add).then_inc(self.added[j], 1)
        self.tiles(dve, add)


def program(nc, x, src, dst, edge_attr_4, edge_weight, L0_gnn_W1, L0_gnn_b1, L0_gnn_W2, L0_gnn_b2, L0_ffn_router_w,
            L0_ffn_w1, L0_ffn_b1, L0_ffn_w2, L0_ffn_b2, L1_gnn_mlp_w, L1_gnn_mlp_b, L1_gnn_ew1, L1_gnn_ew2,
            L1_gnn_bn_g, L1_gnn_bn_b, L1_ffn_W_gat, L1_ffn_att_src, L1_ffn_att_dst, L1_ffn_b_gat, L1_ffn_ln_gamma,
            L1_ffn_ln_beta, L1_ffn_W1, L1_ffn_b1, L1_ffn_W2, L1_ffn_b2, L1_ffn_edge_index, out, last_phase=99):
    table = lambda name, shape: nc.dram_tensor(name, shape, F32, kind="Internal").ap()
    x0, xn0, x1, both1, x2, x3 = (table(n, [NP, D]) for n in ("x0", "xn0", "x1", "both1", "x2", "x3"))
    listA, listC, listD = (table(n, [P * c, r]) for n, c, r in
                           (("listA", NC1, RA), ("listC", NC1, RC), ("listD", NC2, RD)))
    dinv = table("dinv", [NT, P])
    nodesC, nodesD = table("nodesC", [NP, TW]), table("nodesD", [NP, AW])
    lanes = lambda lst: lst.rearrange("(p c) w -> p (c w)", p=P)

    with ExitStack() as whole:
        sb = lambda name, shape, dt=F32: whole.enter_context(nc.sbuf_tensor(name, shape, dt))[:]
        sh = Shared()
        rows = sb("rows", [P, NP])
        cwC, cwD = rows[32:33, 0:NC1].bitcast(I32), rows[64:65, 0:NC2].bitcast(I32)
        sh.agge = rows[0:4, :]
        sh.h, sh.agg = sb("h", [P, FB, NP]), sb("agg", [P, FB, NP])
        sh.ident, sh.iota, sh.ones, sh.below = (sb(n, [P, P]) for n in ("ident", "iota", "ones", "below"))
        sh.wincol = sb("wincol", [P, NT])
        sh.scale, sh.shift, sh.dinv_col = sb("scale", [P, FB]), sb("shift", [P, FB]), sb("dinv_col", [P, NT])

        def cut(whole_tile):
            flat, at = whole_tile.rearrange("p f n -> p (f n)"), [0]

            def take(parts, *shape):
                n = 1
                for d in shape:
                    n *= d
                piece = flat[0:parts, at[0]:at[0] + n]
                at[0] += n
                return piece if len(shape) == 1 else piece.rearrange("p (t w) -> p t w", w=shape[1])
            return take
        take = cut(sh.h)
        cwA = take(1, NC1).bitcast(I32)
        recA, recC = take(E1P, E1T, RA), take(E1P, E1T, RC)
        rowA, rowC = take(E1P, E1T).bitcast(I32), take(E1P, E1T).bitcast(I32)
        recD, rowD = sb("recD", [P, E2T, RD]), sb("rowD", [P, E2T], I32)
        scatC = Scatter(Space(nc, whole, [], "scatC"), E1P, E1T, NC1, rowC, recC, listC, RC)
        scatD = Scatter(Space(nc, whole, [], "scatD"), P, E2T, NC2, rowD, recD, listD, RD)
        take = cut(sh.agg)
        src_sb, dst_sb = take(E1P, E1T).bitcast(I32), take(E1P, E1T).bitcast(I32)
        sh.chunkrow = take(P, NC1)
        wt_sb, attr_sb = take(E1P, E1T), take(E1P, E1T, 4)
        from_sb, to_sb = take(P, E2T).bitcast(I32), take(P, E2T).bitcast(I32)

        def phase(name, build):
            sems = []
            with ExitStack() as mem:
                build(lambda part: Space(nc, mem, sems, f"{name}_{part}"))
            numbers = sorted(s.num for s in sems)
            while numbers:
                n = next((i for i in range(1, len(numbers)) if numbers[i] != numbers[0] + i), len(numbers))
                nc.sync.sem_clear(range(numbers[0], numbers[n - 1] + 1))
                numbers = numbers[n:]
            nc.all_engine_barrier()
            for s in sems:
                nc.release_semaphore(s)

        def setup(space):
            sp_ = space("in")
            sort = Sort(space("sort"), sh, E1P, E1T, NC1, src_sb, recA, rowA, cwA)
            pads = [sp_.sb(f"pad{n}", [P, c, r]) for n, c, r in ((0, NC1, RA), (1, NC1, RC), (2, NC2, RD))]
            zero = sp_.sb("zero", [NP - N, D])
            loaded, stored = sp_.sem("loaded", dma=True), sp_.sem("stored", dma=True)
            const, padded, recs, ready = (sp_.sem(n) for n in ("const", "padded", "recs", "ready"))
            cut1 = lambda a: a.rearrange("(p t) -> p t", p=E1P)
            with nc.Block() as block:
                @block.sync
                def _(sp):
                    sp.dma_start(src_sb, cut1(src)).then_inc(loaded, 16)
                    sp.dma_start(dst_sb, cut1(dst)).then_inc(loaded, 16)
                    sp.dma_start(wt_sb, cut1(edge_weight)).then_inc(loaded, 16)
                    sp.dma_start(attr_sb, edge_attr_4.rearrange("(p t) w -> p t w", p=E1P)).then_inc(loaded, 16)
                    for n, to in ((0, from_sb), (1, to_sb)):
                        sp.dma_start(to[:, 0:E2T - NT], L1_ffn_edge_index[n].rearrange("(p t) -> p t",
                                                                                      p=P)).then_inc(loaded, 16)
                    sp.dma_start(x0[0:N, :], x).then_inc(stored, 16)
                    sp.wait_ge(padded, START + 4)
                    hold(sp)
                    sp.dma_start(x0[N:NP, :], zero).then_inc(stored, 16)
                    for pad, lst in zip(pads, (listA, listC, listD)):
                        sp.dma_start(lanes(lst), pad.rearrange("p c w -> p (c w)")).then_inc(stored, 16)
                    sp.wait_ge(stored, 5 * 16)
                    sp.wait_ge(recs, START + 1)

                @block.gpsimd
                def _(pool):
                    nc.gpsimd.iota(sh.iota, [[1, P]], base=0, channel_multiplier=0,
                                   allow_small_or_imprecise_dtypes=True)
                    nc.gpsimd.iota(sh.wincol, [[1, NT]], base=0, channel_multiplier=0,
                                   allow_small_or_imprecise_dtypes=True)
                    nc.gpsimd.iota(sh.chunkrow, [[P, NC1]], base=0, channel_multiplier=0,
                                   allow_small_or_imprecise_dtypes=True)
                    nc.gpsimd.memset(sh.ones, 1.0)
                    nc.gpsimd.memset(sh.below, 1.0)
                    nc.gpsimd.memset(sh.ident, 0.0).then_inc(const, 1)
                    for to in (from_sb, to_sb):
                        nc.gpsimd.iota(to[:, E2T - NT:E2T], [[P, NT]], base=0, channel_multiplier=1)
                    pool.wait_ge(const, START + 1)
                    nc.gpsimd.affine_select(out=sh.below, in_=sh.below, compare_op=ALU.is_gt, fill=0.0, base=0,
                                            pattern=[[1, P]], channel_multiplier=-1)
                    nc.gpsimd.affine_select(out=sh.ident, in_=sh.ident, compare_op=ALU.not_equal, fill=1.0, base=0,
                                            pattern=[[-1, P]], channel_multiplier=1).then_inc(ready, 1)
                    nc.gpsimd.memset(zero, 0.0).then_inc(padded, 1)
                    for n, pad in enumerate(pads):
                        nc.gpsimd.memset(pad, 0.0).then_inc(const, 1)
                        pool.wait_ge(const, START + n * 2 + 2)
                        nc.gpsimd.memset(pad[:, :, 1], -1.0).then_inc(const, 1)
                        nc.gpsimd.memset(pad.bitcast(I32)[:, :, 0], N).then_inc(padded, 1)

                @block.scalar
                def _(act):
                    act.wait_ge(loaded, 6 * 16)
                    act.wait_ge(ready, START + 1)
                    nc.scalar.copy(recA.bitcast(I32)[:, :, 0], dst_sb)
                    nc.scalar.copy(recA[:, :, 2], wt_sb)
                    nc.scalar.copy(recC.bitcast(I32)[:, :, 0], src_sb)
                    nc.scalar.copy(recC[:, :, 2:6], attr_sb)
                    nc.scalar.copy(recD.bitcast(I32)[:, :, 0], from_sb).then_inc(recs, 1)

                @block.vector
                def _(dve):
                    dve.wait_ge(loaded, 6 * 16)
                    dve.wait_ge(ready, START + 1)
                    sort.dve(nc, dve)

                @block.tensor
                def _(pe):
                    pe.wait_ge(ready, START + 1)
                    sort.pe(nc, pe)

        def place_first(space):
            norm = Norm(space("norm"), sh, x0, normed=xn0, depth=1)
            scat = Scatter(space("scat"), E1P, E1T, NC1, rowA, recA, listA, RA)
            with ExitStack() as psum:
                sortC = Sort(space("sortC"), sh, E1P, E1T, NC1, dst_sb, recC, rowC, cwC)
                deg = Degree(space("deg"), sh, sortC.win, recC[:, :, 1], dinv)
                sortD = Sort(space("sortD"), sh, P, E2T, NC2, to_sb, recD, rowD, cwD)
                with nc.Block() as block:
                    @block.sync
                    def _(sp):
                        norm.sp(nc, sp)
                        deg.sp(nc, sp)

                    @block.scalar
                    def _(act):
                        norm.act(nc, act)
                        deg.act(nc, act)

                    @block.gpsimd
                    def _(pool):
                        scat.pool(nc, pool, 0, scat.sets, True)
                        scat.pool_rest(nc, pool)

                    @block.vector
                    def _(dve):
                        norm.dve(nc, dve)
                        sortC.dve(nc, dve)
                        deg.dve(nc, dve)
                        sortD.dve(nc, dve)

                    @block.tensor
                    def _(pe):
                        sortC.pe(nc, pe)
                        deg.pe(nc, pe)
                        sortD.pe(nc, pe)

        def first_sums(space):
            sp_ = space("sums")
            edges = sp_.sb("edges", [P, NC1, RA])
            g = Gather(space("gather"), NC1, edges, RA, xn0, D)
            a = Aggregate(space("agg"), sh, g, edges, cwA, sh.agg, True)
            here, zeroed = sp_.sem("here", dma=True), sp_.sem("zeroed")
            with nc.Block() as block:
                @block.sync
                def _(sp):
                    sp.dma_start(edges.rearrange("p c w -> p (c w)"), lanes(listA)).then_inc(here, 16)

                @block.scalar
                def _(act):
                    act.wait_ge(here, 16)
                    hold(act)
                    with act.Fori(0, g.turns) as i:
                        for s in range(S):
                            g.act_set(nc, act, i, i, s)

                @block.gpsimd
                def _(pool):
                    with pool.Fori(0, g.turns) as i:
                        for s in range(S):
                            g.pool_set(nc, pool, i, s)

                @block.vector
                def _(dve):
                    nc.vector.memset(sh.agg, 0.0).then_inc(zeroed, 1)
                    dve.wait_ge(zeroed, START + 1)
                    dve.wait_ge(here, 16)
                    hold(dve)
                    a.dve(nc, dve, 0, False)

                @block.tensor
                def _(pe):
                    nc.tensor.sem_inc(g.used, AHEAD)
                    with pe.Fori(0, g.turns) as i:
                        for s in range(S):
                            a.pe_set(nc, pe, i, s, False)

        def first_add(space):
            add = AddTurned(space("add"), sh, xn0)
            with nc.Block() as block:
                @block.gpsimd
                def _(pool):
                    scatC.pool(nc, pool, 0, PARTS_C[0], True)

                @block.sync
                def _(sp):
                    add.sp(nc, sp)

                @block.tensor
                def _(pe):
                    add.pe(nc, pe)

                @block.vector
                def _(dve):
                    add.dve(nc, dve)

        def dense(space, ffn, pool_part=None, ones=None):
            with nc.Block() as block:
                @block.sync
                def _(sp):
                    ffn.sp_load(nc, sp)
                    ffn.sp(nc, sp)

                @block.scalar
                def _(act):
                    ffn.act(nc, act)

                @block.tensor
                def _(pe):
                    ffn.pe(nc, pe)

                @block.vector
                def _(dve):
                    if ones is not None:
                        tile, done = ones
                        nc.vector.memset(tile, 1.0).then_inc(done, 1)
                        dve.wait_ge(done, START + 1)
                    ffn.dve(nc, dve)

                if pool_part is not None:
                    @block.gpsimd
                    def _(pool):
                        pool_part(pool)

        def first_ffn(space):
            sp_ = space("one")
            share = sp_.sb("share", [P, NT, 1])
            one = lambda a: a.rearrange("(o k) m -> o k m", o=1)
            row = lambda a: a.rearrange("(o m) -> o m", o=1)
            ffn = Ffn(space("ffn"), sh, sh.agg, 1, 4, one(L0_gnn_W1), row(L0_gnn_b1), one(L0_gnn_W2), row(L0_gnn_b2),
                      ACT.Relu, share, x0, x1)
            dense(space, ffn, lambda pool: scatC.pool(nc, pool, sum(PARTS_C[:1]), PARTS_C[1], False),
                  (share, sp_.sem("done")))

        def first_mixture(space):
            sp_ = space("mix")
            share = sp_.sb("share", [P, NT, XB])
            with ExitStack() as part:
                space2 = lambda n: Space(nc, part, sp_.sems, "mix_" + n)
                q = space2("router")
                head, logits = q.sb("head", [P, FB, XB]), q.sb("logits", [P, NT, XB])
                norm = Norm(space2("norm"), sh, x1, both=both1, tok=sh.agg, head=head, head_out=logits)
                gate = Shares(space2("gate"), logits, XB, True, share)
                head_here, link, done = q.sem("head_here", dma=True), q.sem("link"), q.sem("done")
                with nc.Block() as block:
                    @block.sync
                    def _(sp):
                        for f in range(FB):
                            sp.dma_start(head[:, f, :], L0_ffn_router_w[:, f * P:(f + 1) * P].rearrange(
                                "e p -> p e"), allow_slow_non_contiguous=True).then_inc(head_here, 16)
                        norm.sp(nc, sp)

                    @block.scalar
                    def _(act):
                        norm.act(nc, act)
                        gate.act(nc, act)

                    @block.gpsimd
                    def _(pool):
                        scatC.pool(nc, pool, sum(PARTS_C[:2]), PARTS_C[2], False)

                    @block.tensor
                    def _(pe):
                        pe.wait_ge(head_here, 16 * FB)
                        norm.pe(nc, pe)

                    @block.vector
                    def _(dve):
                        norm.dve(nc, dve)
                        dve.wait_ge(norm.head_used, START + NG)
                        gate.dve(nc, dve, Chain(dve, link))
            ffn = Ffn(space("ffn"), sh, sh.agg, XB, 2, L0_ffn_w1, L0_ffn_b1, L0_ffn_w2, L0_ffn_b2, ACT.Gelu, share,
                      both1, x2)
            def rest_of_list(pool):
                scatC.pool(nc, pool, sum(PARTS_C[:3]), scatC.sets - sum(PARTS_C[:3]), False)
                scatC.pool_rest(nc, pool)
                scatD.pool(nc, pool, 0, PART_D, True)
            dense(space, ffn, rest_of_list)

        def messages(space):
            sp_ = space("msg")
            edges = sp_.sb("edges", [P, NC1, RC])
            sh.dinv_row = sp_.sb("dinv_row", [P, NP])
            here = sp_.sem("here", dma=True)
            with ExitStack() as part:
                space2 = lambda n: Space(nc, part, sp_.sems, "msg_" + n)
                norm = Norm(space2("norm"), sh, x2, tok=sh.h)
                with nc.Block() as block:
                    @block.sync
                    def _(sp):
                        sp.dma_start(edges.rearrange("p c w -> p (c w)"), lanes(listC)).then_inc(here, 16)
                        sp.dma_start(sh.dinv_row, dinv.rearrange("t p -> (t p)").partition_broadcast(P)).then_inc(here, 16)
                        norm.sp(nc, sp)
                        sp.wait_ge(here, 32)

                    @block.scalar
                    def _(act):
                        norm.act(nc, act)

                    @block.tensor
                    def _(pe):
                        norm.pe(nc, pe)

                    @block.vector
                    def _(dve):
                        norm.dve(nc, dve)
            layers = Layers(space("layers"), sh, scatD, edges, cwC, nodesC, L1_gnn_mlp_w, L1_gnn_mlp_b, L1_gnn_ew1,
                            L1_gnn_ew2, L1_gnn_bn_g, L1_gnn_bn_b)
            with nc.Block() as block:
                @block.sync
                def _(sp):
                    layers.sp(nc, sp)

                @block.scalar
                def _(act):
                    layers.act(nc, act)

                @block.gpsimd
                def _(pool):
                    layers.pool(nc, pool)

                @block.tensor
                def _(pe):
                    layers.pe(nc, pe)

                @block.vector
                def _(dve):
                    layers.dve(nc, dve)

        def last_mixture(space):
            sp_ = space("gat")
            share = sp_.sb("share", [P, NT, XD])
            with ExitStack() as part:
                space2 = lambda n: Space(nc, part, sp_.sems, "gat_" + n)
                q = space2("in")
                h16, edges = q.sb("h16", [P, NT, HX]), q.sb("edges", [P, NC2 + SU, RD])
                here = q.sem("here", dma=True)
                with ExitStack() as part1:
                    space3 = lambda n: Space(nc, part1, sp_.sems, "gat_" + n)
                    head = space3("head").sb("w", [P, FB, HX])
                    norm = Norm(space3("norm"), sh, x2, tok=sh.h, head=head, head_out=h16, add=sh.h, summed=x3)
                    with nc.Block() as block:
                        @block.sync
                        def _(sp):
                            sp.dma_start(head, L1_ffn_W_gat.rearrange("(f p) m -> p f m", p=P)).then_inc(here, 16)
                            sp.dma_start(edges[:, 0:NC2, :].rearrange("p c w -> p (c w)"),
                                         lanes(listD)).then_inc(here, 16)
                            norm.sp(nc, sp)
                            sp.wait_ge(here, 32)

                        @block.gpsimd
                        def _(pool):
                            nc.gpsimd.memset(edges[:, NC2:NC2 + SU, :].bitcast(I32), N)

                        @block.scalar
                        def _(act):
                            norm.act(nc, act)

                        @block.tensor
                        def _(pe):
                            pe.wait_ge(here, 32)
                            norm.pe(nc, pe)

                        @block.vector
                        def _(dve):
                            norm.dve(nc, dve)
                att = Attention(space2("att"), sh, h16, nodesD, edges, cwD, share,
                                [L1_ffn_att_src.rearrange("h x -> (h x)"), L1_ffn_att_dst.rearrange("h x -> (h x)"),
                                 L1_ffn_b_gat, L1_ffn_ln_gamma, L1_ffn_ln_beta])
                with nc.Block() as block:
                    @block.sync
                    def _(sp):
                        att.sp(nc, sp)

                    @block.gpsimd
                    def _(pool):
                        att.pool(nc, pool)

                    @block.scalar
                    def _(act):
                        att.act(nc, act)

                    @block.tensor
                    def _(pe):
                        att.pe(nc, pe)

                    @block.vector
                    def _(dve):
                        att.dve(nc, dve)
            ffn = Ffn(space("ffn"), sh, sh.h, XD, 4, L1_ffn_W1, L1_ffn_b1, L1_ffn_W2, L1_ffn_b2, ACT.Gelu, share, x3,
                      out)
            dense(space, ffn)

        phases = [("p1", setup), ("p2", place_first), ("p3", first_sums), ("p4", first_add), ("p5", first_ffn),
                  ("p6", first_mixture), ("p7", messages), ("p8", last_mixture)]
        for name, build in phases[:last_phase]:
            phase(name, build)


_INS = ['x', 'src', 'dst', 'edge_attr_4', 'edge_weight', 'L0_gnn_W1', 'L0_gnn_b1', 'L0_gnn_W2', 'L0_gnn_b2',
        'L0_ffn_router_w', 'L0_ffn_w1', 'L0_ffn_b1', 'L0_ffn_w2', 'L0_ffn_b2', 'L1_gnn_mlp_w', 'L1_gnn_mlp_b',
        'L1_gnn_ew1', 'L1_gnn_ew2', 'L1_gnn_bn_g', 'L1_gnn_bn_b', 'L1_ffn_W_gat', 'L1_ffn_att_src', 'L1_ffn_att_dst',
        'L1_ffn_b_gat', 'L1_ffn_ln_gamma', 'L1_ffn_ln_beta', 'L1_ffn_W1', 'L1_ffn_b1', 'L1_ffn_W2', 'L1_ffn_b2',
        'L1_ffn_edge_index']


def kernel(**inputs):
    import numpy as _np
    import concourse.bacc as _bacc
    from concourse import mybir as _mybir
    from concourse.bass_utils import run_bass_kernel_spmd as _run

    nc = _bacc.Bacc("TRN2", target_bir_lowering=False, num_devices=1)
    arrays, args = {}, []
    for name in _INS:
        a = _np.ascontiguousarray(inputs[name])
        arrays[f"in_{name}_dram"] = a
        args.append(nc.dram_tensor(f"in_{name}_dram", a.shape, _mybir.dt.from_np(a.dtype), kind="ExternalInput").ap())
    out = nc.dram_tensor("out_0_dram", (N, D), F32, kind="ExternalOutput").ap()
    program(nc, *args, out)
    r = _run(nc, [arrays], core_ids=[0])
    return r.results[0]["out_0_dram"]
```
